# Optimizing a Trainium2 kernel written in Bass

```python
import numpy as np
import jax
import jax.numpy as jnp

def _softmax(x, axis=-1):
    return jax.nn.softmax(x, axis=axis)

def _gelu(x):
    return jax.nn.gelu(x, approximate=True)

def _silu(x):
    return jax.nn.silu(x)

def _sigmoid(x):
    return jax.nn.sigmoid(x)

def _layernorm(x, axis=-1, eps=1e-05):
    m = jnp.mean(x, axis=axis, keepdims=True)
    v = jnp.var(x, axis=axis, keepdims=True)
    return (x - m) / jnp.sqrt(v + eps)

def _scatter_add(tgt, idx, src, axis=0):
    return tgt.at[idx].add(src)

def _segment_sum(src, seg, n):
    return jax.ops.segment_sum(src, seg, n)
kernel_name = 'mk_gnn_resnorm_d4_gnn_r32_1283e8'

def setup_inputs(seed: int=0):
    np.random.seed(seed)
    _w = jnp.asarray

    def _rec_inputs():
        import jax
        import jax.numpy as jnp
        _gk = jax.random.key(seed)
        x = -0.0003713 + 1 * jax.random.normal(jax.random.fold_in(_gk, 1), (50000, 128), jnp.float32)
        src = jax.random.randint(jax.random.fold_in(_gk, 2), (25000,), 0, 50000, jnp.int32)
        dst = jnp.minimum((50000 * jax.random.uniform(jax.random.fold_in(_gk, 3), (25000,)) ** 2.0).astype(jnp.int32), 49999)
        _o = jnp.argsort(dst, stable=True)
        src = src[_o]
        dst = dst[_o]
        edge_attr_16 = 0.000254156 + 0.999948 * jax.random.normal(jax.random.fold_in(_gk, 12), (25000, 16), jnp.float32)
        edge_type_8 = jax.random.randint(jax.random.fold_in(_gk, 14), (25000,), 0, 8, jnp.int32)
        edge_weight = jax.random.uniform(jax.random.fold_in(_gk, 15), (25000,), jnp.float32, 0.0, 0.999998)
        edge_weight1 = jax.random.uniform(jax.random.fold_in(_gk, 16), (25000, 1), jnp.float32, 0.0, 0.999999)
        return (x, src, dst, edge_attr_16, edge_type_8, edge_weight, edge_weight1)
    x, src, dst, edge_attr_16, edge_type_8, edge_weight, edge_weight1 = _rec_inputs()

    def _L0_gnn_setup():
        import jax, jax.numpy as jnp
        import numpy as np
        N_NODES = 3125
        N_EDGES = 50000
        D = 128

        def _sage_conv(x, src, dst, Wl, bl, Wr, n_nodes):
            msg = x[src]
            summed = jax.ops.segment_sum(msg, dst, num_segments=n_nodes)
            cnt = jax.ops.segment_sum(jnp.ones((src.shape[0],), x.dtype), dst, num_segments=n_nodes)
            mean = summed / jnp.maximum(cnt, 1.0)[:, None]
            return mean @ Wl + bl + x @ Wr
        key = jax.random.key(seed)
        ks = jax.random.split(key, 12)
        scale = 1.0 / np.sqrt(D)
        inp = {'x': jax.random.normal(ks[0], (N_NODES, D), jnp.float32), 'edge_index': jax.random.randint(ks[1], (2, N_EDGES), 0, N_NODES, dtype=jnp.int64)}
        for i in range(3):
            inp[f'Wl{i}'] = jax.random.normal(ks[2 + 3 * i], (D, D), jnp.float32) * scale
            inp[f'bl{i}'] = jnp.zeros((D,), jnp.float32)
            inp[f'Wr{i}'] = jax.random.normal(ks[3 + 3 * i], (D, D), jnp.float32) * scale
        return inp
    _L0_gnn_all = _L0_gnn_setup()
    _L0_gnn_in = {k: v for k, v in _L0_gnn_all.items() if k in ('Wl0', 'bl0', 'Wr0', 'Wl1', 'bl1', 'Wr1', 'Wl2', 'bl2', 'Wr2')}
    del _L0_gnn_all

    def _L1_gnn_setup():
        import jax, jax.numpy as jnp
        import numpy as np
        N, E, D_EDGE, D, D_HID = (50000, 25000, 16, 128, 256)
        key = jax.random.key(seed)
        ks = jax.random.split(key, 8)
        x = jax.random.normal(ks[0], (N, D), dtype=jnp.float32)
        edge_index = jax.random.randint(ks[1], (2, E), 0, N, dtype=jnp.int64)
        edge_attr = jax.random.normal(ks[2], (E, D_EDGE), dtype=jnp.float32)
        edge_weight = jax.random.uniform(ks[3], (E, 1), dtype=jnp.float32)
        bond_W = jax.random.normal(ks[4], (D_EDGE, D), dtype=jnp.float32) * (1.0 / np.sqrt(D_EDGE))
        bond_b = jnp.zeros((D,), dtype=jnp.float32)
        eps = jnp.zeros((1,), dtype=jnp.float32)
        W1 = jax.random.normal(ks[5], (D, D_HID), dtype=jnp.float32) * (1.0 / np.sqrt(D))
        b1 = jnp.zeros((D_HID,), dtype=jnp.float32)
        W2 = jax.random.normal(ks[6], (D_HID, D), dtype=jnp.float32) * (1.0 / np.sqrt(D_HID))
        b2 = jnp.zeros((D,), dtype=jnp.float32)
        return {'x': x, 'edge_index': edge_index, 'edge_attr': edge_attr, 'edge_weight': edge_weight, 'bond_W': bond_W, 'bond_b': bond_b, 'eps': eps, 'W1': W1, 'b1': b1, 'W2': W2, 'b2': b2}
    _L1_gnn_all = _L1_gnn_setup()
    _L1_gnn_in = {k: v for k, v in _L1_gnn_all.items() if k in ('bond_W', 'bond_b', 'eps', 'W1', 'b1', 'W2', 'b2')}
    del _L1_gnn_all

    def _L2_gnn_setup():
        import jax, jax.numpy as jnp
        import numpy as np
        N, C, E, T = (3125, 128, 18750, 128)
        EPS = 1e-05

        def gcn_conv(x, edge_index, edge_weight, W, b, improved_fill=2.0):
            n = x.shape[0]
            xw = x @ W
            loop = jnp.arange(n)
            row = jnp.concatenate([edge_index[0], loop])
            col = jnp.concatenate([edge_index[1], loop])
            ew = jnp.concatenate([edge_weight, jnp.full((n,), improved_fill, edge_weight.dtype)])
            deg = jax.ops.segment_sum(ew, col, num_segments=n)
            dinv = jnp.where(deg > 0, deg ** (-0.5), 0.0)
            norm = dinv[row] * ew * dinv[col]
            msg = xw[row] * norm[:, None]
            agg = jax.ops.segment_sum(msg, col, num_segments=n)
            return agg + b

        def layer_norm(x, g, b):
            mu = jnp.mean(x, axis=-1, keepdims=True)
            var = jnp.mean((x - mu) ** 2, axis=-1, keepdims=True)
            return (x - mu) * jax.lax.rsqrt(var + EPS) * g + b
        key = jax.random.key(seed)
        ks = jax.random.split(key, 16)
        s = 1.0 / np.sqrt(C)
        return {'x': jax.random.normal(ks[0], (N, C), jnp.float32), 'edge_index': jax.random.randint(ks[1], (2, E), 0, N, jnp.int64), 'edge_weight': jax.random.uniform(ks[2], (E,), jnp.float32), 't': jax.random.normal(ks[3], (T,), jnp.float32), 'W1': jax.random.normal(ks[4], (C, C), jnp.float32) * s, 'b1': jnp.zeros((C,), jnp.float32), 'g1': jnp.ones((C,), jnp.float32), 'be1': jnp.zeros((C,), jnp.float32), 'W2': jax.random.normal(ks[5], (C, C), jnp.float32) * s, 'b2': jnp.zeros((C,), jnp.float32), 'g2': jnp.ones((C,), jnp.float32), 'be2': jnp.zeros((C,), jnp.float32), 'Wt': jax.random.normal(ks[6], (T, C), jnp.float32) * (1.0 / np.sqrt(T)), 'bt': jnp.zeros((C,), jnp.float32)}
    _L2_gnn_all = _L2_gnn_setup()
    _L2_gnn_in = {k: v for k, v in _L2_gnn_all.items() if k in ('t', 'W1', 'b1', 'g1', 'be1', 'W2', 'b2', 'g2', 'be2', 'Wt', 'bt')}
    del _L2_gnn_all

    def _L3_gnn_setup():
        import jax, jax.numpy as jnp
        import numpy as np
        N = 3125
        E = 50000
        R = 8
        D = 128

        def _rel_conv(h, W, loop_w, b, src, dst, etype, relu):
            h_rel = jnp.einsum('ni,rio->rno', h, W)
            msg = h_rel[etype, src]
            agg = jax.ops.segment_sum(msg, dst, num_segments=h.shape[0])
            out = agg + h @ loop_w + b
            return jax.nn.relu(out) if relu else out
        key = jax.random.key(seed)
        ks = jax.random.split(key, 10)
        feats = jax.random.normal(ks[0], (N, D), dtype=jnp.float32)
        src = jax.random.randint(ks[1], (E,), 0, N, dtype=jnp.int32)
        dst = jax.random.randint(ks[2], (E,), 0, N, dtype=jnp.int32)
        etype = jax.random.randint(ks[3], (E,), 0, R, dtype=jnp.int32)
        s = 0.05
        W1 = jax.random.normal(ks[4], (R, D, D), dtype=jnp.float32) * s
        loop_w1 = jax.random.normal(ks[5], (D, D), dtype=jnp.float32) * s
        b1 = jnp.zeros((D,), dtype=jnp.float32)
        W2 = jax.random.normal(ks[6], (R, D, D), dtype=jnp.float32) * s
        loop_w2 = jax.random.normal(ks[7], (D, D), dtype=jnp.float32) * s
        b2 = jnp.zeros((D,), dtype=jnp.float32)
        return {'feats': feats, 'W1': W1, 'loop_w1': loop_w1, 'b1': b1, 'W2': W2, 'loop_w2': loop_w2, 'b2': b2, 'src': src, 'dst': dst, 'etype': etype}
    _L3_gnn_all = _L3_gnn_setup()
    _L3_gnn_in = {k: v for k, v in _L3_gnn_all.items() if k in ('W1', 'loop_w1', 'b1', 'W2', 'loop_w2', 'b2')}
    del _L3_gnn_all
    return {'x': x, 'src': src, 'dst': dst, 'edge_attr_16': edge_attr_16, 'edge_type_8': edge_type_8, 'edge_weight': edge_weight, 'edge_weight1': edge_weight1, 'L0_gnn_Wl0': _L0_gnn_in['Wl0'], 'L0_gnn_bl0': _L0_gnn_in['bl0'], 'L0_gnn_Wr0': _L0_gnn_in['Wr0'], 'L0_gnn_Wl1': _L0_gnn_in['Wl1'], 'L0_gnn_bl1': _L0_gnn_in['bl1'], 'L0_gnn_Wr1': _L0_gnn_in['Wr1'], 'L0_gnn_Wl2': _L0_gnn_in['Wl2'], 'L0_gnn_bl2': _L0_gnn_in['bl2'], 'L0_gnn_Wr2': _L0_gnn_in['Wr2'], 'L1_gnn_bond_W': _L1_gnn_in['bond_W'], 'L1_gnn_bond_b': _L1_gnn_in['bond_b'], 'L1_gnn_eps': _L1_gnn_in['eps'], 'L1_gnn_W1': _L1_gnn_in['W1'], 'L1_gnn_b1': _L1_gnn_in['b1'], 'L1_gnn_W2': _L1_gnn_in['W2'], 'L1_gnn_b2': _L1_gnn_in['b2'], 'L2_gnn_t': _L2_gnn_in['t'], 'L2_gnn_W1': _L2_gnn_in['W1'], 'L2_gnn_b1': _L2_gnn_in['b1'], 'L2_gnn_g1': _L2_gnn_in['g1'], 'L2_gnn_be1': _L2_gnn_in['be1'], 'L2_gnn_W2': _L2_gnn_in['W2'], 'L2_gnn_b2': _L2_gnn_in['b2'], 'L2_gnn_g2': _L2_gnn_in['g2'], 'L2_gnn_be2': _L2_gnn_in['be2'], 'L2_gnn_Wt': _L2_gnn_in['Wt'], 'L2_gnn_bt': _L2_gnn_in['bt'], 'L3_gnn_W1': _L3_gnn_in['W1'], 'L3_gnn_loop_w1': _L3_gnn_in['loop_w1'], 'L3_gnn_b1': _L3_gnn_in['b1'], 'L3_gnn_W2': _L3_gnn_in['W2'], 'L3_gnn_loop_w2': _L3_gnn_in['loop_w2'], 'L3_gnn_b2': _L3_gnn_in['b2']}

def reference(x, src, dst, edge_attr_16, edge_type_8, edge_weight, edge_weight1, L0_gnn_Wl0, L0_gnn_bl0, L0_gnn_Wr0, L0_gnn_Wl1, L0_gnn_bl1, L0_gnn_Wr1, L0_gnn_Wl2, L0_gnn_bl2, L0_gnn_Wr2, L1_gnn_bond_W, L1_gnn_bond_b, L1_gnn_eps, L1_gnn_W1, L1_gnn_b1, L1_gnn_W2, L1_gnn_b2, L2_gnn_t, L2_gnn_W1, L2_gnn_b1, L2_gnn_g1, L2_gnn_be1, L2_gnn_W2, L2_gnn_b2, L2_gnn_g2, L2_gnn_be2, L2_gnn_Wt, L2_gnn_bt, L3_gnn_W1, L3_gnn_loop_w1, L3_gnn_b1, L3_gnn_W2, L3_gnn_loop_w2, L3_gnn_b2):
    import jax
    import jax.numpy as jnp

    def _L0_gnn_ref(x, edge_index, Wl0, bl0, Wr0, Wl1, bl1, Wr1, Wl2, bl2, Wr2):
        import jax, jax.numpy as jnp
        import numpy as np
        N_NODES = 3125
        N_EDGES = 50000
        D = 128

        def _sage_conv(x, src, dst, Wl, bl, Wr, n_nodes):
            msg = x[src]
            summed = jax.ops.segment_sum(msg, dst, num_segments=n_nodes)
            cnt = jax.ops.segment_sum(jnp.ones((src.shape[0],), x.dtype), dst, num_segments=n_nodes)
            mean = summed / jnp.maximum(cnt, 1.0)[:, None]
            return mean @ Wl + bl + x @ Wr
        src, dst = (edge_index[0], edge_index[1])
        n = x.shape[0]
        layers = [(Wl0, bl0, Wr0), (Wl1, bl1, Wr1), (Wl2, bl2, Wr2)]
        h = x
        for Wl, bl, Wr in layers[:-1]:
            h = _sage_conv(h, src, dst, Wl, bl, Wr, n)
            h = jax.nn.relu(h)
        Wl, bl, Wr = layers[-1]
        return _sage_conv(h, src, dst, Wl, bl, Wr, n)

    def _L1_gnn_ref(x, edge_index, edge_attr, edge_weight, bond_W, bond_b, eps, W1, b1, W2, b2):
        import jax, jax.numpy as jnp
        import numpy as np
        N, E, D_EDGE, D, D_HID = (50000, 25000, 16, 128, 256)
        edge_emb = edge_attr @ bond_W + bond_b
        src = edge_index[0]
        dst = edge_index[1]
        message = jax.nn.gelu(x[src] + edge_emb, approximate=False) * edge_weight
        agg = jax.ops.segment_sum(message, dst, num_segments=x.shape[0])
        h = (1.0 + eps) * x + agg
        h = jax.nn.relu(h @ W1 + b1)
        return h @ W2 + b2

    def _L2_gnn_ref(x, edge_index, edge_weight, t, W1, b1, g1, be1, W2, b2, g2, be2, Wt, bt):
        import jax, jax.numpy as jnp
        import numpy as np
        N, C, E, T = (3125, 128, 18750, 128)
        EPS = 1e-05

        def gcn_conv(x, edge_index, edge_weight, W, b, improved_fill=2.0):
            n = x.shape[0]
            xw = x @ W
            loop = jnp.arange(n)
            row = jnp.concatenate([edge_index[0], loop])
            col = jnp.concatenate([edge_index[1], loop])
            ew = jnp.concatenate([edge_weight, jnp.full((n,), improved_fill, edge_weight.dtype)])
            deg = jax.ops.segment_sum(ew, col, num_segments=n)
            dinv = jnp.where(deg > 0, deg ** (-0.5), 0.0)
            norm = dinv[row] * ew * dinv[col]
            msg = xw[row] * norm[:, None]
            agg = jax.ops.segment_sum(msg, col, num_segments=n)
            return agg + b

        def layer_norm(x, g, b):
            mu = jnp.mean(x, axis=-1, keepdims=True)
            var = jnp.mean((x - mu) ** 2, axis=-1, keepdims=True)
            return (x - mu) * jax.lax.rsqrt(var + EPS) * g + b
        h = gcn_conv(x, edge_index, edge_weight, W1, b1)
        h = layer_norm(jax.nn.relu(h), g1, be1)
        h = h + jax.nn.relu(t @ Wt + bt)
        h = gcn_conv(h, edge_index, edge_weight, W2, b2)
        h = layer_norm(jax.nn.relu(h), g2, be2)
        return h

    def _L3_gnn_ref(feats, W1, loop_w1, b1, W2, loop_w2, b2, src, dst, etype):
        import jax, jax.numpy as jnp
        import numpy as np
        N = 3125
        E = 50000
        R = 8
        D = 128

        def _rel_conv(h, W, loop_w, b, src, dst, etype, relu):
            h_rel = jnp.einsum('ni,rio->rno', h, W)
            msg = h_rel[etype, src]
            agg = jax.ops.segment_sum(msg, dst, num_segments=h.shape[0])
            out = agg + h @ loop_w + b
            return jax.nn.relu(out) if relu else out
        h = _rel_conv(feats, W1, loop_w1, b1, src, dst, etype, relu=True)
        h = _rel_conv(h, W2, loop_w2, b2, src, dst, etype, relu=False)
        return h
    edge_index = jnp.stack([src, dst])
    x = _layernorm(x + _L0_gnn_ref(x, edge_index, L0_gnn_Wl0, L0_gnn_bl0, L0_gnn_Wr0, L0_gnn_Wl1, L0_gnn_bl1, L0_gnn_Wr1, L0_gnn_Wl2, L0_gnn_bl2, L0_gnn_Wr2), axis=-1)
    x = _layernorm(x + _L1_gnn_ref(x, edge_index, edge_attr_16, edge_weight1, L1_gnn_bond_W, L1_gnn_bond_b, L1_gnn_eps, L1_gnn_W1, L1_gnn_b1, L1_gnn_W2, L1_gnn_b2), axis=-1)
    x = _layernorm(x + _L2_gnn_ref(x, edge_index, edge_weight, L2_gnn_t, L2_gnn_W1, L2_gnn_b1, L2_gnn_g1, L2_gnn_be1, L2_gnn_W2, L2_gnn_b2, L2_gnn_g2, L2_gnn_be2, L2_gnn_Wt, L2_gnn_bt), axis=-1)
    x = _layernorm(x + _L3_gnn_ref(x, L3_gnn_W1, L3_gnn_loop_w1, L3_gnn_b1, L3_gnn_W2, L3_gnn_loop_w2, L3_gnn_b2, src, dst, edge_type_8), axis=-1)
    return x

_drawn_inputs = setup_inputs


def setup_inputs(seed=0):
    import zlib

    import numpy as np

    out = dict(_drawn_inputs(seed))
    spreads = {'L0_gnn_bl0': (0.0, 0.1),
     'L0_gnn_bl1': (0.0, 0.1),
     'L0_gnn_bl2': (0.0, 0.1),
     'L1_gnn_bond_b': (0.0, 0.715),
     'L1_gnn_b1': (0.0, 0.1),
     'L1_gnn_b2': (0.0, 0.1),
     'L2_gnn_b1': (0.0, 0.1),
     'L2_gnn_g1': (1.0, 0.2),
     'L2_gnn_be1': (0.0, 0.1),
     'L2_gnn_b2': (0.0, 0.1),
     'L2_gnn_g2': (1.0, 0.2),
     'L2_gnn_be2': (0.0, 0.1),
     'L2_gnn_bt': (0.0, 0.1),
     'L3_gnn_b1': (0.0, 0.1),
     'L3_gnn_b2': (0.0, 0.1)}
    factors = {}
    for name, (base, spread) in spreads.items():
        noise = np.random.default_rng([zlib.crc32(name.encode()), seed]).standard_normal(out[name].shape)
        drawn = base * np.exp(spread * noise) if base else spread * noise
        out[name] = jnp.asarray(drawn.astype(out[name].dtype))
    for name, factor in factors.items():
        out[name] = (out[name] * factor).astype(out[name].dtype)
    return out
```

```python
from contextlib import ExitStack

import concourse.bass as bass
from concourse import mybir

F32 = mybir.dt.float32
F16 = mybir.dt.float16
I32 = mybir.dt.int32
ALU = mybir.AluOpType
ACT = mybir.ActivationFunctionType
AX = mybir.AxisListType

P = 128
N, E, D = 50000, 25000, 128
TILES = -(-E // P)
LAST = E - (TILES - 1) * P
BATCH = 7
BATCHES = TILES // BATCH
RING = 4
HALF = 512
PAIR = 2 * HALF
NPAIR = -(-N // PAIR)
NHALF = 2 * NPAIR
BLOCKS = PAIR // P
TAIL = N - PAIR
OH = 4
REL = 8
DE = 16
HT = TILES // 2
TURNS = BATCHES // RING
LROW = 8
EPS = 1e-5
assert TILES % BATCH == 0 and BATCHES % RING == 0 and TILES % 2 == 0

SAGE, GIN, GCN, RGCN = "sage", "gin", "gcn", "rgcn"


class Round:

    def __init__(self, kind, layer, source, out, res=None, relu=False, norm=False):
        self.kind, self.layer, self.source, self.out = kind, layer, source, out
        self.res, self.relu, self.norm = res, relu, norm


class RoundSemaphores:

    def __init__(self, counted, before, oh_ready, oh_used):
        self.before, self.oh_ready, self.oh_used = before, oh_ready, oh_used
        self.weights_in = counted["weights_in"]
        self.h_loaded = counted["h_loaded"]
        self.stored = counted["stored"]
        self.stored2 = counted["stored2"]
        self.res_loaded = counted["res_loaded"]
        self.res_used = counted["res_used"]
        self.idx_ready = counted["idx_ready"]
        self.batch_in = counted["batch_in"]
        self.hi_done = counted["hi_done"]
        self.lo_done = counted["lo_done"]
        self.split_done = counted["split_done"]
        self.tr_done = counted["tr_done"]
        self.ht_done = counted["ht_done"]
        self.agg_done = counted["agg_done"]
        self.dense_done = counted["dense_done"]
        self.u_done = counted["u_done"]
        self.out_done = counted["out_done"]
        self.relu_done = counted["relu_done"]
        self.var_done = counted["var_done"]
        self.std_done = counted["std_done"]
        self.stats_done = counted["stats_done"]
        self.norm_done = counted["norm_done"]
        self.dve_step = counted["dve_step"]
        self.et_done = counted["et_done"]
        self.et_ready = counted["et_ready"]
        self.rel_done = counted["rel_done"]
        self.sel_step = counted["sel_step"]


ROUNDS = [
    Round(SAGE, 0, "x", "s1", relu=True),
    Round(SAGE, 1, "s1", "s2", relu=True),
    Round(SAGE, 2, "s2", "x1", res="x", norm=True),
    Round(GIN, 0, "x1", "x2", res="x1", norm=True),
    Round(GCN, 1, "s1", "s2", relu=True, norm=True),
    Round(GCN, 2, "s2", "x3", res="x2", relu=True, norm=True),
    Round(RGCN, 1, "x3", "s1", relu=True),
    Round(RGCN, 2, "s1", "out", res="x3", norm=True),
]
NROUNDS = len(ROUNDS)


def build_gnn(nc, A, out_ap, rounds=ROUNDS):
    ctx = ExitStack()
    with ctx:
        def sb(name, shape, dt=F32):
            return ctx.enter_context(nc.sbuf_tensor(name, shape, dt))

        def ps(name, shape):
            return ctx.enter_context(nc.psum_tensor(name, shape, F32))

        def sem(name):
            return ctx.enter_context(nc.semaphore(name))

        dram = {"x": A["x"], "out": out_ap}
        for name in ("s1", "s2", "x1", "x2", "x3"):
            dram[name] = nc.dram_tensor(f"node_{name}", (N, D), F32, kind="Internal").ap()
        list_dram = nc.dram_tensor("list_scratch", (NHALF, LROW), I32, kind="Internal").ap()

        raw = sb("raw", [P, RING * BATCH, D])
        msg = sb("msg", [P, TILES, 2 * D], F16)
        edge_v = sb("edge_v", [P, BATCH, D])
        attr = sb("attr", [BATCH * DE, RING, P])
        attr_now = sb("attr_now", [P, P])
        src_i = sb("src_i", [P, TILES], I32)
        idx_now = sb("idx_now", [P, RING * BATCH], I32)
        dst_f = sb("dst_f", [P, TILES])
        etype_f = sb("etype_f", [P, TILES])
        ew = sb("ew", [P, TILES])
        ew1 = sb("ew1", [P, TILES])
        mask = sb("mask", [P, REL, TILES])
        ecol = sb("ecol", [P, TILES + 32, 4], F16)
        edge_t = sb("edge_t", [P, 2, P])
        onehot = sb("onehot", [P, OH, HALF], F16)
        h_in = sb("h_in", [P, BLOCKS, D])
        h_t = sb("h_t", [P, 2, HALF])
        agg_t = sb("agg_t", [P, 2, HALF])
        res_in = sb("res_in", [P, BLOCKS, D])
        u = sb("u", [P, BLOCKS, D])
        v = sb("v", [P, BLOCKS, D])
        o = sb("o", [P, BLOCKS, D])
        o2 = sb("o2", [P, BLOCKS, D])
        hid = sb("hid", [P, 2, 2, HALF])
        count = sb("count", [P, 4])
        stats = sb("stats", [P, BLOCKS, 6])
        mv = sb("mv", [P, BLOCKS, 2])
        std = sb("std", [P, BLOCKS])
        eps_col = sb("eps_col", [P, 1])
        rstd = sb("rstd", [P, BLOCKS])
        nmr = sb("nmr", [P, BLOCKS])
        rstd_d = sb("rstd_d", [P, BLOCKS])
        nmr_d = sb("nmr_d", [P, BLOCKS])
        deg_rows = sb("deg_rows", [4, HALF])
        deg = sb("deg", [P, NHALF * 4])
        inv = sb("inv", [P, NHALF * 4])
        dinv = sb("dinv", [P, NHALF * 4])
        w = sb("w", [P, REL + 1, D])
        bond = sb("bond", [P, BATCH, D])
        bias = sb("bias", [P, D])
        gain = sb("gain", [P, D])
        shift = sb("shift", [P, D])
        b1_col = sb("b1_col", [P, 2])
        one_eps = sb("one_eps", [P, 1])
        t_col = sb("t_col", [P, 1])
        t_rep = sb("t_rep", [P, P])
        bt = sb("bt", [P, D])
        col_i = sb("col_i", [P, HALF], I32)
        row_i = sb("row_i", [P, 1], I32)
        base_i = sb("base_i", [P, NHALF], I32)
        colf = sb("colf", [P, P])
        rowf = sb("rowf", [P, 1])
        iota = sb("iota", [P, HALF], F16)
        basef = sb("basef", [P, NHALF])
        negbase = sb("negbase", [P, NHALF])
        ident = sb("ident", [P, P])
        ident16 = sb("ident16", [P, P], F16)
        deg_sel = sb("deg_sel", [4, 2])
        ones = sb("ones", [P, P])
        lists = sb("lists", [1, NHALF * LROW], I32)

        dst_i = sb("dst_i", [P, TILES], I32)
        etype_i = sb("etype_i", [P, TILES], I32)
        dst_rows = sb("dst_rows", [HT, 2, P], I32)
        touch = sb("touch", [HT, 4, NHALF])
        before = sb("before", [P, P])
        diag = sb("diag", [P, P])
        ahead = sb("ahead", [P, P])
        list_f = sb("list_f", [NHALF, LROW])
        list_rows = sb("list_rows", [NHALF, LROW], I32)
        t_max, t_min = sb("t_max", [HT, 2]), sb("t_min", [HT, 2])
        col = [sb(f"setup_col{k}", [P, 1]) for k in range(8)]
        n_items, n_batches = sb("n_items", [P, 1]), sb("n_batches", [P, 1])
        edge_arrays = [("src", src_i), ("edge_weight", ew), ("edge_weight1", ew1), ("dst", dst_i),
                       ("edge_type_8", etype_i)]
        edge_loads = len(edge_arrays) + 3

        p_agg = ps("p_agg", [P, 2, HALF])
        p_dense = ps("p_dense", [P, 2, HALF])
        p_wide = ps("p_wide", [P, 2, HALF])
        p_tr = ps("p_tr", [P, HALF])
        p_edge = ps("p_edge", [P, HALF])

        pads_set = sem("pads_set")
        edges_in = sem("edges_in")
        iotas = sem("iotas")
        dve_prep = sem("dve_prep")
        prep_to_pe = sem("prep_to_pe")
        pe_prep = sem("pe_prep")
        rows_ready = sem("rows_ready")
        rows_stored = sem("rows_stored")
        lists_in = sem("lists_in")
        passed = sem("passed")

        def adds(rd):
            norms = norms_of(rd)
            return dict(
                weights_in=16 * len(round_weights(rd)), h_loaded=16 * NPAIR, stored=16 * NPAIR,
                var_done=NPAIR * norms, std_done=NPAIR * norms, stored2=16 * NPAIR if rd.kind == GIN else 0, res_loaded=16 * NPAIR if rd.res else 0,
                res_used=NPAIR if rd.res else 0, idx_ready=BATCHES, batch_in=BATCHES,
                hi_done=2 * BATCHES if rd.kind == RGCN else BATCHES, lo_done=BATCHES, tr_done=NHALF,
                ht_done=NHALF, agg_done=NHALF, dense_done=NHALF, u_done=NPAIR, out_done=NPAIR,
                relu_done=NPAIR if rd.relu and rd.norm else 0, stats_done=NPAIR * norms,
                norm_done=NPAIR if rd.kind in (GIN, GCN) else 0, dve_step=NPAIR * steps_of(rd),
                split_done=BATCHES + 1 if rd.kind == RGCN else 0, et_done=TILES if rd.kind == RGCN else 0, et_ready=TILES if rd.kind == RGCN else 0,
                rel_done=2 * TILES if rd.kind == RGCN else 0,
                sel_step=REL * (TILES + 1) if rd.kind == RGCN else 0)

        gathered = [sem(f"gathered{q}") for q in range(RING)]
        attr_ready, emb_done, emb_used, gelu_done = sem("attr_ready"), sem("emb_done"), sem("emb_used"), sem("gelu_done")
        hid_done, hid_ready = sem("hid_done"), sem("hid_ready")
        deg_copied, deg_tr, deg_used = sem("deg_copied"), sem("deg_tr"), sem("deg_used")
        count_done, deg_ready, deg_root = sem("count_done"), sem("deg_ready"), sem("deg_root")
        const_pe, const_used, const_dve = sem("const_pe"), sem("const_used"), sem("const_dve")
        per_batch = [BATCH + (rd.kind == GIN) for rd in rounds]
        landed_before = [TURNS * sum(per_batch[:r]) for r in range(len(rounds))]

        def round_weights(rd):
            def rep(name):
                return A[name].partition_broadcast(P)

            if rd.kind == SAGE:
                k = rd.layer
                return [(w[:, 0, :], A[f"L0_gnn_Wl{k}"]), (w[:, 1, :], A[f"L0_gnn_Wr{k}"]),
                        (bias[:, :], rep(f"L0_gnn_bl{k}"))]
            if rd.kind == GIN:
                out = [(w[:, q, :], A["L1_gnn_W1"][:, q * D:(q + 1) * D]) for q in range(2)]
                out += [(w[:, 2 + q, :], A["L1_gnn_W2"][q * P:(q + 1) * P, :]) for q in range(2)]
                out += [(bias[:, :], rep("L1_gnn_b2")), (b1_col[:, :], A["L1_gnn_b1"]),
                        (one_eps[:, :], rep("L1_gnn_eps"))]
                for j in range(BATCH):
                    out.append((bond[j * DE:(j + 1) * DE, j, :], A["L1_gnn_bond_W"]))
                    out.append((bond[BATCH * DE:BATCH * DE + 1, j, :], A["L1_gnn_bond_b"].partition_broadcast(1)))
                return out
            if rd.kind == GCN:
                k = rd.layer
                out = [(w[:, 0, :], A[f"L2_gnn_W{k}"]), (bias[:, :], rep(f"L2_gnn_b{k}")),
                       (gain[:, :], rep(f"L2_gnn_g{k}")), (shift[:, :], rep(f"L2_gnn_be{k}"))]
                if k == 1:
                    out += [(w[:, 1, :], A["L2_gnn_Wt"]), (t_col[:, :], A["L2_gnn_t"].rearrange("(p o) -> p o", o=1)),
                            (bt[:, :], rep("L2_gnn_bt"))]
                return out
            k = rd.layer
            return [(w[:, 0:REL, :], A[f"L3_gnn_W{k}"].rearrange("r i o -> i r o")),
                    (w[:, REL, :], A[f"L3_gnn_loop_w{k}"]), (bias[:, :], rep(f"L3_gnn_b{k}"))]

        def norms_of(rd):
            return (2 if rd.kind == GCN and rd.layer == 2 else 1) if rd.norm else 0

        def scaled_by_dinv(rd):
            return rd.kind == GIN or (rd.kind == GCN and rd.layer == 1)

        def steps_of(rd):
            return ((rd.kind == SAGE) + 2 * norms_of(rd) + scaled_by_dinv(rd) + (rd.layer if rd.kind == GCN else 0))

        counted = {name: sem(name) for name in adds(rounds[0])}
        R = []
        for r, rd in enumerate(rounds):
            earlier = {name: sum(adds(x)[name] for x in rounds[:r]) for name in counted}
            R.append(RoundSemaphores(counted, earlier, sem(f"oh_ready{r}"), sem(f"oh_used{r}")))

        def is_zero(it):
            return isinstance(it, int) and it == 0

        def load_list(eng, kind, at, count):
            return nc.values_load_multi_w_load_instructions(
                lists[0:1, bass.ds(at, count)], engines=[kind], min_val=0, max_val=NHALF * TILES)[1]

        def batch_range(eng, kind, it):
            e0, e1 = load_list(eng, kind, it * (2 * LROW) + LROW + 3, 2)
            return e0.with_bounds(min_val=0, max_val=BATCHES), e1.with_bounds(min_val=0, max_val=BATCHES)

        def item_range(eng, kind, it, a):
            t0, i0, i1 = load_list(eng, kind, it * (2 * LROW) + a * LROW, 3)
            return t0.with_bounds(min_val=0, max_val=TILES - 2), i0, i1

        def tile_of(t0, i0, i):
            return (t0 + (i - i0)).with_bounds(min_val=0, max_val=TILES - 1)

        def each_batch(eng, e0, e1, body):
            with eng.If(e0 < e1):
                with eng.Fori(e0, e1) as e:
                    body(e.with_bounds(min_val=0, max_val=BATCHES - 1))

        def wait_apart(eng, semaphore, value):
            eng.wait_ge(semaphore, value)
            eng.sem_inc(passed, 1)

        def flat(ap):
            return ap.rearrange("p a d -> p (a d)")

        def tile_ap(buf, t, lo=None, hi=None):
            s = buf[:, bass.ds(t, 1), :] if lo is None else buf[:, bass.ds(t, 1), lo:hi]
            return flat(s)

        block = ctx.enter_context(nc.Block())

        @block.sync
        def _(sp):
            sp.wait_ge(pads_set, 1)
            for name, buf in edge_arrays:
                sp.dma_start(buf[:, :], A[name]).then_inc(edges_in, 16)
            flat_dst = A["dst_flat"]
            sp.dma_start(dst_rows[:, 0, :], flat_dst[0:HT * P].rearrange("(p e) -> p e", e=P)).then_inc(edges_in, 16)
            sp.dma_start(dst_rows[0:HT - 1, 1, :],
                         flat_dst[HT * P:(TILES - 1) * P].rearrange("(p e) -> p e", e=P)).then_inc(edges_in, 16)
            sp.dma_start(dst_rows[HT - 1:HT, 1, 0:LAST],
                         flat_dst[(TILES - 1) * P:E].rearrange("(p e) -> p e", p=1)).then_inc(edges_in, 16)
            sp.wait_ge(rows_ready, 1)
            sp.dma_start(list_dram, list_rows[0:NHALF, :]).then_inc(rows_stored, 16)
            sp.wait_ge(rows_stored, 16)
            sp.dma_start(lists[0:1, :], list_dram.rearrange("(o g) c -> o (g c)", o=1)).then_inc(lists_in, 16)

            for r, rd in enumerate(rounds):
                s = R[r]
                if r:
                    sp.wait_ge(R[r - 1].stored, 16 * NPAIR + R[r - 1].before["stored"])
                    if rounds[r - 1].kind == GIN:
                        sp.wait_ge(R[r - 1].stored2, 16 * NPAIR + R[r - 1].before["stored2"])
                for dst_ap, src_ap in round_weights(rd):
                    sp.dma_start(dst_ap, src_ap).then_inc(s.weights_in, 16)
                src_d, out_d = dram[rd.source], dram[rd.out]

                def rows_of(d, base):
                    return d[bass.ds(base, PAIR), :].rearrange("(b p) d -> p b d", p=P)

                def store(it, base):
                    sp.wait_ge(s.out_done, it + 1 + s.before["out_done"])
                    sp.dma_start(rows_of(out_d, base), o[:, :, :]).then_inc(s.stored, 16)
                    if rd.kind == GIN:
                        sp.dma_start(rows_of(dram["s1"], base), o2[:, :, :]).then_inc(s.stored2, 16)

                def step(it, next_base, base, last_base):
                    if next_base is not None:
                        sp.wait_ge(s.tr_done, 2 * it + 2 + s.before["tr_done"])
                        sp.dma_start(h_in[:, :, :], rows_of(src_d, next_base)).then_inc(s.h_loaded, 16)
                    if rd.res:
                        if last_base is not None:
                            sp.wait_ge(s.res_used, it + s.before["res_used"])
                        sp.dma_start(res_in[:, :, :], rows_of(dram[rd.res], base)).then_inc(s.res_loaded, 16)
                    if last_base is not None:
                        store(it - 1, last_base)

                sp.dma_start(h_in[:, :, :], rows_of(src_d, 0)).then_inc(s.h_loaded, 16)
                step(0, PAIR, 0, None)
                with sp.Fori(1, NPAIR - 2) as it:
                    step(it, (it + 1) * PAIR, it * PAIR, (it - 1) * PAIR)
                step(NPAIR - 2, TAIL, (NPAIR - 2) * PAIR, (NPAIR - 3) * PAIR)
                step(NPAIR - 1, None, TAIL, (NPAIR - 2) * PAIR)
                sp.wait_ge(s.stored, 16 * (NPAIR - 1) + s.before["stored"])
                if rd.kind == GIN:
                    sp.wait_ge(s.stored2, 16 * (NPAIR - 1) + s.before["stored2"])
                store(NPAIR - 1, TAIL)
            sp.wait_ge(R[-1].stored, 16 * NPAIR + R[-1].before["stored"])

        @block.gpsimd
        def _(pool):
            nc.gpsimd.iota(col_i[:, :], pattern=[[1, HALF]], base=0, channel_multiplier=0).then_inc(iotas, 1)
            nc.gpsimd.iota(row_i[:, :], pattern=[[0, 1]], base=0, channel_multiplier=1).then_inc(iotas, 1)
            nc.gpsimd.iota(base_i[:, :], pattern=[[PAIR, NPAIR], [HALF, 2]], base=0,
                           channel_multiplier=0).then_inc(iotas, 1)
            pool.wait_ge(edges_in, 16 * edge_loads)
            for r, rd in enumerate(rounds):
                s = R[r]
                if r:
                    pool.wait_ge(R[r - 1].stored, 16 * NPAIR + R[r - 1].before["stored"])
                    if rounds[r - 1].kind == GIN:
                        pool.wait_ge(R[r - 1].stored2, 16 * NPAIR + R[r - 1].before["stored2"])
                src_d = dram[rd.source]

                def pass_on(q, turns):
                    wait_apart(pool, gathered[q], turns * (16 * per_batch[r]) + 16 * landed_before[r])
                    pool.sem_inc(s.batch_in, 1)

                def turn(k, first):
                    for q in range(RING):
                        if not first:
                            pool.wait_ge(s.lo_done, RING * k + (q - RING + 1) + s.before["lo_done"])
                        nc.gpsimd.tensor_copy(
                            idx_now[:, q * BATCH:(q + 1) * BATCH],
                            src_i[:, bass.ds((k * RING + q) * BATCH, BATCH)]).then_inc(s.idx_ready, 1)
                        wait_apart(pool, s.idx_ready, RING * k + (q + 1) + s.before["idx_ready"])
                        for j in range(q * BATCH, (q + 1) * BATCH):
                            nc.gpsimd.indirect_dma_start(
                                out=raw[:, j, :], out_offset=None, in_=src_d,
                                in_offset=bass.IndirectOffsetOnAxis(ap=idx_now[:, j:j + 1], axis=0),
                            ).then_inc(gathered[q], 16)
                        if rd.kind == GIN:
                            pool.dma_start(attr[:, q, :], A["edge_attr_16"][bass.ds(k * RING + q, 1), :, :].rearrange(
                                "o f e -> f (o e)")).then_inc(gathered[q], 16)
                        if q:
                            pass_on(q - 1, k + 1)
                        elif not first:
                            pass_on(RING - 1, k)

                turn(0, True)
                with pool.Fori(1, TURNS) as k:
                    turn(k, False)
                pass_on(RING - 1, TURNS)

        @block.scalar
        def _(act):
            PT = mybir.EngineType.Activation
            act.wait_ge(lists_in, 16)
            for r, rd in enumerate(rounds):
                s = R[r]
                act.wait_ge(s.weights_in, 16 * len(round_weights(rd)) + s.before["weights_in"])
                if r == 1:
                    act.wait_ge(deg_ready, 1)
                    nc.scalar.activation(dinv[:, :], dinv[:, :], ACT.Sqrt).then_inc(deg_root, 1)
                if rd.kind == GIN:
                    act.wait_ge(const_dve, 1)

                def parts_hi(e, source, slot, weight):
                    if weight is None:
                        nc.scalar.activation(msg[:, bass.ds(e * BATCH, BATCH), 0:D],
                                             source[:, bass.ds(slot * BATCH, BATCH), :], ACT.Copy
                                             ).then_inc(s.hi_done, 1)
                        return
                    for j in range(BATCH):
                        last = nc.scalar.activation(
                            tile_ap(msg, e * BATCH + j, 0, D), tile_ap(source, slot * BATCH + j), ACT.Copy,
                            scale=weight[:, bass.ds(e * BATCH + j, 1)])
                    last.then_inc(s.hi_done, 1)

                def batch(e):
                    wait_apart(act, s.batch_in, e + 1 + s.before["batch_in"])
                    if rd.kind == SAGE:
                        parts_hi(e, raw, e % RING, None)
                    elif rd.kind == GCN:
                        parts_hi(e, raw, e % RING, ew)
                    elif rd.kind == GIN:
                        nc.scalar.activation(attr_now[0:BATCH * DE, :], tile_ap(attr, (e % RING)), ACT.Copy
                                             ).then_inc(attr_ready, 1)
                        act.wait_ge(emb_used, 2 * e + 3)
                        nc.scalar.activation(flat(edge_v[:, :, :]), flat(edge_v[:, :, :]), ACT.Gelu
                                             ).then_inc(gelu_done, 1)
                        wait_apart(act, gelu_done, e + 1)
                        parts_hi(e, edge_v, 0, ew1)
                    else:
                        parts_hi(e, raw, e % RING, None)
                        for j in range(BATCH):
                            act.wait_ge(s.et_done, e * BATCH + (j + 1) + s.before["et_done"])
                            nc.scalar.activation(edge_t[:, j % 2, :], (p_edge, p_tr)[j % 2][:, 0:P], ACT.Copy).then_inc(s.et_ready, 1)
                        wait_apart(act, s.sel_step, e * (REL * BATCH) + REL * (BATCH + 1) + s.before["sel_step"])
                        nc.scalar.activation(msg[:, bass.ds(e * BATCH, BATCH), 0:D], edge_v[:, :, :],
                                             ACT.Copy).then_inc(s.hi_done, 1)

                def turn_half(it, a):
                    if r == 0:
                        act.wait_ge(s.tr_done, it * 2 + (a + 1) + s.before["tr_done"])
                        nc.scalar.activation(deg_rows[:, :], p_edge[0:4, :], ACT.Copy).then_inc(deg_copied, 1)
                    act.wait_ge(s.tr_done, it * 2 + (a + 1) + s.before["tr_done"])
                    scale = {GIN: one_eps[:, 0:1], GCN: 2.0}.get(rd.kind, 1.0)
                    nc.scalar.activation(h_t[:, a, :], p_tr[:, :], ACT.Copy, scale=scale).then_inc(s.ht_done, 1)

                def early(it):
                    if not rd.relu:
                        return
                    act.wait_ge(s.u_done, it + 1 + s.before["u_done"])
                    if rd.norm:
                        nc.scalar.activation(v[:, :, :], u[:, :, :], ACT.Relu).then_inc(s.relu_done, 1)
                    else:
                        store_free(it)
                        nc.scalar.activation(o[:, :, :], u[:, :, :], ACT.Relu).then_inc(s.out_done, 1)

                def store_free(it):
                    if is_zero(it):
                        return
                    wait_apart(act, s.stored, it * 16 + s.before["stored"])

                def normalise(dst, source, scale, shift_, semaphore):
                    for b in range(BLOCKS):
                        last = nc.scalar.activation(dst[:, b, :], source[:, b, :], ACT.Identity,
                                                    bias=shift_[:, b:b + 1], scale=scale[:, b:b + 1])
                    last.then_inc(semaphore, 1)

                def deviation(it, nth):
                    act.wait_ge(s.var_done, norms * it + (nth + 1) + s.before["var_done"])
                    nc.scalar.activation(std[:, :], mv[:, :, 1:2].rearrange("p b o -> p (b o)"), ACT.Sqrt,
                                         bias=eps_col[:, 0:1]).then_inc(s.std_done, 1)

                def late(it):
                    if not rd.norm:
                        return
                    deviation(it, 0)
                    wait_apart(act, s.stats_done, norms * it + 1 + s.before["stats_done"])
                    if rd.kind == GCN:
                        normalise(v, v, rstd_d if rd.layer == 1 else rstd, nmr_d if rd.layer == 1 else nmr,
                                  s.norm_done)
                        if rd.layer == 1:
                            return
                        deviation(it, 1)
                        wait_apart(act, s.stats_done, norms * it + 2 + s.before["stats_done"])
                        store_free(it)
                        normalise(o, u, rstd, nmr, s.out_done)
                    else:
                        store_free(it)
                        if rd.kind == GIN:
                            if not is_zero(it):
                                wait_apart(act, s.stored2, it * 16 + s.before["stored2"])
                            normalise(o2, u, rstd_d, nmr_d, s.norm_done)
                        normalise(o, u, rstd, nmr, s.out_done)

                norms = norms_of(rd)

                def hidden(it, a):
                    for q in range(2):
                        act.wait_ge(hid_done, it * 4 + (2 * a + q + 1))
                        nc.scalar.activation(hid[:, a, q, :], p_wide[:, q, :], ACT.Relu,
                                             bias=b1_col[:, q:q + 1]).then_inc(hid_ready, 1)

                def step(it, first):
                    e0, e1 = batch_range(act, PT, it)
                    each_batch(act, e0, e1, batch)
                    turn_half(it, 0)
                    if not first:
                        early(it - 1)
                    turn_half(it, 1)
                    if not first:
                        late(it - 1)
                    if rd.kind == GIN:
                        hidden(it, 0)
                        hidden(it, 1)

                step(0, True)
                step(1, False)
                with act.Fori(2, NPAIR) as it:
                    step(it, False)
                early(NPAIR - 1)
                late(NPAIR - 1)

        @block.tensor
        def _(pe):
            PT = mybir.EngineType.PE
            pe.wait_ge(prep_to_pe, 1)
            for q in range(4):
                last = nc.tensor.transpose(p_tr[0:NHALF, q * NHALF:(q + 1) * NHALF],
                                           touch[0:HT, q, :], ident[0:HT, 0:HT])
            last.then_inc(pe_prep, 1)
            pe.wait_ge(prep_to_pe, 2)
            nc.tensor.matmul(p_edge[0:NHALF, 0:1], before[0:NHALF, 0:NHALF], n_items[0:NHALF, 0:1],
                             start=True, stop=True)
            nc.tensor.matmul(p_wide[0:NHALF, 0, 0:NHALF], ones[0:NHALF, 0:NHALF], diag[0:NHALF, 0:NHALF],
                             start=True, stop=True).then_inc(pe_prep, 1)
            pe.wait_ge(prep_to_pe, 3)
            nc.tensor.matmul(p_wide[0:NHALF, 1, 0:1], ahead[0:NHALF, 0:NHALF], n_batches[0:NHALF, 0:1],
                             start=True, stop=True).then_inc(pe_prep, 1)
            pe.wait_ge(lists_in, 16)
            for r, rd in enumerate(rounds):
                s = R[r]
                pe.wait_ge(s.weights_in, 16 * len(round_weights(rd)) + s.before["weights_in"])
                if rd.kind == GCN and rd.layer == 1:
                    pe.wait_ge(const_pe, 1)
                    nc.tensor.matmul(p_wide[:, 0, 0:D], t_rep[:, :], w[:, 1, :], start=True, stop=True
                                     ).then_inc(const_used, 1)
                pe.sem_inc(s.oh_used, OH)
                if rd.kind == GIN:
                    pe.sem_inc(emb_used, 1)
                if rd.kind == RGCN:
                    pe.sem_inc(s.sel_step, REL)

                def item(a, t0, i0, i, first):
                    wait_apart(pe, s.oh_ready, i + 1)
                    t = tile_of(t0, i0, i)
                    oh = tile_ap(onehot, (i % OH).with_bounds(min_val=0, max_val=OH - 1))
                    if r == 0:
                        nc.tensor.matmul(p_edge[:, :], flat(ecol[:, bass.ds(t, 32), :]), oh, start=first,
                                         stop=True, skip_group_check=True)
                    nc.tensor.matmul(p_agg[:, a, :], tile_ap(msg, t, 0, D), oh, start=first, stop=True,
                                     skip_group_check=True)
                    nc.tensor.matmul(p_agg[:, a, :], tile_ap(msg, t, D, 2 * D), oh, start=False, stop=True,
                                     skip_group_check=True).then_inc(s.oh_used, 1)

                def batch(e):
                    if rd.kind == GIN:
                        for q, (j0, j1) in enumerate(((0, 4), (4, BATCH))):
                            if q == 0:
                                wait_apart(pe, attr_ready, e + 1)
                            pe.wait_ge(emb_used, 2 * e + (q + 1))
                            for j in range(j0, j1):
                                last = nc.tensor.matmul(
                                    p_edge[:, (j - j0) * D:(j - j0 + 1) * D],
                                    attr_now[0:BATCH * DE + 1, :], bond[0:BATCH * DE + 1, j, :], start=True, stop=True)
                            last.then_inc(emb_done, 1)
                    elif rd.kind == RGCN:
                        def transposed(j):
                            t = (e * BATCH + j).with_bounds(min_val=0, max_val=TILES - 1)
                            out = (p_edge, p_tr)[j % 2][:, 0:P]
                            nc.tensor.matmul(out, tile_ap(msg, t, 0, D), ident16[:, :], start=True, stop=False)
                            nc.tensor.matmul(out, tile_ap(msg, t, D, 2 * D), ident16[:, :], start=False, stop=True
                                             ).then_inc(s.et_done, 1)

                        wait_apart(pe, s.lo_done, e + 1 + s.before["lo_done"])
                        transposed(0)
                        for j in range(BATCH):
                            if j + 1 < BATCH:
                                transposed(j + 1)
                            pe.wait_ge(s.et_ready, e * BATCH + (j + 1) + s.before["et_ready"])
                            for q in range(2):
                                pe.wait_ge(s.sel_step, e * (REL * BATCH) + (REL * j + 4 * q + 4) + s.before["sel_step"])
                                nc.tensor.matmul(p_wide[:, q, :], edge_t[:, j % 2, :],
                                                 flat(w[:, 4 * q:4 * q + 4, :]), start=True, stop=True
                                                 ).then_inc(s.rel_done, 1)

                def half(it, a):
                    t0, i0, i1 = item_range(pe, PT, it, a)
                    if r == 0 and not (is_zero(it) and a == 0):
                        wait_apart(pe, deg_used, it * 2 + a)
                    if not is_zero(it):
                        wait_apart(pe, s.agg_done, it * 2 + (a - 1) + s.before["agg_done"])
                    item(a, t0, i0, i0, True)
                    with pe.Fori(i0 + 1, i1) as i:
                        item(a, t0, i0, i, False)
                    if not (is_zero(it) and a == 0):
                        pe.wait_ge(s.ht_done, it * 2 + a + s.before["ht_done"])
                    if a == 0:
                        wait_apart(pe, s.h_loaded, it * 16 + 16 + s.before["h_loaded"])
                    for b in range(4):
                        last = nc.tensor.transpose(p_tr[:, b * P:(b + 1) * P], h_in[:, 4 * a + b, :], ident[:, :])
                    last.then_inc(s.tr_done, 1)
                    if r == 0:
                        pe.wait_ge(deg_copied, it * 2 + (a + 1))
                        for b in range(4):
                            last = nc.tensor.matmul(p_edge[:, 2 * b:2 * b + 2], deg_rows[:, b * P:(b + 1) * P],
                                                    deg_sel[:, :], start=True, stop=True)
                        last.then_inc(deg_tr, 1)

                def dense(it, a):
                    if not is_zero(it):
                        pe.wait_ge(s.u_done, it + s.before["u_done"])
                    if rd.kind == GIN:
                        pe.wait_ge(hid_ready, it * 4 + (2 * a + 2))
                        for b in range(4):
                            for q in range(2):
                                last = nc.tensor.matmul(
                                    p_dense[:, a, b * D:(b + 1) * D], hid[:, a, q, b * P:(b + 1) * P],
                                    w[:, 2 + q, :], start=q == 0, stop=q == 1)
                        last.then_inc(s.dense_done, 1)
                        return
                    pe.wait_ge(s.agg_done, it * 2 + (a + 1) + s.before["agg_done"])
                    if rd.kind != GCN:
                        pe.wait_ge(s.ht_done, it * 2 + (a + 1) + s.before["ht_done"])
                    for b in range(4):
                        sl = slice(b * D, (b + 1) * D)
                        if rd.kind == SAGE:
                            nc.tensor.matmul(p_wide[:, a, sl], agg_t[:, a, sl], w[:, 0, :], start=True, stop=True)
                            last = nc.tensor.matmul(p_dense[:, a, sl], h_t[:, a, sl], w[:, 1, :],
                                                    start=True, stop=True)
                        elif rd.kind == GCN:
                            last = nc.tensor.matmul(p_dense[:, a, sl], agg_t[:, a, sl], w[:, 0, :],
                                                    start=True, stop=True)
                        else:
                            nc.tensor.matmul(p_dense[:, a, sl], agg_t[:, a, sl], ident[:, :], start=True, stop=False)
                            last = nc.tensor.matmul(p_dense[:, a, sl], h_t[:, a, sl], w[:, REL, :],
                                                    start=False, stop=True)
                    last.then_inc(s.dense_done, 1)

                def hidden(it, a):
                    pe.wait_ge(s.agg_done, it * 2 + (a + 1) + s.before["agg_done"])
                    for q in range(2):
                        if not (is_zero(it) and a == 0):
                            pe.wait_ge(hid_ready, it * 4 + (2 * a + q - 1))
                        nc.tensor.matmul(p_wide[:, q, :], w[:, q, :], agg_t[:, a, :], start=True, stop=True
                                         ).then_inc(hid_done, 1)

                def step(it):
                    if rd.kind in (GIN, RGCN):
                        e0, e1 = batch_range(pe, PT, it)
                        each_batch(pe, e0, e1, batch)
                    half(it, 0)
                    half(it, 1)
                    if rd.kind == GIN:
                        hidden(it, 0)
                        hidden(it, 1)
                    dense(it, 0)
                    dense(it, 1)

                step(0)
                with pe.Fori(1, NPAIR) as it:
                    step(it)

        @block.vector
        def _(dve):
            PT = mybir.EngineType.DVE
            V = nc.vector
            prepared = [0]

            def link(ins):
                prepared[0] += 1
                ins.then_inc(dve_prep, 1)
                dve.wait_ge(dve_prep, prepared[0])

            V.memset(dst_rows[:, :, :], -1)
            V.memset(bond[:, :, :], 0.0)
            V.memset(attr_now[:, :], 1.0).then_inc(pads_set, 1)
            V.memset(ecol[:, :, 0:3], 0.0)
            V.memset(ecol[:, :, 3:4], 1.0)
            V.memset(eps_col[:, :], EPS)
            V.memset(ones[:, :], 1.0)
            dve.wait_ge(iotas, 3)
            V.tensor_copy(iota[:, :], col_i[:, :])
            V.tensor_copy(colf[:, :], col_i[:, 0:P])
            V.tensor_copy(basef[:, :], base_i[:, :])
            link(V.tensor_copy(rowf[:, :], row_i[:, :]))
            for a in range(2):
                link(V.memset(basef[:, NHALF - 2 + a:NHALF - 1 + a], float(TAIL + a * HALF)))
            V.tensor_scalar(negbase[:, :], basef[:, :], -1.0, None, ALU.mult)
            V.tensor_scalar(ident[:, :], colf[:, :], rowf[:, 0:1], None, ALU.is_equal)
            V.tensor_scalar(ident16[:, :], colf[:, :], rowf[:, 0:1], None, ALU.is_equal)
            V.tensor_scalar(before[:, :], colf[:, :], rowf[:, 0:1], None, ALU.is_gt)
            V.tensor_scalar(deg_sel[:, 0:1], rowf[0:4, :], 3.0, None, ALU.is_lt)
            V.tensor_scalar(deg_sel[:, 1:2], rowf[0:4, :], 3.0, None, ALU.is_equal)
            link(V.tensor_scalar(ahead[:, :], colf[:, :], 2.0, float(NHALF - 1), ALU.add, ALU.min))
            link(V.tensor_scalar(ahead[:, :], ahead[:, :], rowf[:, 0:1], None, ALU.is_equal))
            dve.wait_ge(edges_in, 16 * edge_loads)
            V.tensor_copy(etype_f[:, :], etype_i[:, :])
            link(V.tensor_copy(dst_f[:, :], dst_i[:, :]))
            last_tile = dst_f[:, TILES - 1:TILES]
            V.tensor_scalar(col[0][:, :], rowf[:, :], float(LAST), None, ALU.is_lt)
            link(V.tensor_scalar(last_tile, last_tile, 1.0, None, ALU.add))
            link(V.tensor_tensor(last_tile, last_tile, col[0][:, :], ALU.mult))
            link(V.tensor_scalar(last_tile, last_tile, -1.0, None, ALU.add))
            for k in range(REL):
                V.tensor_scalar(mask[:, k, :], etype_f[:, :], float(k), None, ALU.is_equal)
            rest = flat(u[:, 0:2, :])[:, 0:TILES]
            part = [ecol[:, 0:TILES, k:k + 1].rearrange("p t o -> p (t o)") for k in range(3)]
            link(V.tensor_copy(part[0], ew[:, :]))
            link(V.tensor_tensor(rest, ew[:, :], part[0], ALU.subtract))
            link(V.tensor_copy(part[1], rest))
            link(V.tensor_tensor(rest, rest, part[1], ALU.subtract))
            link(V.tensor_copy(part[2], rest))

            rows, low = v[0:HT, 0:2, :], u[0:HT, 2:4, :]
            link(V.tensor_copy(rows, dst_rows[:, :, :]))
            link(V.tensor_scalar(low, rows, 0.0, 1e6, ALU.is_lt, ALU.mult))
            link(V.tensor_tensor(low, low, rows, ALU.add))
            V.tensor_reduce(t_max[:, :], rows, AX.X, ALU.max)
            link(V.tensor_reduce(t_min[:, :], low, AX.X, ALU.min))
            high, both = o[0:HT, 0, 0:NHALF], o2[0:HT, 0, 0:NHALF]
            for q in range(2):
                V.tensor_scalar(col[q][0:HT, :], rowf[0:HT, :], -1.0, float(2 * P - q * HT), ALU.mult, ALU.add)
                V.tensor_scalar(col[2 + q][0:HT, :], rowf[0:HT, :], float(1 + q * HT), None, ALU.add)
                V.tensor_scalar(high, basef[0:HT, :], t_max[:, q:q + 1], None, ALU.is_le)
                link(V.tensor_scalar(both, basef[0:HT, :], float(HALF - 1), t_min[:, q:q + 1], ALU.add, ALU.is_ge))
                link(V.tensor_tensor(both, both, high, ALU.mult))
                V.tensor_scalar(touch[:, q, :], both, col[q][0:HT, 0:1], None, ALU.mult)
                link(V.tensor_scalar(touch[:, 2 + q, :], both, col[2 + q][0:HT, 0:1], None, ALU.mult))
            V.drain().then_inc(prep_to_pe, 1)
            g = slice(0, NHALF)
            near, far, some, first, last1 = (c[g, :] for c in col[0:5])
            dve.wait_ge(pe_prep, 1)
            V.tensor_reduce(near, p_tr[g, 0:2 * NHALF], AX.X, ALU.max)
            link(V.tensor_reduce(far, p_tr[g, 2 * NHALF:4 * NHALF], AX.X, ALU.max))
            V.tensor_scalar(some, near, 0.0, None, ALU.is_gt)
            link(V.tensor_scalar(first, near, -1.0, float(2 * P), ALU.mult, ALU.add))
            link(V.tensor_tensor(first, first, some, ALU.mult))
            link(V.tensor_scalar(first, first, float(TILES - 2), None, ALU.min))
            link(V.tensor_scalar(last1, first, 2.0, None, ALU.add))
            link(V.tensor_tensor(last1, last1, far, ALU.max))
            link(V.tensor_tensor(n_items[g, :], last1, first, ALU.subtract))
            link(V.tensor_scalar(diag[g, g], ident[g, g], last1, None, ALU.mult))
            V.drain().then_inc(prep_to_pe, 1)
            needed, seen = col[5][g, :], o[g, 0, g]
            dve.wait_ge(pe_prep, 2)
            V.memset(list_f[:, :], 0.0)
            link(V.tensor_scalar(seen, colf[g, g], rowf[g, 0:1], None, ALU.is_le))
            link(V.tensor_tensor(seen, seen, p_wide[g, 0, g], ALU.mult))
            link(V.tensor_reduce(needed, seen, AX.X, ALU.max))
            link(V.tensor_scalar(o[g, 1, 0:BATCHES], colf[g, 0:BATCHES], float(BATCH), needed, ALU.mult, ALU.is_lt))
            link(V.tensor_reduce(n_batches[g, :], o[g, 1, 0:BATCHES], AX.X, ALU.add))
            V.drain().then_inc(prep_to_pe, 1)
            V.tensor_copy(list_f[:, 0:1], first)
            link(V.tensor_copy(list_f[:, 1:2], p_edge[g, 0:1]))
            link(V.tensor_tensor(list_f[:, 2:3], list_f[:, 1:2], n_items[g, :], ALU.add))
            link(V.tensor_scalar(some, rowf[g, :], 1.5, None, ALU.is_gt))
            link(V.tensor_tensor(list_f[:, 3:4], n_batches[g, :], some, ALU.mult))
            link(V.tensor_scalar(far, rowf[g, :], float(NHALF - 1), float(BATCHES), ALU.is_equal, ALU.mult))
            dve.wait_ge(pe_prep, 3)
            link(V.tensor_tensor(list_f[:, 4:5], far, p_wide[g, 1, 0:1], ALU.max))
            V.tensor_copy(list_rows[:, :], list_f[:, :]).then_inc(rows_ready, 1)
            dve.wait_ge(lists_in, 16)

            for r, rd in enumerate(rounds):
                s = R[r]
                sage, gin, gcn, rgcn = (rd.kind == k for k in (SAGE, GIN, GCN, RGCN))
                dve.wait_ge(s.weights_in, 16 * len(round_weights(rd)) + s.before["weights_in"])
                if r == 1:
                    link(V.tensor_scalar(deg[:, :], deg[:, :], 2.0, None, ALU.add))
                    V.tensor_scalar(dinv[:, :], deg[:, :], 1e-30, None, ALU.max).then_inc(deg_ready, 1)
                    dve.wait_ge(deg_root, 1)
                    link(V.reciprocal(dinv[:, :], dinv[:, :]))
                    link(V.tensor_scalar(deg[:, :], deg[:, :], 0.0, None, ALU.is_gt))
                    link(V.tensor_tensor(dinv[:, :], dinv[:, :], deg[:, :], ALU.mult))
                if gin:
                    V.tensor_scalar(one_eps[:, :], one_eps[:, :], 1.0, None, ALU.add).then_inc(const_dve, 1)
                if gcn and rd.layer == 1:
                    V.tensor_scalar(t_rep[:, :], ones[:, :], t_col[:, 0:1], None, ALU.mult).then_inc(const_pe, 1)
                    dve.wait_ge(const_used, 1)
                    link(V.tensor_tensor(bt[:, :], bt[:, :], p_wide[:, 0, 0:D], ALU.add))
                    link(V.tensor_scalar(bt[:, :], bt[:, :], 0.0, None, ALU.max))
                    link(V.tensor_tensor(bt[:, :], bt[:, :], shift[:, :], ALU.add))

                def parts_lo(e, source, slot, weight):
                    if weight is None:
                        return V.tensor_tensor(msg[:, bass.ds(e * BATCH, BATCH), D:2 * D],
                                               source[:, bass.ds(slot * BATCH, BATCH), :],
                                               msg[:, bass.ds(e * BATCH, BATCH), 0:D], ALU.subtract)
                    for j in range(BATCH):
                        t = e * BATCH + j
                        last = V.scalar_tensor_tensor(
                            out=tile_ap(msg, t, D, 2 * D), in0=tile_ap(source, slot * BATCH + j),
                            scalar=weight[:, bass.ds(t, 1)], in1=tile_ap(msg, t, 0, D),
                            op0=ALU.mult, op1=ALU.subtract)
                    return last

                if rgcn:
                    dve.sem_inc(s.split_done, 1)

                def batch(e):
                    if gin:
                        dve.wait_ge(s.lo_done, e + s.before["lo_done"])
                        for q, (j0, j1) in enumerate(((0, 4), (4, BATCH))):
                            dve.wait_ge(emb_done, 2 * e + (q + 1))
                            V.tensor_tensor(
                                edge_v[:, j0:j1, :], raw[:, bass.ds((e % RING) * BATCH + j0, j1 - j0), :],
                                p_edge[:, 0:(j1 - j0) * D].rearrange("p (j d) -> p j d", d=D),
                                ALU.add).then_inc(emb_used, 1)
                        dve.wait_ge(s.hi_done, e + 1 + s.before["hi_done"])
                        parts_lo(e, edge_v, 0, ew1).then_inc(s.lo_done, 1)
                    elif sage or gcn:
                        dve.wait_ge(s.hi_done, e + 1 + s.before["hi_done"])
                        parts_lo(e, raw, e % RING, ew if gcn else None).then_inc(s.lo_done, 1)
                    else:
                        dve.wait_ge(s.hi_done, 2 * e + 1 + s.before["hi_done"])
                        parts_lo(e, raw, e % RING, None).then_inc(s.lo_done, 1)
                        dve.wait_ge(s.split_done, e + 1 + s.before["split_done"])
                        for j in range(BATCH):
                            for k in range(REL):
                                if k % 4 == 0:
                                    dve.wait_ge(s.rel_done, e * (2 * BATCH) + (2 * j + k // 4 + 1) + s.before["rel_done"])
                                product = p_wide[:, k // 4, (k % 4) * D:(k % 4 + 1) * D]
                                chosen = mask[:, k, bass.ds(e * BATCH + j, 1)]
                                if k == 0:
                                    ins = V.tensor_scalar(edge_v[:, j, :], product, chosen, None, ALU.mult)
                                else:
                                    dve.wait_ge(s.sel_step, e * (REL * BATCH) + (REL * (j + 1) + k) + s.before["sel_step"])
                                    ins = V.scalar_tensor_tensor(out=edge_v[:, j, :], in0=product, scalar=chosen,
                                                                 in1=edge_v[:, j, :], op0=ALU.mult, op1=ALU.add)
                                ins.then_inc(s.sel_step, 1)
                        dve.wait_ge(s.hi_done, 2 * e + 2 + s.before["hi_done"])
                        parts_lo(e, edge_v, 0, None).then_inc(s.split_done, 1)

                def onehots(it, a):
                    t0, i0, i1 = item_range(dve, PT, it, a)
                    with dve.Fori(i0, i1) as i:
                        dve.wait_ge(s.oh_used, i + 1)
                        V.tensor_scalar(tile_ap(onehot, (i % OH).with_bounds(min_val=0, max_val=OH - 1)),
                                        iota[:, :], dst_f[:, bass.ds(tile_of(t0, i0, i), 1)],
                                        negbase[:, bass.ds(it * 2 + a, 1)], ALU.subtract, ALU.is_equal
                                        ).then_inc(s.oh_ready, 1)

                def sums(it, a):
                    dve.wait_ge(s.tr_done, it * 2 + (a + 1) + s.before["tr_done"])
                    if gin or gcn:
                        dve.wait_ge(s.ht_done, it * 2 + (a + 1) + s.before["ht_done"])
                        V.tensor_tensor(agg_t[:, a, :], p_agg[:, a, :], h_t[:, a, :], ALU.add).then_inc(s.agg_done, 1)
                    else:
                        V.tensor_copy(agg_t[:, a, :], p_agg[:, a, :]).then_inc(s.agg_done, 1)

                def degrees(it, a):
                    dve.wait_ge(deg_tr, it * 2 + (a + 1))
                    pairs_ = p_edge[:, 0:8].rearrange("p (b c) -> p b c", c=2)
                    at = bass.ds(it * BLOCKS + 4 * a, 4)
                    V.tensor_copy(deg[:, at], pairs_[:, :, 0:1].rearrange("p b c -> p (b c)"))
                    V.tensor_scalar(count[:, :], pairs_[:, :, 1:2].rearrange("p b c -> p (b c)"),
                                    1.0, None, ALU.max).then_inc(count_done, 1)
                    dve.wait_ge(count_done, it * 2 + (a + 1))
                    V.reciprocal(inv[:, at], count[:, :]).then_inc(deg_used, 1)

                steps = {"k": 0, "per": steps_of(rd)}

                def step_link(it, ins):
                    steps["k"] += 1
                    ins.then_inc(s.dve_step, 1)
                    dve.wait_ge(s.dve_step, it * steps["per"] + steps["k"] + s.before["dve_step"])

                def wide(row):
                    return row[:, :].unsqueeze(1).to_broadcast([P, BLOCKS, D])

                def blocks(psum):
                    return psum.rearrange("p a (b d) -> p (a b) d", d=D)

                def take(it):
                    steps["k"] = 0
                    dve.wait_ge(s.dense_done, it * 2 + 2 + s.before["dense_done"])
                    if not is_zero(it):
                        dve.wait_ge(s.out_done, it + s.before["out_done"])
                    if r == 0:
                        dve.wait_ge(deg_used, it * 2 + 2)
                    if sage or gcn:
                        scale, source = (inv, p_wide) if sage else (dinv, p_dense)
                        for b in range(BLOCKS):
                            last = V.scalar_tensor_tensor(
                                out=u[:, b, :], in0=source[:, b // 4, (b % 4) * D:(b % 4 + 1) * D],
                                scalar=scale[:, bass.ds(it * BLOCKS + b, 1)], in1=bias[:, :],
                                op0=ALU.mult, op1=ALU.add)
                        if sage:
                            step_link(it, last)
                            last = V.tensor_tensor(u[:, :, :], u[:, :, :], blocks(p_dense), ALU.add)
                    else:
                        last = V.tensor_tensor(u[:, :, :], blocks(p_dense), wide(bias), ALU.add)
                    last.then_inc(s.u_done, 1)

                def layernorm_stats(it, source, scaled, nth=0):
                    for b in range(BLOCKS):
                        last = V.bn_stats(stats[:, b, :], source[:, b, :])
                    step_link(it, last)
                    dve.sem_inc(passed, 1)
                    for b in range(BLOCKS):
                        last = V.bn_aggr(mv[:, b, :], stats[:, b, :])
                    last.then_inc(s.var_done, 1)
                    mean = mv[:, :, 0:1].rearrange("p b o -> p (b o)")
                    dve.wait_ge(s.std_done, norms_of(rd) * it + (nth + 1) + s.before["std_done"])
                    step_link(it, V.reciprocal(rstd[:, :], std[:, :]))
                    last = V.scalar_tensor_tensor(out=nmr[:, :], in0=mean, scalar=-1.0, in1=rstd[:, :],
                                                  op0=ALU.mult, op1=ALU.mult)
                    if scaled:
                        step_link(it, last)
                        at = bass.ds(it * BLOCKS, BLOCKS)
                        V.tensor_tensor(rstd_d[:, :], rstd[:, :], dinv[:, at], ALU.mult)
                        last = V.tensor_tensor(nmr_d[:, :], nmr[:, :], dinv[:, at], ALU.mult)
                    last.then_inc(s.stats_done, 1)

                def add_residual(it):
                    dve.wait_ge(s.res_loaded, it * 16 + 16 + s.before["res_loaded"])
                    ins = V.tensor_tensor(u[:, :, :], u[:, :, :], res_in[:, :, :], ALU.add)
                    ins.then_inc(s.res_used, 1)
                    dve.wait_ge(s.res_used, it + 1 + s.before["res_used"])

                def finish(it):
                    if not rd.norm:
                        return
                    if not gcn:
                        dve.wait_ge(s.u_done, it + 1 + s.before["u_done"])
                        add_residual(it)
                        layernorm_stats(it, u, gin)
                        return
                    dve.wait_ge(s.relu_done, it + 1 + s.before["relu_done"])
                    layernorm_stats(it, v, rd.layer == 1)
                    dve.wait_ge(s.norm_done, it + 1 + s.before["norm_done"])
                    step_link(it, V.tensor_tensor(u[:, :, :], v[:, :, :], wide(gain), ALU.mult))
                    if rd.layer == 1:
                        if not is_zero(it):
                            dve.wait_ge(s.stored, it * 16 + s.before["stored"])
                        for b in range(BLOCKS):
                            last = V.scalar_tensor_tensor(
                                out=o[:, b, :], in0=bt[:, :], scalar=dinv[:, bass.ds(it * BLOCKS + b, 1)],
                                in1=u[:, b, :], op0=ALU.mult, op1=ALU.add)
                        last.then_inc(s.out_done, 1)
                        return
                    step_link(it, V.tensor_tensor(u[:, :, :], u[:, :, :], wide(shift), ALU.add))
                    add_residual(it)
                    layernorm_stats(it, u, False, nth=1)

                def step(it):
                    e0, e1 = batch_range(dve, PT, it)
                    each_batch(dve, e0, e1, batch)
                    onehots(it, 0)
                    if r == 0:
                        sums(it, 0)
                        degrees(it, 0)
                    if not is_zero(it):
                        take(it - 1)
                    onehots(it, 1)
                    if r:
                        sums(it, 0)
                    sums(it, 1)
                    if r == 0:
                        degrees(it, 1)
                    if not is_zero(it):
                        finish(it - 1)

                step(0)
                step(1)
                with dve.Fori(2, NPAIR) as it:
                    step(it)
                take(NPAIR - 1)
                finish(NPAIR - 1)
                assert steps["k"] == steps["per"]


def kernel(**inputs):
    import numpy as _np
    import concourse.bacc as _bacc
    from concourse import mybir as _mybir
    from concourse.bass_utils import run_bass_kernel_spmd as _run

    edge_arrays = ("src", "dst", "edge_weight", "edge_weight1", "edge_type_8")

    def by_tile(a):
        full = _np.zeros(TILES * P, a.dtype)
        full[:E] = a.reshape(E)
        return _np.ascontiguousarray(full.reshape(TILES, P).T)

    def by_batch(a):
        full = _np.zeros((TILES * P, DE), a.dtype)
        full[:E] = a
        return _np.ascontiguousarray(full.reshape(BATCHES, BATCH, P, DE).transpose(0, 1, 3, 2)).reshape(
            BATCHES, BATCH * DE, P)

    nc = _bacc.Bacc("TRN2", target_bir_lowering=False, num_devices=1)
    laid = {"dst_flat": _np.ascontiguousarray(inputs["dst"])}
    for name, a in inputs.items():
        a = _np.asarray(a)
        if name in edge_arrays:
            a = by_tile(a)
        elif name == "edge_attr_16":
            a = by_batch(a)
        elif name == "L1_gnn_b1":
            a = a.reshape(2, P).T
        laid[name] = _np.ascontiguousarray(a)
    arrays, aps = {}, {}
    for name, a in laid.items():
        arrays[f"in_{name}"] = a
        aps[name] = nc.dram_tensor(f"in_{name}", a.shape, _mybir.dt.from_np(a.dtype), kind="ExternalInput").ap()
    out = nc.dram_tensor("out", (N, D), F32, kind="ExternalOutput").ap()
    build_gnn(nc, aps, out)
    return _run(nc, [arrays], core_ids=[0]).results[0]["out"]
```

```python
from contextlib import ExitStack

import concourse.bass as bass
from concourse import mybir

F32 = mybir.dt.float32
F16 = mybir.dt.float16
I32 = mybir.dt.int32
ALU = mybir.AluOpType
ACT = mybir.ActivationFunctionType
AX = mybir.AxisListType

P = 128
N, E, D = 50000, 25000, 128
TILES = -(-E // P)
LAST = E - (TILES - 1) * P
BATCH = 7
BATCHES = TILES // BATCH
RING = 4
HALF = 512
PAIR = 2 * HALF
NPAIR = -(-N // PAIR)
NHALF = 2 * NPAIR
BLOCKS = PAIR // P
TOP = N - PAIR
EVERY = 2
MORE = 2
REL = 8
DE = 16
HT = TILES // 2
TURNS = BATCHES // RING
LROW = 8
EPS = 1e-5
assert TILES % BATCH == 0 and BATCHES % RING == 0 and TILES % 2 == 0

SAGE, GIN, GCN, RGCN = "sage", "gin", "gcn", "rgcn"


class Round:

    def __init__(self, kind, layer, source, out, res=None, relu=False, norm=False):
        self.kind, self.layer, self.source, self.out = kind, layer, source, out
        self.res, self.relu, self.norm = res, relu, norm


class RoundSemaphores:

    def __init__(self, counted, before, oh_ready, oh_used):
        self.before, self.oh_ready, self.oh_used = before, oh_ready, oh_used
        self.weights_in = counted["weights_in"]
        self.h_loaded = [counted["h_loaded0"], counted["h_loaded1"]]
        self.stored = counted["stored"]
        self.stored2 = counted["stored2"]
        self.res_loaded = counted["res_loaded"]
        self.res_used = counted["res_used"]
        self.idx_ready = counted["idx_ready"]
        self.batch_in = counted["batch_in"]
        self.hi_done = counted["hi_done"]
        self.lo_done = counted["lo_done"]
        self.split_done = counted["split_done"]
        self.tr_done = counted["tr_done"]
        self.ht_done = counted["ht_done"]
        self.agg_done = counted["agg_done"]
        self.dense_done = counted["dense_done"]
        self.u_done = counted["u_done"]
        self.out_done = counted["out_done"]
        self.relu_done = counted["relu_done"]
        self.var_done = [counted["var_done0"], counted["var_done1"]]
        self.std_done = [counted["std_done0"], counted["std_done1"]]
        self.stats_done = [counted["stats_done0"], counted["stats_done1"]]
        self.bn_done = [counted["bn_done0"], counted["bn_done1"]]
        self.rstd_step = [counted["rstd_step0"], counted["rstd_step1"]]
        self.norm_done = counted["norm_done"]
        self.scaled_done = counted["scaled_done"]
        self.gain_step = counted["gain_step"]
        self.every_ready = counted["every_ready"]
        self.every_used = counted["every_used"]
        self.et_done = counted["et_done"]
        self.et_ready = counted["et_ready"]
        self.rel_done = counted["rel_done"]
        self.low_chosen = counted["low_chosen"]
        self.high_chosen = counted["high_chosen"]
        self.tile_summed = counted["tile_summed"]


ROUNDS = [
    Round(SAGE, 0, "x", "s1", relu=True),
    Round(SAGE, 1, "s1", "s2", relu=True),
    Round(SAGE, 2, "s2", "x1", res="x", norm=True),
    Round(GIN, 0, "x1", "x2", res="x1", norm=True),
    Round(GCN, 1, "s1", "s2", relu=True, norm=True),
    Round(GCN, 2, "s2", "x3", res="x2", relu=True, norm=True),
    Round(RGCN, 1, "x3", "s1", relu=True),
    Round(RGCN, 2, "s1", "out", res="x3", norm=True),
]
NROUNDS = len(ROUNDS)


def build_gnn(nc, A, out_ap, rounds=ROUNDS):
    ctx = ExitStack()
    with ctx:
        def sb(name, shape, dt=F32):
            return ctx.enter_context(nc.sbuf_tensor(name, shape, dt))

        def ps(name, shape):
            return ctx.enter_context(nc.psum_tensor(name, shape, F32))

        def sem(name):
            return ctx.enter_context(nc.semaphore(name))

        dram = {"x": A["x"], "out": out_ap}
        for name in ("s1", "s2", "x1", "x2", "x3"):
            dram[name] = nc.dram_tensor(f"node_{name}", (N, D), F32, kind="Internal").ap()
        list_dram = nc.dram_tensor("list_scratch", (NHALF, LROW), I32, kind="Internal").ap()

        raw = sb("raw", [P, RING * BATCH, D])
        msg = sb("msg", [P, TILES, 2 * D], F16)
        edge_v = sb("edge_v", [P, BATCH, D])
        attr = sb("attr", [BATCH * DE, RING, P])
        attr_now = sb("attr_now", [P, P])
        src_i = sb("src_i", [P, TILES], I32)
        idx_now = sb("idx_now", [P, RING * BATCH], I32)
        dst_f = sb("dst_f", [P, TILES])
        etype_f = sb("etype_f", [P, TILES])
        ew = sb("ew", [P, TILES])
        ew1 = sb("ew1", [P, TILES])
        mask = sb("mask", [P, TILES, REL])
        ecol = sb("ecol", [P, TILES, 4], F16)
        edge_t = sb("edge_t", [P, 2, P])
        onehot = sb("onehot", [P, 2 * EVERY + MORE, HALF], F16)
        h_in = sb("h_in", [P, BLOCKS, D])
        h_t = sb("h_t", [P, 2, HALF])
        agg_t = sb("agg_t", [P, 2, HALF])
        res_in = sb("res_in", [P, BLOCKS, D])
        u = sb("u", [P, BLOCKS, D])
        v = sb("v", [P, BLOCKS, D])
        o = sb("o", [P, BLOCKS, D])
        o2 = sb("o2", [P, BLOCKS, D])
        hid = sb("hid", [P, 2, 2, HALF])
        chosen = hid.rearrange("p a q (k d) -> p a (q k) d", d=D)
        count = sb("count", [P, 4])
        stats = [sb(f"stats{n}", [P, BLOCKS, 6]) for n in range(2)]
        mv = [sb(f"mv{n}", [P, BLOCKS, 2]) for n in range(2)]
        std = [sb(f"std{n}", [P, BLOCKS]) for n in range(2)]
        eps_col = sb("eps_col", [P, 1])
        rstd = [sb(f"rstd{n}", [P, BLOCKS]) for n in range(2)]
        nmr = [sb(f"nmr{n}", [P, BLOCKS]) for n in range(2)]
        rstd_d = sb("rstd_d", [P, BLOCKS])
        nmr_d = sb("nmr_d", [P, BLOCKS])
        deg = sb("deg", [P, NHALF * 4])
        inv = sb("inv", [P, NHALF * 4])
        dinv = sb("dinv", [P, NHALF * 4])
        w = sb("w", [P, REL + 1, D])
        bond = sb("bond", [P, BATCH, D])
        bias = sb("bias", [P, D])
        gain = sb("gain", [P, D])
        shift = sb("shift", [P, D])
        b1_col = sb("b1_col", [P, 2])
        one_eps = sb("one_eps", [P, 1])
        t_col = sb("t_col", [P, 1])
        t_rep = sb("t_rep", [P, P])
        bt = sb("bt", [P, D])
        col_i = sb("col_i", [P, HALF], I32)
        row_i = sb("row_i", [P, 1], I32)
        base_i = sb("base_i", [P, NHALF], I32)
        colf = sb("colf", [P, P])
        rowf = sb("rowf", [P, 1])
        iota = sb("iota", [P, HALF], F16)
        basef = sb("basef", [P, NHALF])
        negbase = sb("negbase", [P, NHALF])
        ident = sb("ident", [P, P])
        ident16 = sb("ident16", [P, P], F16)
        ones = sb("ones", [P, P])
        lists = sb("lists", [1, NHALF * LROW], I32)

        dst_i = sb("dst_i", [P, TILES], I32)
        etype_i = sb("etype_i", [P, TILES], I32)
        dst_rows = sb("dst_rows", [HT, 2, P], I32)
        before, diag, ahead = (edge_v[:, k, :] for k in range(3))
        touch = edge_v[0:HT, 3:7, 0:NHALF]
        list_f = sb("list_f", [NHALF, LROW])
        list_rows = sb("list_rows", [NHALF, LROW], I32)
        t_max, t_min = sb("t_max", [HT, 2]), sb("t_min", [HT, 2])
        col = [sb(f"setup_col{k}", [P, 1]) for k in range(8)]
        n_items, n_batches = sb("n_items", [P, 1]), sb("n_batches", [P, 1])
        edge_arrays = [("src", src_i), ("edge_weight", ew), ("edge_weight1", ew1), ("dst", dst_i),
                       ("edge_type_8", etype_i)]
        edge_loads = len(edge_arrays) + 3

        p_agg = ps("p_agg", [P, 2, HALF])
        p_dense = ps("p_dense", [P, 2, HALF])
        p_wide = ps("p_wide", [P, 2, HALF])
        p_tr = ps("p_tr", [P, HALF])
        p_edge = ps("p_edge", [P, HALF])

        pads_set = sem("pads_set")
        edges_in = sem("edges_in")
        iotas = sem("iotas")
        dve_prep = sem("dve_prep")
        prep_to_pe = sem("prep_to_pe")
        pe_prep = sem("pe_prep")
        rows_ready = sem("rows_ready")
        rows_stored = sem("rows_stored")
        lists_in = sem("lists_in")
        passed = sem("passed")

        def adds(rd):
            first, second = NPAIR * (norms_of(rd) > 0), NPAIR * (norms_of(rd) > 1)
            rgcn = rd.kind == RGCN
            return dict(
                weights_in=16 * len(round_weights(rd)), h_loaded0=16 * NPAIR, h_loaded1=16 * NPAIR,
                stored=16 * NPAIR, stored2=16 * NPAIR if rd.kind == GIN else 0,
                res_loaded=16 * NPAIR if rd.res else 0, res_used=NPAIR if rd.res else 0,
                idx_ready=BATCHES, batch_in=BATCHES, hi_done=(1 + rgcn) * BATCHES, lo_done=BATCHES,
                tr_done=NHALF, ht_done=NHALF, agg_done=NHALF, dense_done=NHALF, u_done=NHALF,
                every_ready=NHALF, every_used=NHALF, out_done=NPAIR,
                relu_done=NPAIR if rd.relu and rd.norm else 0, norm_done=NPAIR if rd.kind == GCN else 0,
                var_done0=first, var_done1=second, std_done0=first, std_done1=second,
                stats_done0=first, stats_done1=second, bn_done0=first, bn_done1=second,
                rstd_step0=first * (1 + scaled_by_dinv(rd)), rstd_step1=second,
                scaled_done=NHALF if rd.kind == SAGE else 0,
                gain_step=NPAIR * rd.layer if rd.kind == GCN else 0,
                split_done=BATCHES + 1 if rgcn else 0, et_done=TILES * rgcn, et_ready=TILES * rgcn,
                rel_done=2 * TILES * rgcn, low_chosen=(TILES + 1) * rgcn, high_chosen=(TILES + 1) * rgcn,
                tile_summed=(TILES + 2) * rgcn)

        gathered = [sem(f"gathered{q}") for q in range(RING)]
        attr_ready, emb_done, emb_used, gelu_done = sem("attr_ready"), sem("emb_done"), sem("emb_used"), sem("gelu_done")
        hid_done, hid_ready = sem("hid_done"), sem("hid_ready")
        deg_used = sem("deg_used")
        count_done, deg_ready, deg_root = sem("count_done"), sem("deg_ready"), sem("deg_root")
        const_pe, const_used, const_dve = sem("const_pe"), sem("const_used"), sem("const_dve")
        per_batch = [BATCH + (rd.kind == GIN) for rd in rounds]
        landed_before = [TURNS * sum(per_batch[:r]) for r in range(len(rounds))]

        def round_weights(rd):
            def rep(name):
                return A[name].partition_broadcast(P)

            if rd.kind == SAGE:
                k = rd.layer
                return [(w[:, 0, :], A[f"L0_gnn_Wl{k}"]), (w[:, 1, :], A[f"L0_gnn_Wr{k}"]),
                        (bias[:, :], rep(f"L0_gnn_bl{k}"))]
            if rd.kind == GIN:
                out = [(w[:, q, :], A["L1_gnn_W1"][:, q * D:(q + 1) * D]) for q in range(2)]
                out += [(w[:, 2 + q, :], A["L1_gnn_W2"][q * P:(q + 1) * P, :]) for q in range(2)]
                out += [(bias[:, :], rep("L1_gnn_b2")), (b1_col[:, :], A["L1_gnn_b1"]),
                        (one_eps[:, :], rep("L1_gnn_eps"))]
                for j in range(BATCH):
                    out.append((bond[j * DE:(j + 1) * DE, j, :], A["L1_gnn_bond_W"]))
                    out.append((bond[BATCH * DE:BATCH * DE + 1, j, :], A["L1_gnn_bond_b"].partition_broadcast(1)))
                return out
            if rd.kind == GCN:
                k = rd.layer
                out = [(w[:, 0, :], A[f"L2_gnn_W{k}"]), (bias[:, :], rep(f"L2_gnn_b{k}")),
                       (gain[:, :], rep(f"L2_gnn_g{k}")), (shift[:, :], rep(f"L2_gnn_be{k}"))]
                if k == 1:
                    out += [(w[:, 1, :], A["L2_gnn_Wt"]), (t_col[:, :], A["L2_gnn_t"].rearrange("(p o) -> p o", o=1)),
                            (bt[:, :], rep("L2_gnn_bt"))]
                return out
            k = rd.layer
            return [(w[:, 0:REL, :], A[f"L3_gnn_W{k}"].rearrange("r i o -> i r o")),
                    (w[:, REL, :], A[f"L3_gnn_loop_w{k}"]), (bias[:, :], rep(f"L3_gnn_b{k}"))]

        def norms_of(rd):
            return (2 if rd.kind == GCN and rd.layer == 2 else 1) if rd.norm else 0

        def scaled_by_dinv(rd):
            return rd.kind == GIN or (rd.kind == GCN and rd.layer == 1)

        def lag_of(rd):
            return 2 if rd.kind == GIN else 1

        def steps_before_loop(rd):
            return 4 if rd.kind == GCN else 3 if rd.kind == GIN else 2

        def steps_after(rd):
            return 3 if rd.kind == GCN else 2

        counted = {name: sem(name) for name in adds(rounds[0])}
        R = []
        for r, rd in enumerate(rounds):
            earlier = {name: sum(adds(x)[name] for x in rounds[:r]) for name in counted}
            R.append(RoundSemaphores(counted, earlier, sem(f"oh_ready{r}"), sem(f"oh_used{r}")))

        def is_zero(it):
            return isinstance(it, int) and it == 0

        def exists(it):
            return not isinstance(it, int) or 0 <= it < NPAIR

        def back(it, a, halves):
            return it - (halves - a + 1) // 2, (a - halves) % 2

        def load_list(eng, kind, at, count):
            return nc.values_load_multi_w_load_instructions(
                lists[0:1, bass.ds(at, count)], engines=[kind], min_val=0, max_val=NHALF * TILES)[1]

        def batch_range(eng, kind, it):
            e0, e1 = load_list(eng, kind, it * (2 * LROW) + LROW + 3, 2)
            return e0.with_bounds(min_val=0, max_val=BATCHES), e1.with_bounds(min_val=0, max_val=BATCHES)

        def first_batches(eng, kind, body):
            (end,) = load_list(eng, kind, LROW + 3, 1)
            with eng.Fori(0, end.with_bounds(min_val=1, max_val=BATCHES)) as e:
                body(e.with_bounds(min_val=0, max_val=BATCHES - 1))

        def item_range(eng, kind, it, a):
            t0, i0, i1 = load_list(eng, kind, it * (2 * LROW) + a * LROW, 3)
            return t0.with_bounds(min_val=0, max_val=TILES - EVERY), i0, i1

        def tile_of(t0, i0, i):
            return (t0 + (i - i0) + EVERY).with_bounds(min_val=0, max_val=TILES - 1)

        def ring_place(i):
            return ((i % MORE) + 2 * EVERY).with_bounds(min_val=2 * EVERY, max_val=2 * EVERY + MORE - 1)

        def each_batch(eng, e0, e1, body):
            with eng.If(e0 < e1):
                with eng.Fori(e0, e1) as e:
                    body(e.with_bounds(min_val=0, max_val=BATCHES - 1))

        def wait_apart(eng, semaphore, value):
            eng.wait_ge(semaphore, value)
            eng.sem_inc(passed, 1)

        def flat(ap):
            return ap.rearrange("p a d -> p (a d)")

        def tile_ap(buf, t, lo=None, hi=None):
            s = buf[:, bass.ds(t, 1), :] if lo is None else buf[:, bass.ds(t, 1), lo:hi]
            return flat(s)

        block = ctx.enter_context(nc.Block())

        @block.sync
        def _(sp):
            sp.wait_ge(pads_set, 1)
            for name, buf in edge_arrays:
                sp.dma_start(buf[:, :], A[name]).then_inc(edges_in, 16)
            flat_dst = A["dst_flat"]
            sp.dma_start(dst_rows[:, 0, :], flat_dst[0:HT * P].rearrange("(p e) -> p e", e=P)).then_inc(edges_in, 16)
            sp.dma_start(dst_rows[0:HT - 1, 1, :],
                         flat_dst[HT * P:(TILES - 1) * P].rearrange("(p e) -> p e", e=P)).then_inc(edges_in, 16)
            sp.dma_start(dst_rows[HT - 1:HT, 1, 0:LAST],
                         flat_dst[(TILES - 1) * P:E].rearrange("(p e) -> p e", p=1)).then_inc(edges_in, 16)
            sp.wait_ge(rows_ready, 1)
            sp.dma_start(list_dram, list_rows[0:NHALF, :]).then_inc(rows_stored, 16)
            sp.wait_ge(rows_stored, 16)
            sp.dma_start(lists[0:1, :], list_dram.rearrange("(o g) c -> o (g c)", o=1)).then_inc(lists_in, 16)

            for r, rd in enumerate(rounds):
                s = R[r]
                if r:
                    sp.wait_ge(R[r - 1].stored, 16 * NPAIR + R[r - 1].before["stored"])
                    if rounds[r - 1].kind == GIN:
                        sp.wait_ge(R[r - 1].stored2, 16 * NPAIR + R[r - 1].before["stored2"])
                for dst_ap, src_ap in round_weights(rd):
                    sp.dma_start(dst_ap, src_ap).then_inc(s.weights_in, 16)
                src_d, out_d = dram[rd.source], dram[rd.out]

                def rows_of(d, base):
                    return d[bass.ds(base, PAIR), :].rearrange("(b p) d -> p b d", p=P)

                def half_of(it, a):
                    return (0 if isinstance(it, int) and it == NPAIR - 1 else it * (-PAIR) + TOP) + a * HALF

                def load(it, a):
                    if not is_zero(it):
                        sp.wait_ge(s.tr_done, it * 2 + (a - 1) + s.before["tr_done"])
                    sp.dma_start(h_in[:, 4 * a:4 * a + 4, :],
                                 src_d[bass.ds(half_of(it, a), HALF), :].rearrange("(b p) d -> p b d", p=P)
                                 ).then_inc(s.h_loaded[a], 16)

                def load_residual(it):
                    if not exists(it) or not rd.res:
                        return
                    if not is_zero(it):
                        sp.wait_ge(s.res_used, it + s.before["res_used"])
                    sp.dma_start(res_in[:, :, :], rows_of(dram[rd.res], half_of(it, 0))).then_inc(s.res_loaded, 16)

                def store(it):
                    if not exists(it):
                        return
                    if isinstance(it, int) and it == NPAIR - 1:
                        sp.wait_ge(s.stored, 16 * it + s.before["stored"])
                        if rd.kind == GIN:
                            sp.wait_ge(s.stored2, 16 * it + s.before["stored2"])
                    sp.wait_ge(s.out_done, it + 1 + s.before["out_done"])
                    sp.dma_start(rows_of(out_d, half_of(it, 0)), o[:, :, :]).then_inc(s.stored, 16)
                    if rd.kind == GIN:
                        sp.dma_start(rows_of(dram["s1"], half_of(it, 0)), o2[:, :, :]).then_inc(s.stored2, 16)

                def step(it):
                    if rd.kind == GIN:
                        store(it - 2)
                    elif rd.kind == GCN and rd.layer == 2:
                        store(it - 3)
                    elif not rd.norm:
                        store(it - 1)
                    if rd.kind in (SAGE, RGCN):
                        load_residual(it)
                    if exists(it + 1):
                        load(it + 1, 0)
                    if rd.kind == GIN:
                        load_residual(it)
                    if exists(it + 1):
                        load(it + 1, 1)
                    if rd.kind == GCN:
                        load_residual(it - 1)
                        if rd.layer == 1:
                            store(it - 2)
                    elif rd.norm and rd.kind != GIN:
                        store(it - 1)

                load(0, 0)
                load(0, 1)
                for it in range(steps_before_loop(rd)):
                    step(it)
                with sp.Fori(steps_before_loop(rd), NPAIR - 2) as it:
                    step(it)
                for it in range(NPAIR - 2, NPAIR + steps_after(rd)):
                    step(it)
            sp.wait_ge(R[-1].stored, 16 * NPAIR + R[-1].before["stored"])

        @block.gpsimd
        def _(pool):
            nc.gpsimd.iota(col_i[:, :], pattern=[[1, HALF]], base=0, channel_multiplier=0).then_inc(iotas, 1)
            nc.gpsimd.iota(row_i[:, :], pattern=[[0, 1]], base=0, channel_multiplier=1).then_inc(iotas, 1)
            nc.gpsimd.iota(base_i[:, :], pattern=[[-PAIR, NPAIR], [HALF, 2]], base=TOP,
                           channel_multiplier=0).then_inc(iotas, 1)
            pool.wait_ge(edges_in, 16 * edge_loads)
            for r, rd in enumerate(rounds):
                s = R[r]
                if r:
                    pool.wait_ge(R[r - 1].stored, 16 * NPAIR + R[r - 1].before["stored"])
                    if rounds[r - 1].kind == GIN:
                        pool.wait_ge(R[r - 1].stored2, 16 * NPAIR + R[r - 1].before["stored2"])
                src_d = dram[rd.source]

                def pass_on(q, turns):
                    wait_apart(pool, gathered[q], turns * (16 * per_batch[r]) + 16 * landed_before[r])
                    pool.sem_inc(s.batch_in, 1)

                def turn(k, first):
                    for q in range(RING):
                        if not first:
                            pool.wait_ge(s.lo_done, RING * k + (q - RING + 1) + s.before["lo_done"])
                        nc.gpsimd.tensor_copy(
                            idx_now[:, q * BATCH:(q + 1) * BATCH],
                            src_i[:, bass.ds((k * RING + q) * BATCH, BATCH)]).then_inc(s.idx_ready, 1)
                        wait_apart(pool, s.idx_ready, RING * k + (q + 1) + s.before["idx_ready"])
                        for j in range(q * BATCH, (q + 1) * BATCH):
                            nc.gpsimd.indirect_dma_start(
                                out=raw[:, j, :], out_offset=None, in_=src_d,
                                in_offset=bass.IndirectOffsetOnAxis(ap=idx_now[:, j:j + 1], axis=0),
                            ).then_inc(gathered[q], 16)
                        if rd.kind == GIN:
                            pool.dma_start(attr[:, q, :], A["edge_attr_16"][bass.ds(k * RING + q, 1), :, :].rearrange(
                                "o f e -> f (o e)")).then_inc(gathered[q], 16)
                        if q:
                            pass_on(q - 1, k + 1)
                        elif not first:
                            pass_on(RING - 1, k)

                turn(0, True)
                with pool.Fori(1, TURNS) as k:
                    turn(k, False)
                pass_on(RING - 1, TURNS)

        @block.scalar
        def _(act):
            PT = mybir.EngineType.Activation
            act.wait_ge(lists_in, 16)
            for r, rd in enumerate(rounds):
                s = R[r]
                act.wait_ge(s.weights_in, 16 * len(round_weights(rd)) + s.before["weights_in"])
                if r == 1:
                    act.wait_ge(deg_ready, 1)
                    nc.scalar.activation(dinv[:, :], dinv[:, :], ACT.Sqrt).then_inc(deg_root, 1)
                if rd.kind == GIN:
                    act.wait_ge(const_dve, 1)

                def parts_hi(e, source, slot, weight):
                    if weight is None:
                        nc.scalar.activation(msg[:, bass.ds(e * BATCH, BATCH), 0:D],
                                             source[:, bass.ds(slot * BATCH, BATCH), :], ACT.Copy
                                             ).then_inc(s.hi_done, 1)
                        return
                    for j in range(BATCH):
                        last = nc.scalar.activation(
                            tile_ap(msg, e * BATCH + j, 0, D), tile_ap(source, slot * BATCH + j), ACT.Copy,
                            scale=weight[:, bass.ds(e * BATCH + j, 1)])
                    last.then_inc(s.hi_done, 1)

                def batch(e):
                    wait_apart(act, s.batch_in, e + 1 + s.before["batch_in"])
                    if rd.kind == SAGE:
                        parts_hi(e, raw, e % RING, None)
                    elif rd.kind == GCN:
                        parts_hi(e, raw, e % RING, ew)
                    elif rd.kind == GIN:
                        nc.scalar.activation(attr_now[0:BATCH * DE, :], tile_ap(attr, (e % RING)), ACT.Copy
                                             ).then_inc(attr_ready, 1)
                        act.wait_ge(emb_used, 2 * e + 3)
                        nc.scalar.activation(flat(edge_v[:, :, :]), flat(edge_v[:, :, :]), ACT.Gelu
                                             ).then_inc(gelu_done, 1)
                        wait_apart(act, gelu_done, e + 1)
                        parts_hi(e, edge_v, 0, ew1)
                    else:
                        parts_hi(e, raw, e % RING, None)
                        def transposed(j):
                            act.wait_ge(s.et_done, e * BATCH + (j + 1) + s.before["et_done"])
                            nc.scalar.activation(edge_t[:, j % 2, :], (p_edge, p_tr)[j % 2][:, 0:P], ACT.Copy
                                                 ).then_inc(s.et_ready, 1)

                        def choose(j):
                            wait_apart(act, s.tile_summed, e * BATCH + max(j + 1, 2) + s.before["tile_summed"])
                            wait_apart(act, s.rel_done, e * (2 * BATCH) + (2 * j + 2) + s.before["rel_done"])
                            for k in range(4):
                                last = nc.scalar.activation(
                                    chosen[:, j % 2, 4 + k, :],
                                    p_wide[:, 1, k * D:(k + 1) * D], ACT.Copy,
                                    scale=tile_ap(mask, e * BATCH + j, 4 + k, 5 + k))
                            last.then_inc(s.high_chosen, 1)

                        transposed(0)
                        for j in range(BATCH):
                            if j + 1 < BATCH:
                                transposed(j + 1)
                            choose(j)
                        wait_apart(act, s.tile_summed, (e + 1) * BATCH + 2 + s.before["tile_summed"])
                        nc.scalar.activation(msg[:, bass.ds(e * BATCH, BATCH), 0:D], edge_v[:, :, :],
                                             ACT.Copy).then_inc(s.hi_done, 1)

                def turn_half(it, a):
                    act.wait_ge(s.tr_done, it * 2 + (a + 1) + s.before["tr_done"])
                    scale = {GIN: one_eps[:, 0:1], GCN: 2.0}.get(rd.kind, 1.0)
                    nc.scalar.activation(h_t[:, a, :], p_tr[:, :], ACT.Copy, scale=scale).then_inc(s.ht_done, 1)

                def store_free(it):
                    if not is_zero(it):
                        wait_apart(act, s.stored, it * 16 + s.before["stored"])

                def relu(it):
                    if not exists(it) or not rd.relu:
                        return
                    act.wait_ge(s.u_done, it * 2 + 2 + s.before["u_done"])
                    if rd.norm:
                        if not is_zero(it):
                            act.wait_ge(s.norm_done, it + s.before["norm_done"])
                        nc.scalar.activation(v[:, :, :], u[:, :, :], ACT.Relu).then_inc(s.relu_done, 1)
                    else:
                        store_free(it)
                        nc.scalar.activation(o[:, :, :], u[:, :, :], ACT.Relu).then_inc(s.out_done, 1)

                def normalise(dst, source, scale, shift_):
                    for b in range(BLOCKS):
                        last = nc.scalar.activation(dst[:, b, :], source[:, b, :], ACT.Identity,
                                                    bias=shift_[:, b:b + 1], scale=scale[:, b:b + 1])
                    return last

                def deviation(it, n):
                    if not exists(it) or n >= norms_of(rd):
                        return
                    act.wait_ge(s.var_done[n], it + 1 + s.before[f"var_done{n}"])
                    nc.scalar.activation(std[n][:, :], mv[n][:, :, 1:2].rearrange("p b o -> p (b o)"), ACT.Sqrt,
                                         bias=eps_col[:, 0:1]).then_inc(s.std_done[n], 1)

                def first_norm(it):
                    if not exists(it):
                        return
                    wait_apart(act, s.stats_done[0], it + 1 + s.before["stats_done0"])
                    if not is_zero(it):
                        wait_apart(act, s.out_done, it + s.before["out_done"])
                    scale, move = (rstd_d, nmr_d) if rd.layer == 1 else (rstd[0], nmr[0])
                    normalise(o2, v, scale, move).then_inc(s.norm_done, 1)

                def last_norm(it):
                    if not exists(it):
                        return
                    n = norms_of(rd) - 1
                    wait_apart(act, s.stats_done[n], it + 1 + s.before[f"stats_done{n}"])
                    store_free(it)
                    source = o2 if rd.kind == GCN else v
                    if rd.kind == GIN:
                        if not is_zero(it):
                            wait_apart(act, s.stored2, it * 16 + s.before["stored2"])
                        normalise(o2, v, rstd_d, nmr_d)
                    normalise(o, source, rstd[n], nmr[n]).then_inc(s.out_done, 1)

                def hidden(it, a):
                    for q in range(2):
                        act.wait_ge(hid_done, it * 4 + (2 * a + q + 1))
                        nc.scalar.activation(hid[:, a, q, :], p_wide[:, q, :], ACT.Relu,
                                             bias=b1_col[:, q:q + 1]).then_inc(hid_ready, 1)

                def stage(it, a):
                    nxt, na = back(it, a, -1)
                    if exists(nxt):
                        turn_half(nxt, na)
                    if rd.kind == GIN and exists(it):
                        hidden(it, a)
                    pair, ta = back(it, a, lag_of(rd))
                    if rd.kind == GCN:
                        if ta == 1:
                            if rd.layer == 2:
                                last_norm(pair - 2)
                            first_norm(pair - 1)
                            relu(pair)
                        else:
                            deviation(pair - 2, 1)
                            deviation(pair - 1, 0)
                    elif ta == 1:
                        relu(pair)
                        deviation(pair, 0)
                    elif rd.norm:
                        last_norm(pair - 1)

                def batches(it):
                    if exists(it + 1):
                        e0, e1 = batch_range(act, PT, it)
                        each_batch(act, e0, e1, batch)

                def step(it):
                    if rd.kind in (SAGE, GCN):
                        batches(it)
                    stage(it, 0)
                    if rd.kind in (GIN, RGCN):
                        batches(it)
                    stage(it, 1)

                first_batches(act, PT, batch)
                turn_half(0, 0)
                for it in range(steps_before_loop(rd)):
                    step(it)
                with act.Fori(steps_before_loop(rd), NPAIR - 1) as it:
                    step(it)
                for it in range(NPAIR - 1, NPAIR + steps_after(rd)):
                    step(it)

        @block.tensor
        def _(pe):
            PT = mybir.EngineType.PE
            pe.wait_ge(prep_to_pe, 1)
            for q in range(4):
                last = nc.tensor.transpose(p_tr[0:NHALF, q * NHALF:(q + 1) * NHALF],
                                           touch[0:HT, q, :], ident[0:HT, 0:HT])
            last.then_inc(pe_prep, 1)
            pe.wait_ge(prep_to_pe, 2)
            nc.tensor.matmul(p_edge[0:NHALF, 0:1], before[0:NHALF, 0:NHALF], n_items[0:NHALF, 0:1],
                             start=True, stop=True)
            nc.tensor.matmul(p_wide[0:NHALF, 0, 0:NHALF], ones[0:NHALF, 0:NHALF], diag[0:NHALF, 0:NHALF],
                             start=True, stop=True).then_inc(pe_prep, 1)
            pe.wait_ge(prep_to_pe, 3)
            nc.tensor.matmul(p_wide[0:NHALF, 1, 0:1], ahead[0:NHALF, 0:NHALF], n_batches[0:NHALF, 0:1],
                             start=True, stop=True).then_inc(pe_prep, 1)
            pe.wait_ge(lists_in, 16)
            for r, rd in enumerate(rounds):
                s = R[r]
                pe.wait_ge(s.weights_in, 16 * len(round_weights(rd)) + s.before["weights_in"])
                if rd.kind == GCN and rd.layer == 1:
                    pe.wait_ge(const_pe, 1)
                    nc.tensor.matmul(p_wide[:, 0, 0:D], t_rep[:, :], w[:, 1, :], start=True, stop=True
                                     ).then_inc(const_used, 1)
                pe.sem_inc(s.oh_used, MORE)
                if rd.kind == GIN:
                    pe.sem_inc(emb_used, 1)
                if rd.kind == RGCN:
                    pe.sem_inc(s.low_chosen, 1)
                    pe.sem_inc(s.high_chosen, 1)

                def oh_block(slot, b):
                    return flat(onehot[:, bass.ds(slot, 1), b * P:(b + 1) * P])

                def item(a, t, slot, first):
                    oh = tile_ap(onehot, slot)
                    if r == 0:
                        for b in range(4):
                            nc.tensor.matmul(p_edge[:, 4 * b:4 * b + 4], oh_block(slot, b), tile_ap(ecol, t),
                                             start=first and b == 0, stop=True, skip_group_check=True)
                    nc.tensor.matmul(p_agg[:, a, :], tile_ap(msg, t, 0, D), oh, start=first, stop=True,
                                     skip_group_check=True)
                    return nc.tensor.matmul(p_agg[:, a, :], tile_ap(msg, t, D, 2 * D), oh, start=False, stop=True,
                                            skip_group_check=True)

                def batch(e):
                    if rd.kind == GIN:
                        for q, (j0, j1) in enumerate(((0, 4), (4, BATCH))):
                            if q == 0:
                                wait_apart(pe, attr_ready, e + 1)
                            pe.wait_ge(emb_used, 2 * e + (q + 1))
                            for j in range(j0, j1):
                                last = nc.tensor.matmul(
                                    p_edge[:, (j - j0) * D:(j - j0 + 1) * D],
                                    attr_now[0:BATCH * DE + 1, :], bond[0:BATCH * DE + 1, j, :], start=True, stop=True)
                            last.then_inc(emb_done, 1)
                    elif rd.kind == RGCN:
                        def transposed(j):
                            t = (e * BATCH + j).with_bounds(min_val=0, max_val=TILES - 1)
                            out = (p_edge, p_tr)[j % 2][:, 0:P]
                            nc.tensor.matmul(out, tile_ap(msg, t, 0, D), ident16[:, :], start=True, stop=False)
                            nc.tensor.matmul(out, tile_ap(msg, t, D, 2 * D), ident16[:, :], start=False, stop=True
                                             ).then_inc(s.et_done, 1)

                        wait_apart(pe, s.lo_done, e + 1 + s.before["lo_done"])
                        transposed(0)
                        for j in range(BATCH):
                            if j + 1 < BATCH:
                                transposed(j + 1)
                            pe.wait_ge(s.et_ready, e * BATCH + (j + 1) + s.before["et_ready"])
                            for q in range(2):
                                name = ("low_chosen", "high_chosen")[q]
                                pe.wait_ge((s.low_chosen, s.high_chosen)[q], e * BATCH + (j + 1) + s.before[name])
                                nc.tensor.matmul(p_wide[:, q, :], edge_t[:, j % 2, :],
                                                 flat(w[:, 4 * q:4 * q + 4, :]), start=True, stop=True
                                                 ).then_inc(s.rel_done, 1)

                def half(it, a):
                    t0, i0, i1 = item_range(pe, PT, it, a)
                    if r == 0 and not (is_zero(it) and a == 0):
                        wait_apart(pe, count_done, it * 2 + a)
                    if not is_zero(it):
                        wait_apart(pe, s.agg_done, it * 2 + (a - 1) + s.before["agg_done"])
                    wait_apart(pe, s.every_ready, it * 2 + (a + 1) + s.before["every_ready"])
                    for k in range(EVERY):
                        last = item(a, (t0 + k).with_bounds(min_val=0, max_val=TILES - 1), EVERY * a + k, k == 0)
                    last.then_inc(s.every_used, 1)

                    def more(i):
                        wait_apart(pe, s.oh_ready, i + 1)
                        item(a, tile_of(t0, i0, i), ring_place(i), False).then_inc(s.oh_used, 1)

                    with pe.If(i0 < i1):
                        with pe.Fori(i0, i1) as i:
                            more(i)
                    if not (is_zero(it) and a == 0):
                        pe.wait_ge(s.ht_done, it * 2 + a + s.before["ht_done"])
                    wait_apart(pe, s.h_loaded[a], it * 16 + 16 + s.before[f"h_loaded{a}"])
                    for b in range(4):
                        last = nc.tensor.transpose(p_tr[:, b * P:(b + 1) * P], h_in[:, 4 * a + b, :], ident[:, :])
                    last.then_inc(s.tr_done, 1)

                def dense(it, a):
                    if not is_zero(it):
                        pe.wait_ge(s.u_done, it * 2 + (a - 1) + s.before["u_done"])
                    if rd.kind == GIN:
                        pe.wait_ge(hid_ready, it * 4 + (2 * a + 2))
                        for b in range(4):
                            for q in range(2):
                                last = nc.tensor.matmul(
                                    p_dense[:, a, b * D:(b + 1) * D], hid[:, a, q, b * P:(b + 1) * P],
                                    w[:, 2 + q, :], start=q == 0, stop=q == 1)
                        last.then_inc(s.dense_done, 1)
                        return
                    pe.wait_ge(s.agg_done, it * 2 + (a + 1) + s.before["agg_done"])
                    if rd.kind != GCN:
                        pe.wait_ge(s.ht_done, it * 2 + (a + 1) + s.before["ht_done"])
                    for b in range(4):
                        sl = slice(b * D, (b + 1) * D)
                        if rd.kind == SAGE:
                            nc.tensor.matmul(p_wide[:, a, sl], agg_t[:, a, sl], w[:, 0, :], start=True, stop=True)
                            last = nc.tensor.matmul(p_dense[:, a, sl], h_t[:, a, sl], w[:, 1, :],
                                                    start=True, stop=True)
                        elif rd.kind == GCN:
                            last = nc.tensor.matmul(p_dense[:, a, sl], agg_t[:, a, sl], w[:, 0, :],
                                                    start=True, stop=True)
                        else:
                            nc.tensor.matmul(p_dense[:, a, sl], agg_t[:, a, sl], ident[:, :], start=True, stop=False)
                            last = nc.tensor.matmul(p_dense[:, a, sl], h_t[:, a, sl], w[:, REL, :],
                                                    start=False, stop=True)
                    last.then_inc(s.dense_done, 1)

                def hidden(it, a):
                    pe.wait_ge(s.agg_done, it * 2 + (a + 1) + s.before["agg_done"])
                    for q in range(2):
                        if not (is_zero(it) and a == 0):
                            pe.wait_ge(hid_ready, it * 4 + (2 * a + q - 1))
                        nc.tensor.matmul(p_wide[:, q, :], w[:, q, :], agg_t[:, a, :], start=True, stop=True
                                         ).then_inc(hid_done, 1)

                def batches(it):
                    if rd.kind not in (GIN, RGCN) or not exists(it + 1):
                        return
                    if rd.kind == RGCN:
                        pe.wait_ge(s.ht_done, it * 2 + 2 + s.before["ht_done"])
                    e0, e1 = batch_range(pe, PT, it)
                    each_batch(pe, e0, e1, batch)

                def stage(it, a):
                    nxt, na = back(it, a, -1)
                    if exists(nxt):
                        half(nxt, na)
                    if rd.kind == GIN:
                        if exists(it):
                            hidden(it, a)
                        last, la = back(it, a, 1)
                        if exists(last):
                            dense(last, la)
                    else:
                        dense(it, a)

                def step(it):
                    stage(it, 0)
                    batches(it)
                    stage(it, 1)

                if rd.kind in (GIN, RGCN):
                    first_batches(pe, PT, batch)
                half(0, 0)
                step(0)
                with pe.Fori(1, NPAIR - 1) as it:
                    step(it)
                step(NPAIR - 1)
                if rd.kind == GIN:
                    dense(NPAIR - 1, 1)

        @block.vector
        def _(dve):
            PT = mybir.EngineType.DVE
            V = nc.vector
            prepared = [0]

            def link(ins):
                prepared[0] += 1
                ins.then_inc(dve_prep, 1)
                dve.wait_ge(dve_prep, prepared[0])

            V.memset(dst_rows[:, :, :], -1)
            V.memset(bond[:, :, :], 0.0)
            V.memset(attr_now[:, :], 1.0).then_inc(pads_set, 1)
            V.memset(ecol[:, :, 0:3], 0.0)
            V.memset(ecol[:, :, 3:4], 1.0)
            V.memset(eps_col[:, :], EPS)
            V.memset(ones[:, :], 1.0)
            dve.wait_ge(iotas, 3)
            V.tensor_copy(iota[:, :], col_i[:, :])
            V.tensor_copy(colf[:, :], col_i[:, 0:P])
            V.tensor_copy(basef[:, :], base_i[:, :])
            link(V.tensor_copy(rowf[:, :], row_i[:, :]))
            for a in range(2):
                link(V.memset(basef[:, NHALF - 2 + a:NHALF - 1 + a], float(a * HALF)))
            V.tensor_scalar(negbase[:, :], basef[:, :], -1.0, None, ALU.mult)
            V.tensor_scalar(ident[:, :], colf[:, :], rowf[:, 0:1], None, ALU.is_equal)
            V.tensor_scalar(ident16[:, :], colf[:, :], rowf[:, 0:1], None, ALU.is_equal)
            V.tensor_scalar(before[:, :], colf[:, :], rowf[:, 0:1], None, ALU.is_gt)
            link(V.tensor_scalar(ahead[:, :], colf[:, :], 2.0, float(NHALF - 1), ALU.add, ALU.min))
            link(V.tensor_scalar(ahead[:, :], ahead[:, :], rowf[:, 0:1], None, ALU.is_equal))
            dve.wait_ge(edges_in, 16 * edge_loads)
            V.tensor_copy(etype_f[:, :], etype_i[:, :])
            link(V.tensor_copy(dst_f[:, :], dst_i[:, :]))
            last_tile = dst_f[:, TILES - 1:TILES]
            V.tensor_scalar(col[0][:, :], rowf[:, :], float(LAST), None, ALU.is_lt)
            link(V.tensor_scalar(last_tile, last_tile, 1.0, None, ALU.add))
            link(V.tensor_tensor(last_tile, last_tile, col[0][:, :], ALU.mult))
            link(V.tensor_scalar(last_tile, last_tile, -1.0, None, ALU.add))
            for k in range(REL):
                V.tensor_scalar(mask[:, :, k:k + 1].rearrange("p t o -> p (t o)"), etype_f[:, :], float(k), None, ALU.is_equal)
            rest = flat(u[:, 0:2, :])[:, 0:TILES]
            part = [ecol[:, 0:TILES, k:k + 1].rearrange("p t o -> p (t o)") for k in range(3)]
            link(V.tensor_copy(part[0], ew[:, :]))
            link(V.tensor_tensor(rest, ew[:, :], part[0], ALU.subtract))
            link(V.tensor_copy(part[1], rest))
            link(V.tensor_tensor(rest, rest, part[1], ALU.subtract))
            link(V.tensor_copy(part[2], rest))

            rows, low = v[0:HT, 0:2, :], u[0:HT, 2:4, :]
            link(V.tensor_copy(rows, dst_rows[:, :, :]))
            link(V.tensor_scalar(low, rows, 0.0, 1e6, ALU.is_lt, ALU.mult))
            link(V.tensor_tensor(low, low, rows, ALU.add))
            V.tensor_reduce(t_max[:, :], rows, AX.X, ALU.max)
            link(V.tensor_reduce(t_min[:, :], low, AX.X, ALU.min))
            high, both = o[0:HT, 0, 0:NHALF], o2[0:HT, 0, 0:NHALF]
            for q in range(2):
                V.tensor_scalar(col[q][0:HT, :], rowf[0:HT, :], -1.0, float(2 * P - q * HT), ALU.mult, ALU.add)
                V.tensor_scalar(col[2 + q][0:HT, :], rowf[0:HT, :], float(1 + q * HT), None, ALU.add)
                V.tensor_scalar(high, basef[0:HT, :], t_max[:, q:q + 1], None, ALU.is_le)
                link(V.tensor_scalar(both, basef[0:HT, :], float(HALF - 1), t_min[:, q:q + 1], ALU.add, ALU.is_ge))
                link(V.tensor_tensor(both, both, high, ALU.mult))
                V.tensor_scalar(touch[:, q, :], both, col[q][0:HT, 0:1], None, ALU.mult)
                link(V.tensor_scalar(touch[:, 2 + q, :], both, col[2 + q][0:HT, 0:1], None, ALU.mult))
            V.drain().then_inc(prep_to_pe, 1)
            g = slice(0, NHALF)
            near, far, some, first, last1 = (c[g, :] for c in col[0:5])
            dve.wait_ge(pe_prep, 1)
            V.tensor_reduce(near, p_tr[g, 0:2 * NHALF], AX.X, ALU.max)
            link(V.tensor_reduce(far, p_tr[g, 2 * NHALF:4 * NHALF], AX.X, ALU.max))
            V.tensor_scalar(some, near, 0.0, None, ALU.is_gt)
            link(V.tensor_scalar(first, near, -1.0, float(2 * P), ALU.mult, ALU.add))
            link(V.tensor_tensor(first, first, some, ALU.mult))
            link(V.tensor_scalar(first, first, float(TILES - EVERY), None, ALU.min))
            link(V.tensor_scalar(last1, first, float(EVERY), None, ALU.add))
            link(V.tensor_tensor(last1, last1, far, ALU.max))
            link(V.scalar_tensor_tensor(out=n_items[g, :], in0=last1, scalar=float(-EVERY), in1=first,
                                        op0=ALU.add, op1=ALU.subtract))
            link(V.tensor_scalar(diag[g, g], ident[g, g], last1, None, ALU.mult))
            V.drain().then_inc(prep_to_pe, 1)
            needed, seen = col[5][g, :], o[g, 0, g]
            dve.wait_ge(pe_prep, 2)
            V.memset(list_f[:, :], 0.0)
            link(V.tensor_scalar(seen, colf[g, g], rowf[g, 0:1], None, ALU.is_le))
            link(V.tensor_tensor(seen, seen, p_wide[g, 0, g], ALU.mult))
            link(V.tensor_reduce(needed, seen, AX.X, ALU.max))
            link(V.tensor_scalar(o[g, 1, 0:BATCHES], colf[g, 0:BATCHES], float(BATCH), needed, ALU.mult, ALU.is_lt))
            link(V.tensor_reduce(n_batches[g, :], o[g, 1, 0:BATCHES], AX.X, ALU.add))
            link(V.tensor_scalar(some, rowf[g, :], 0.5, 0.5, ALU.mult, ALU.add))
            link(V.tensor_scalar(some, some, float(BATCHES), None, ALU.min))
            link(V.tensor_tensor(n_batches[g, :], n_batches[g, :], some, ALU.max))
            link(V.tensor_scalar(far, rowf[g, :], float(NHALF - 1), float(BATCHES), ALU.is_equal, ALU.mult))
            link(V.tensor_tensor(n_batches[g, :], n_batches[g, :], far, ALU.max))
            V.drain().then_inc(prep_to_pe, 1)
            V.tensor_copy(list_f[:, 0:1], first)
            link(V.tensor_copy(list_f[:, 1:2], p_edge[g, 0:1]))
            link(V.tensor_tensor(list_f[:, 2:3], list_f[:, 1:2], n_items[g, :], ALU.add))
            link(V.tensor_copy(list_f[:, 3:4], n_batches[g, :]))
            dve.wait_ge(pe_prep, 3)
            link(V.tensor_copy(list_f[:, 4:5], p_wide[g, 1, 0:1]))
            V.tensor_copy(list_rows[:, :], list_f[:, :]).then_inc(rows_ready, 1)
            dve.wait_ge(lists_in, 16)

            for r, rd in enumerate(rounds):
                s = R[r]
                sage, gin, gcn, rgcn = (rd.kind == k for k in (SAGE, GIN, GCN, RGCN))
                dve.wait_ge(s.weights_in, 16 * len(round_weights(rd)) + s.before["weights_in"])
                if r == 1:
                    link(V.tensor_scalar(deg[:, :], deg[:, :], 2.0, None, ALU.add))
                    V.tensor_scalar(dinv[:, :], deg[:, :], 1e-30, None, ALU.max).then_inc(deg_ready, 1)
                    dve.wait_ge(deg_root, 1)
                    link(V.reciprocal(dinv[:, :], dinv[:, :]))
                    link(V.tensor_scalar(deg[:, :], deg[:, :], 0.0, None, ALU.is_gt))
                    link(V.tensor_tensor(dinv[:, :], dinv[:, :], deg[:, :], ALU.mult))
                if gin:
                    V.tensor_scalar(one_eps[:, :], one_eps[:, :], 1.0, None, ALU.add).then_inc(const_dve, 1)
                if gcn and rd.layer == 1:
                    V.tensor_scalar(t_rep[:, :], ones[:, :], t_col[:, 0:1], None, ALU.mult).then_inc(const_pe, 1)
                    dve.wait_ge(const_used, 1)
                    link(V.tensor_tensor(bt[:, :], bt[:, :], p_wide[:, 0, 0:D], ALU.add))
                    link(V.tensor_scalar(bt[:, :], bt[:, :], 0.0, None, ALU.max))
                    link(V.tensor_tensor(bt[:, :], bt[:, :], shift[:, :], ALU.add))

                def parts_lo(e, source, slot, weight):
                    if weight is None:
                        return V.tensor_tensor(msg[:, bass.ds(e * BATCH, BATCH), D:2 * D],
                                               source[:, bass.ds(slot * BATCH, BATCH), :],
                                               msg[:, bass.ds(e * BATCH, BATCH), 0:D], ALU.subtract)
                    for j in range(BATCH):
                        t = e * BATCH + j
                        last = V.scalar_tensor_tensor(
                            out=tile_ap(msg, t, D, 2 * D), in0=tile_ap(source, slot * BATCH + j),
                            scalar=weight[:, bass.ds(t, 1)], in1=tile_ap(msg, t, 0, D),
                            op0=ALU.mult, op1=ALU.subtract)
                    return last

                if rgcn:
                    dve.sem_inc(s.split_done, 1)
                    dve.sem_inc(s.tile_summed, 2)

                def batch(e):
                    if gin:
                        dve.wait_ge(s.lo_done, e + s.before["lo_done"])
                        for q, (j0, j1) in enumerate(((0, 4), (4, BATCH))):
                            dve.wait_ge(emb_done, 2 * e + (q + 1))
                            V.tensor_tensor(
                                edge_v[:, j0:j1, :], raw[:, bass.ds((e % RING) * BATCH + j0, j1 - j0), :],
                                p_edge[:, 0:(j1 - j0) * D].rearrange("p (j d) -> p j d", d=D),
                                ALU.add).then_inc(emb_used, 1)
                        dve.wait_ge(s.hi_done, e + 1 + s.before["hi_done"])
                        parts_lo(e, edge_v, 0, ew1).then_inc(s.lo_done, 1)
                    elif sage or gcn:
                        dve.wait_ge(s.hi_done, e + 1 + s.before["hi_done"])
                        parts_lo(e, raw, e % RING, ew if gcn else None).then_inc(s.lo_done, 1)
                    else:
                        dve.wait_ge(s.hi_done, 2 * e + 1 + s.before["hi_done"])
                        parts_lo(e, raw, e % RING, None).then_inc(s.lo_done, 1)
                        dve.wait_ge(s.split_done, e + 1 + s.before["split_done"])
                        def choose(j):
                            dve.wait_ge(s.tile_summed, e * BATCH + max(j + 1, 2) + s.before["tile_summed"])
                            wait_apart(dve, s.rel_done, e * (2 * BATCH) + (2 * j + 1) + s.before["rel_done"])
                            own = mask[:, bass.ds(e * BATCH + j, 1), 0:4].rearrange("p o k -> p (o k)")
                            V.tensor_tensor(chosen[:, j % 2, 0:4, :],
                                            p_wide[:, 0, :].rearrange("p (k d) -> p k d", d=D),
                                            own.unsqueeze(2).to_broadcast([P, 4, D]), ALU.mult
                                            ).then_inc(s.low_chosen, 1)

                        choose(0)
                        for j in range(BATCH):
                            if j + 1 < BATCH:
                                choose(j + 1)
                            dve.wait_ge(s.low_chosen, e * BATCH + (j + 2) + s.before["low_chosen"])
                            dve.wait_ge(s.high_chosen, e * BATCH + (j + 2) + s.before["high_chosen"])
                            V.tensor_reduce(edge_v[:, j, :], chosen[:, j % 2, :, :].rearrange("p k d -> p d k"),
                                            AX.X, ALU.add).then_inc(s.tile_summed, 1)
                        dve.wait_ge(s.hi_done, 2 * e + 2 + s.before["hi_done"])
                        parts_lo(e, edge_v, 0, None).then_inc(s.split_done, 1)

                def onehots(it, a):
                    t0, i0, i1 = item_range(dve, PT, it, a)

                    def compare(slot, t):
                        return V.tensor_scalar(tile_ap(onehot, slot), iota[:, :], dst_f[:, bass.ds(t, 1)],
                                               negbase[:, bass.ds(it * 2 + a, 1)], ALU.subtract, ALU.is_equal)

                    if not is_zero(it):
                        dve.wait_ge(s.every_used, it * 2 + (a - 1) + s.before["every_used"])
                    for k in range(EVERY):
                        last = compare(EVERY * a + k, (t0 + k).with_bounds(min_val=0, max_val=TILES - 1))
                    last.then_inc(s.every_ready, 1)
                    with dve.If(i0 < i1):
                        with dve.Fori(i0, i1) as i:
                            dve.wait_ge(s.oh_used, i + 1)
                            compare(ring_place(i), tile_of(t0, i0, i)).then_inc(s.oh_ready, 1)

                def sums(it, a):
                    dve.wait_ge(s.tr_done, it * 2 + (a + 1) + s.before["tr_done"])
                    if gin or gcn:
                        dve.wait_ge(s.ht_done, it * 2 + (a + 1) + s.before["ht_done"])
                        V.tensor_tensor(agg_t[:, a, :], p_agg[:, a, :], h_t[:, a, :], ALU.add).then_inc(s.agg_done, 1)
                    else:
                        V.tensor_copy(agg_t[:, a, :], p_agg[:, a, :]).then_inc(s.agg_done, 1)

                def degrees(it, a):
                    dve.wait_ge(s.tr_done, it * 2 + (a + 1) + s.before["tr_done"])
                    if not (is_zero(it) and a == 0):
                        dve.wait_ge(deg_used, it * 2 + a)
                    sums_ = p_edge[:, 0:16].rearrange("p (b c) -> p b c", c=4)
                    V.tensor_reduce(deg[:, bass.ds(it * BLOCKS + 4 * a, 4)], sums_[:, :, 0:3], AX.X, ALU.add)
                    V.tensor_scalar(count[:, :], sums_[:, :, 3:4].rearrange("p b c -> p (b c)"),
                                    1.0, None, ALU.max).then_inc(count_done, 1)

                def one_over_count(it, a):
                    dve.wait_ge(count_done, it * 2 + (a + 1))
                    V.reciprocal(inv[:, bass.ds(it * BLOCKS + 4 * a, 4)], count[:, :]).then_inc(deg_used, 1)

                def chain(ins, semaphore, name, count):
                    ins.then_inc(semaphore, 1)
                    dve.wait_ge(semaphore, count + s.before[name])

                def wide(row):
                    return row[:, :].unsqueeze(1).to_broadcast([P, BLOCKS, D])

                def take(it, a):
                    if not exists(it):
                        return
                    if a == 0 and not is_zero(it):
                        if not rd.relu:
                            dve.wait_ge(s.res_used, it + s.before["res_used"])
                        elif rd.norm:
                            dve.wait_ge(s.relu_done, it + s.before["relu_done"])
                        else:
                            dve.wait_ge(s.out_done, it + s.before["out_done"])
                    if r == 0:
                        dve.wait_ge(deg_used, it * 2 + (a + 1))
                    dve.wait_ge(s.dense_done, it * 2 + (a + 1) + s.before["dense_done"])
                    half_u = u[:, 4 * a:4 * a + 4, :]
                    product = p_dense[:, a, :].rearrange("p (b d) -> p b d", d=D)
                    if sage or gcn:
                        scale, source = (inv, p_wide) if sage else (dinv, p_dense)
                        for b in range(4):
                            last = V.scalar_tensor_tensor(
                                out=u[:, 4 * a + b, :], in0=source[:, a, b * D:(b + 1) * D],
                                scalar=scale[:, bass.ds(it * BLOCKS + (4 * a + b), 1)], in1=bias[:, :],
                                op0=ALU.mult, op1=ALU.add)
                        if sage:
                            chain(last, s.scaled_done, "scaled_done", it * 2 + (a + 1))
                            last = V.tensor_tensor(half_u, half_u, product, ALU.add)
                    else:
                        last = V.tensor_tensor(half_u, product, bias[:, :].unsqueeze(1).to_broadcast([P, 4, D]), ALU.add)
                    last.then_inc(s.u_done, 1)

                def mean_variance(it, source, n):
                    if not is_zero(it):
                        dve.wait_ge(s.stats_done[n], it + s.before[f"stats_done{n}"])
                    for b in range(BLOCKS):
                        last = V.bn_stats(stats[n][:, b, :], source[:, b, :])
                    chain(last, s.bn_done[n], f"bn_done{n}", it + 1)
                    dve.sem_inc(passed, 1)
                    for b in range(BLOCKS):
                        last = V.bn_aggr(mv[n][:, b, :], stats[n][:, b, :])
                    last.then_inc(s.var_done[n], 1)

                def scale_and_move(it, n):
                    if not exists(it) or n >= norms_of(rd):
                        return
                    scaled = scaled_by_dinv(rd)
                    step, name, per = s.rstd_step[n], f"rstd_step{n}", 1 + scaled
                    mean = mv[n][:, :, 0:1].rearrange("p b o -> p (b o)")
                    dve.wait_ge(s.std_done[n], it + 1 + s.before[f"std_done{n}"])
                    chain(V.reciprocal(rstd[n][:, :], std[n][:, :]), step, name, it * per + 1)
                    last = V.scalar_tensor_tensor(out=nmr[n][:, :], in0=mean, scalar=-1.0, in1=rstd[n][:, :],
                                                  op0=ALU.mult, op1=ALU.mult)
                    if scaled:
                        chain(last, step, name, it * per + 2)
                        at = bass.ds(it * BLOCKS, BLOCKS)
                        V.tensor_tensor(rstd_d[:, :], rstd[n][:, :], dinv[:, at], ALU.mult)
                        last = V.tensor_tensor(nmr_d[:, :], nmr[n][:, :], dinv[:, at], ALU.mult)
                    last.then_inc(s.stats_done[n], 1)

                def add_residual(it, dst, source):
                    dve.wait_ge(s.res_loaded, it * 16 + 16 + s.before["res_loaded"])
                    V.tensor_tensor(dst[:, :, :], source[:, :, :], res_in[:, :, :], ALU.add).then_inc(s.res_used, 1)
                    dve.wait_ge(s.res_used, it + 1 + s.before["res_used"])

                def residual_and_stats(it):
                    if not exists(it) or not rd.norm:
                        return
                    if not is_zero(it):
                        dve.wait_ge(s.out_done, it + s.before["out_done"])
                    dve.wait_ge(s.u_done, it * 2 + 2 + s.before["u_done"])
                    add_residual(it, v, u)
                    mean_variance(it, v, 0)

                def relu_stats(it):
                    if not exists(it):
                        return
                    dve.wait_ge(s.relu_done, it + 1 + s.before["relu_done"])
                    mean_variance(it, v, 0)

                def gain_and_shift(it):
                    if not exists(it):
                        return
                    per = rd.layer
                    dve.wait_ge(s.norm_done, it + 1 + s.before["norm_done"])
                    chain(V.tensor_tensor(o2[:, :, :], o2[:, :, :], wide(gain), ALU.mult),
                          s.gain_step, "gain_step", it * per + 1)
                    if rd.layer == 1:
                        if not is_zero(it):
                            dve.wait_ge(s.stored, it * 16 + s.before["stored"])
                        for b in range(BLOCKS):
                            last = V.scalar_tensor_tensor(
                                out=o[:, b, :], in0=bt[:, :], scalar=dinv[:, bass.ds(it * BLOCKS + b, 1)],
                                in1=o2[:, b, :], op0=ALU.mult, op1=ALU.add)
                        last.then_inc(s.out_done, 1)
                        return
                    chain(V.tensor_tensor(o2[:, :, :], o2[:, :, :], wide(shift), ALU.add),
                          s.gain_step, "gain_step", it * per + 2)
                    add_residual(it, o2, o2)
                    mean_variance(it, o2, 1)

                def stage(it, a):
                    if r == 0 and exists(it):
                        degrees(it, a)
                    nxt, na = back(it, a, -1)
                    if exists(nxt):
                        onehots(nxt, na)
                    if exists(it):
                        sums(it, a)
                        if r == 0:
                            one_over_count(it, a)
                    pair, ta = back(it, a, lag_of(rd))
                    take(pair, ta)
                    if gcn:
                        if ta == 1:
                            scale_and_move(pair - 2, 1)
                            scale_and_move(pair - 1, 0)
                        else:
                            relu_stats(pair - 1)
                            gain_and_shift(pair - 2)
                    elif ta == 1:
                        residual_and_stats(pair)
                    else:
                        scale_and_move(pair - 1, 0)

                def batches(it):
                    if exists(it + 1):
                        e0, e1 = batch_range(dve, PT, it)
                        each_batch(dve, e0, e1, batch)

                def step(it):
                    stage(it, 0)
                    batches(it)
                    stage(it, 1)

                first_batches(dve, PT, batch)
                onehots(0, 0)
                for it in range(steps_before_loop(rd)):
                    step(it)
                with dve.Fori(steps_before_loop(rd), NPAIR - 1) as it:
                    step(it)
                for it in range(NPAIR - 1, NPAIR + steps_after(rd)):
                    step(it)


def kernel(**inputs):
    import numpy as _np
    import concourse.bacc as _bacc
    from concourse import mybir as _mybir
    from concourse.bass_utils import run_bass_kernel_spmd as _run

    edge_arrays = ("src", "dst", "edge_weight", "edge_weight1", "edge_type_8")

    def by_tile(a):
        full = _np.zeros(TILES * P, a.dtype)
        full[:E] = a.reshape(E)[::-1]
        return _np.ascontiguousarray(full.reshape(TILES, P).T)

    def by_batch(a):
        full = _np.zeros((TILES * P, DE), a.dtype)
        full[:E] = a[::-1]
        return _np.ascontiguousarray(full.reshape(BATCHES, BATCH, P, DE).transpose(0, 1, 3, 2)).reshape(
            BATCHES, BATCH * DE, P)

    nc = _bacc.Bacc("TRN2", target_bir_lowering=False, num_devices=1)
    laid = {"dst_flat": _np.ascontiguousarray(_np.asarray(inputs["dst"])[::-1])}
    for name, a in inputs.items():
        a = _np.asarray(a)
        if name in edge_arrays:
            a = by_tile(a)
        elif name == "edge_attr_16":
            a = by_batch(a)
        elif name == "L1_gnn_b1":
            a = a.reshape(2, P).T
        laid[name] = _np.ascontiguousarray(a)
    arrays, aps = {}, {}
    for name, a in laid.items():
        arrays[f"in_{name}"] = a
        aps[name] = nc.dram_tensor(f"in_{name}", a.shape, _mybir.dt.from_np(a.dtype), kind="ExternalInput").ap()
    out = nc.dram_tensor("out", (N, D), F32, kind="ExternalOutput").ap()
    build_gnn(nc, aps, out)
    return _run(nc, [arrays], core_ids=[0]).results[0]["out"]
```

```python
from contextlib import ExitStack

import concourse.bass as bass
from concourse import mybir

F32 = mybir.dt.float32
F16 = mybir.dt.float16
I32 = mybir.dt.int32
ALU = mybir.AluOpType
ACT = mybir.ActivationFunctionType
AX = mybir.AxisListType

P = 128
N, E, D = 50000, 25000, 128
TILES = -(-E // P)
LAST = E - (TILES - 1) * P
BATCH = 7
BATCHES = TILES // BATCH
RING = 4
HALF = 512
PAIR = 2 * HALF
NPAIR = -(-N // PAIR)
NHALF = 2 * NPAIR
BLOCKS = PAIR // P
TOP = N - PAIR
EVERY = 2
MORE = 2
REL = 8
DE = 16
HT = TILES // 2
TURNS = BATCHES // RING
LROW = 8
EPS = 1e-5
assert TILES % BATCH == 0 and BATCHES % RING == 0 and TILES % 2 == 0

SAGE, GIN, GCN, RGCN = "sage", "gin", "gcn", "rgcn"


class Round:

    def __init__(self, kind, layer, source, out, res=None, relu=False, norm=False):
        self.kind, self.layer, self.source, self.out = kind, layer, source, out
        self.res, self.relu, self.norm = res, relu, norm


class RoundSemaphores:

    def __init__(self, counted, before, oh_ready, oh_used):
        self.before, self.oh_ready, self.oh_used = before, oh_ready, oh_used
        self.weights_in = counted["weights_in"]
        self.h_loaded = [counted["h_loaded0"], counted["h_loaded1"]]
        self.stored = counted["stored"]
        self.stored2 = counted["stored2"]
        self.res_loaded = counted["res_loaded"]
        self.res_used = counted["res_used"]
        self.idx_ready = counted["idx_ready"]
        self.batch_in = counted["batch_in"]
        self.hi_done = counted["hi_done"]
        self.lo_done = counted["lo_done"]
        self.tr_done = counted["tr_done"]
        self.ht_done = counted["ht_done"]
        self.agg_done = counted["agg_done"]
        self.dense_done = counted["dense_done"]
        self.u_done = counted["u_done"]
        self.out_done = counted["out_done"]
        self.relu_done = counted["relu_done"]
        self.var_done = [counted["var_done0"], counted["var_done1"]]
        self.std_done = [counted["std_done0"], counted["std_done1"]]
        self.stats_done = [counted["stats_done0"], counted["stats_done1"]]
        self.bn_done = [counted["bn_done0"], counted["bn_done1"]]
        self.rstd_step = [counted["rstd_step0"], counted["rstd_step1"]]
        self.norm_done = counted["norm_done"]
        self.scaled_done = counted["scaled_done"]
        self.gain_step = counted["gain_step"]
        self.every_ready = counted["every_ready"]
        self.et_done = counted["et_done"]
        self.et_ready = counted["et_ready"]
        self.rel_done = counted["rel_done"]
        self.low_chosen = counted["low_chosen"]
        self.high_chosen = counted["high_chosen"]
        self.tile_summed = counted["tile_summed"]


ROUNDS = [
    Round(SAGE, 0, "x", "s1", relu=True),
    Round(SAGE, 1, "s1", "s2", relu=True),
    Round(SAGE, 2, "s2", "x1", res="x", norm=True),
    Round(GIN, 0, "x1", "x2", res="x1", norm=True),
    Round(GCN, 1, "s1", "s2", relu=True, norm=True),
    Round(GCN, 2, "s2", "x3", res="x2", relu=True, norm=True),
    Round(RGCN, 1, "x3", "s1", relu=True),
    Round(RGCN, 2, "s1", "out", res="x3", norm=True),
]
NROUNDS = len(ROUNDS)


def build_gnn(nc, A, out_ap, rounds=ROUNDS):
    ctx = ExitStack()
    with ctx:
        def sb(name, shape, dt=F32):
            return ctx.enter_context(nc.sbuf_tensor(name, shape, dt))

        def ps(name, shape):
            return ctx.enter_context(nc.psum_tensor(name, shape, F32))

        def sem(name):
            return ctx.enter_context(nc.semaphore(name))

        dram = {"x": A["x"], "out": out_ap}
        for name in ("s1", "s2", "x1", "x2", "x3"):
            dram[name] = nc.dram_tensor(f"node_{name}", (N, D), F32, kind="Internal").ap()
        list_dram = nc.dram_tensor("list_scratch", (NHALF, LROW), I32, kind="Internal").ap()

        raw = sb("raw", [P, RING * BATCH, D])
        msg = sb("msg", [P, TILES, 2 * D], F16)
        edge_v = sb("edge_v", [P, BATCH, D])
        attr = sb("attr", [BATCH * DE, RING, P])
        attr_now = sb("attr_now", [P, P])
        src_i = sb("src_i", [P, TILES], I32)
        idx_now = sb("idx_now", [P, RING * BATCH], I32)
        dst_f = sb("dst_f", [P, TILES])
        etype_f = sb("etype_f", [P, TILES])
        ew = sb("ew", [P, TILES])
        ew1 = sb("ew1", [P, TILES])
        mask = sb("mask", [P, TILES, REL])
        ecol = sb("ecol", [P, TILES, 4], F16)
        onehot = sb("onehot", [P, 2 * EVERY + MORE, HALF], F16)
        h_in = sb("h_in", [P, BLOCKS, D])
        h_t = sb("h_t", [P, 2, HALF])
        agg_t = sb("agg_t", [P, 2, HALF])
        res_in = sb("res_in", [P, BLOCKS, D])
        u = sb("u", [P, BLOCKS, D])
        v = sb("v", [P, BLOCKS, D])
        o = sb("o", [P, BLOCKS, D])
        o2 = sb("o2", [P, BLOCKS, D])
        edge_t = o2
        hid = sb("hid", [P, 2, 2, HALF])
        by_relation = hid.rearrange("p a q (k d) -> p a (q k) d", d=D)
        chosen = (by_relation[:, 0, :, :], by_relation[:, 1, :, :], sb("chosen", [P, REL, D]))
        total = chosen[0]
        count = sb("count", [P, 4])
        stats = [sb(f"stats{n}", [P, BLOCKS, 6]) for n in range(2)]
        mv = [sb(f"mv{n}", [P, BLOCKS, 2]) for n in range(2)]
        std = [sb(f"std{n}", [P, BLOCKS]) for n in range(2)]
        eps_col = sb("eps_col", [P, 1])
        rstd = [sb(f"rstd{n}", [P, BLOCKS]) for n in range(2)]
        nmr = [sb(f"nmr{n}", [P, BLOCKS]) for n in range(2)]
        rstd_d = sb("rstd_d", [P, BLOCKS])
        nmr_d = sb("nmr_d", [P, BLOCKS])
        deg = sb("deg", [P, NHALF * 4])
        inv = sb("inv", [P, NHALF * 4])
        dinv = sb("dinv", [P, NHALF * 4])
        w = sb("w", [P, REL + 1, D])
        bond = sb("bond", [P, BATCH, D])
        bias = sb("bias", [P, D])
        gain = sb("gain", [P, D])
        shift = sb("shift", [P, D])
        b1_col = sb("b1_col", [P, 2])
        one_eps = sb("one_eps", [P, 1])
        t_col = sb("t_col", [P, 1])
        t_rep = sb("t_rep", [P, P])
        bt = sb("bt", [P, D])
        col_i = sb("col_i", [P, HALF], I32)
        row_i = sb("row_i", [P, 1], I32)
        base_i = sb("base_i", [P, NHALF], I32)
        colf = sb("colf", [P, P])
        rowf = sb("rowf", [P, 1])
        iota = sb("iota", [P, HALF], F16)
        basef = sb("basef", [P, NHALF])
        negbase = sb("negbase", [P, NHALF])
        ident = sb("ident", [P, P])
        ones = sb("ones", [P, P])
        lists = sb("lists", [1, NHALF * LROW], I32)

        dst_i = sb("dst_i", [P, TILES], I32)
        etype_i = sb("etype_i", [P, TILES], I32)
        dst_rows = sb("dst_rows", [HT, 2, P], I32)
        before, diag, ahead = (edge_v[:, k, :] for k in range(3))
        touch = edge_v[0:HT, 3:7, 0:NHALF]
        list_f = sb("list_f", [NHALF, LROW])
        list_rows = sb("list_rows", [NHALF, LROW], I32)
        t_max, t_min = sb("t_max", [HT, 2]), sb("t_min", [HT, 2])
        col = [sb(f"setup_col{k}", [P, 1]) for k in range(8)]
        n_items, n_batches = sb("n_items", [P, 1]), sb("n_batches", [P, 1])
        edge_arrays = [("src", src_i), ("edge_weight", ew), ("edge_weight1", ew1), ("dst", dst_i),
                       ("edge_type_8", etype_i)]
        edge_loads = len(edge_arrays) + 3

        p_agg = ps("p_agg", [P, 2, HALF])
        p_dense = ps("p_dense", [P, 2, HALF])
        p_wide = ps("p_wide", [P, 2, HALF])
        p_tr = ps("p_tr", [P, HALF])
        p_edge = ps("p_edge", [P, HALF])

        low_bank = (p_wide[:, 0, :], p_edge[:, :])
        high_bank = (p_wide[:, 1, :], p_tr[:, :])
        QUARTERS = ((0, 4), (4, BATCH))

        pads_set = sem("pads_set")
        edges_in = sem("edges_in")
        iotas = sem("iotas")
        dve_prep = sem("dve_prep")
        prep_to_pe = sem("prep_to_pe")
        pe_prep = sem("pe_prep")
        rows_ready = sem("rows_ready")
        rows_stored = sem("rows_stored")
        lists_in = sem("lists_in")
        passed = sem("passed")

        def adds(rd):
            first, second = NPAIR * (norms_of(rd) > 0), NPAIR * (norms_of(rd) > 1)
            rgcn = rd.kind == RGCN
            return dict(
                weights_in=16 * len(round_weights(rd)), h_loaded0=16 * NPAIR, h_loaded1=16 * NPAIR,
                stored=16 * NPAIR, stored2=16 * NPAIR if rd.kind == GIN else 0,
                res_loaded=16 * NPAIR if rd.res else 0, res_used=NPAIR if rd.res else 0,
                idx_ready=BATCHES, batch_in=BATCHES, hi_done=(1 + rgcn) * BATCHES, lo_done=BATCHES + edge_v_used(rd),
                tr_done=NHALF, ht_done=NHALF, agg_done=NHALF, dense_done=NHALF, u_done=NHALF,
                every_ready=NHALF, out_done=NPAIR,
                relu_done=NPAIR if rd.relu and rd.norm else 0, norm_done=NPAIR if rd.kind in (GIN, GCN) else 0,
                var_done0=first, var_done1=second, std_done0=first, std_done1=second,
                stats_done0=first, stats_done1=second, bn_done0=first, bn_done1=second,
                rstd_step0=first * (1 + scaled_by_dinv(rd)), rstd_step1=second,
                scaled_done=NHALF if rd.kind == SAGE else 0,
                gain_step=NPAIR * rd.layer if rd.kind == GCN else 0,
                et_done=2 * BATCHES * rgcn, et_ready=2 * BATCHES * rgcn,
                rel_done=2 * TILES * rgcn, low_chosen=(TILES + 1) * rgcn, high_chosen=(TILES + 1) * rgcn,
                tile_summed=(TILES + 2) * rgcn)

        gathered = [sem(f"gathered{q}") for q in range(RING)]
        attr_ready, emb_done, emb_used, gelu_done = sem("attr_ready"), sem("emb_done"), sem("emb_used"), sem("gelu_done")
        hid_done, hid_ready = sem("hid_done"), sem("hid_ready")
        weighed = sem("weighed")
        weighed_before = [BATCHES * sum(rd.kind in (GIN, GCN) for rd in rounds[:r]) for r in range(len(rounds))]
        deg_used = sem("deg_used")
        count_done, deg_ready, deg_root = sem("count_done"), sem("deg_ready"), sem("deg_root")
        const_pe, const_used, const_dve = sem("const_pe"), sem("const_used"), sem("const_dve")
        per_batch = [BATCH + (rd.kind == GIN) for rd in rounds]
        landed_before = [TURNS * sum(per_batch[:r]) for r in range(len(rounds))]

        def round_weights(rd):
            def rep(name):
                return A[name].partition_broadcast(P)

            if rd.kind == SAGE:
                k = rd.layer
                return [(w[:, 0, :], A[f"L0_gnn_Wl{k}"]), (w[:, 1, :], A[f"L0_gnn_Wr{k}"]),
                        (bias[:, :], rep(f"L0_gnn_bl{k}"))]
            if rd.kind == GIN:
                out = [(w[:, q, :], A["L1_gnn_W1"][:, q * D:(q + 1) * D]) for q in range(2)]
                out += [(w[:, 2 + q, :], A["L1_gnn_W2"][q * P:(q + 1) * P, :]) for q in range(2)]
                out += [(bias[:, :], rep("L1_gnn_b2")), (b1_col[:, :], A["L1_gnn_b1"]),
                        (one_eps[:, :], rep("L1_gnn_eps"))]
                for j in range(BATCH):
                    out.append((bond[j * DE:(j + 1) * DE, j, :], A["L1_gnn_bond_W"]))
                    out.append((bond[BATCH * DE:BATCH * DE + 1, j, :], A["L1_gnn_bond_b"].partition_broadcast(1)))
                return out
            if rd.kind == GCN:
                k = rd.layer
                out = [(w[:, 0, :], A[f"L2_gnn_W{k}"]), (bias[:, :], rep(f"L2_gnn_b{k}")),
                       (gain[:, :], rep(f"L2_gnn_g{k}")), (shift[:, :], rep(f"L2_gnn_be{k}"))]
                if k == 1:
                    out += [(w[:, 1, :], A["L2_gnn_Wt"]), (t_col[:, :], A["L2_gnn_t"].rearrange("(p o) -> p o", o=1)),
                            (bt[:, :], rep("L2_gnn_bt"))]
                return out
            k = rd.layer
            return [(w[:, 0:REL, :], A[f"L3_gnn_W{k}"].rearrange("r i o -> i r o")),
                    (w[:, REL, :], A[f"L3_gnn_loop_w{k}"]), (bias[:, :], rep(f"L3_gnn_b{k}"))]

        def norms_of(rd):
            return (2 if rd.kind == GCN and rd.layer == 2 else 1) if rd.norm else 0

        def scaled_by_dinv(rd):
            return rd.kind == GCN and rd.layer == 1

        def edge_v_used(rd):
            return int(rd.kind != SAGE)

        def lag_of(rd):
            return 2 if rd.kind == GIN else 1

        def steps_before_loop(rd):
            return 4 if rd.kind == GCN else 3 if rd.kind == GIN else 2

        def steps_after(rd):
            return 3 if rd.kind == GCN else 2

        counted = {name: sem(name) for name in adds(rounds[0])}
        R = []
        for r, rd in enumerate(rounds):
            earlier = {name: sum(adds(x)[name] for x in rounds[:r]) for name in counted}
            R.append(RoundSemaphores(counted, earlier, sem(f"oh_ready{r}"), sem(f"oh_used{r}")))

        def is_zero(it):
            return isinstance(it, int) and it == 0

        def exists(it):
            return not isinstance(it, int) or 0 <= it < NPAIR

        def back(it, a, halves):
            return it - (halves - a + 1) // 2, (a - halves) % 2

        def load_list(eng, kind, at, count):
            return nc.values_load_multi_w_load_instructions(
                lists[0:1, bass.ds(at, count)], engines=[kind], min_val=0)[1]

        def batch_range(e0, e1):
            return e0.with_bounds(min_val=0, max_val=BATCHES), e1.with_bounds(min_val=0, max_val=BATCHES)

        def items_of(t0, i0, i1):
            return t0.with_bounds(min_val=0, max_val=TILES - EVERY), i0, i1

        def first_batches(eng, kind, body):
            (end,) = load_list(eng, kind, LROW + 4, 1)
            with eng.Fori(0, end.with_bounds(min_val=1, max_val=BATCHES)) as e:
                body(e.with_bounds(min_val=0, max_val=BATCHES - 1))

        def single_items(eng, kind, it, a):
            i0, t0, i1 = load_list(eng, kind, (it * 2 + a) * LROW, 3)
            return items_of(t0, i0, i1)

        def step_list(eng, kind, it):
            if not exists(it + 1):
                return None, (single_items(eng, kind, it, 1) if exists(it) else None), None
            e0, e1, i0, t0, i1, next_t0, i2 = load_list(eng, kind, it * (2 * LROW) + LROW + 4, 7)
            return batch_range(e0, e1), items_of(t0, i0, i1), items_of(next_t0, i1, i2)

        def tile_of(t0, i0, i):
            return (t0 + (i - i0) + EVERY).with_bounds(min_val=0, max_val=TILES - 1)

        def ring_place(i):
            return ((i % MORE) + 2 * EVERY).with_bounds(min_val=2 * EVERY, max_val=2 * EVERY + MORE - 1)

        def each_batch(eng, e0, e1, body):
            with eng.If(e0 < e1):
                with eng.Fori(e0, e1) as e:
                    body(e.with_bounds(min_val=0, max_val=BATCHES - 1))

        def wait_apart(eng, semaphore, value):
            eng.wait_ge(semaphore, value)
            eng.sem_inc(passed, 1)

        def flat(ap):
            return ap.rearrange("p a d -> p (a d)")

        def tile_ap(buf, t, lo=None, hi=None):
            s = buf[:, bass.ds(t, 1), :] if lo is None else buf[:, bass.ds(t, 1), lo:hi]
            return flat(s)

        block = ctx.enter_context(nc.Block())

        @block.sync
        def _(sp):
            sp.wait_ge(pads_set, 1)
            for name, buf in edge_arrays:
                sp.dma_start(buf[:, :], A[name]).then_inc(edges_in, 16)
            flat_dst = A["dst_flat"]
            sp.dma_start(dst_rows[:, 0, :], flat_dst[0:HT * P].rearrange("(p e) -> p e", e=P)).then_inc(edges_in, 16)
            sp.dma_start(dst_rows[0:HT - 1, 1, :],
                         flat_dst[HT * P:(TILES - 1) * P].rearrange("(p e) -> p e", e=P)).then_inc(edges_in, 16)
            sp.dma_start(dst_rows[HT - 1:HT, 1, 0:LAST],
                         flat_dst[(TILES - 1) * P:E].rearrange("(p e) -> p e", p=1)).then_inc(edges_in, 16)
            sp.wait_ge(rows_ready, 1)
            sp.dma_start(list_dram, list_rows[0:NHALF, :]).then_inc(rows_stored, 16)
            sp.wait_ge(rows_stored, 16)
            sp.dma_start(lists[0:1, :], list_dram.rearrange("(o g) c -> o (g c)", o=1)).then_inc(lists_in, 16)

            for r, rd in enumerate(rounds):
                s = R[r]
                if r:
                    sp.wait_ge(R[r - 1].stored, 16 * NPAIR + R[r - 1].before["stored"])
                    if rounds[r - 1].kind == GIN:
                        sp.wait_ge(R[r - 1].stored2, 16 * NPAIR + R[r - 1].before["stored2"])
                for dst_ap, src_ap in round_weights(rd):
                    sp.dma_start(dst_ap, src_ap).then_inc(s.weights_in, 16)
                src_d, out_d = dram[rd.source], dram[rd.out]

                def rows_of(d, base):
                    return d[bass.ds(base, PAIR), :].rearrange("(b p) d -> p b d", p=P)

                def half_of(it, a):
                    return (0 if isinstance(it, int) and it == NPAIR - 1 else it * (-PAIR) + TOP) + a * HALF

                def load(it, a):
                    if not is_zero(it):
                        sp.wait_ge(s.tr_done, it * 2 + (a - 1) + s.before["tr_done"])
                    sp.dma_start(h_in[:, 4 * a:4 * a + 4, :],
                                 src_d[bass.ds(half_of(it, a), HALF), :].rearrange("(b p) d -> p b d", p=P)
                                 ).then_inc(s.h_loaded[a], 16)

                def load_residual(it):
                    if not exists(it) or not rd.res:
                        return
                    if not is_zero(it):
                        sp.wait_ge(s.res_used, it + s.before["res_used"])
                    sp.dma_start(res_in[:, :, :], rows_of(dram[rd.res], half_of(it, 0))).then_inc(s.res_loaded, 16)

                def store(it):
                    if not exists(it):
                        return
                    if isinstance(it, int) and it == NPAIR - 1:
                        sp.wait_ge(s.stored, 16 * it + s.before["stored"])
                        if rd.kind == GIN:
                            sp.wait_ge(s.stored2, 16 * it + s.before["stored2"])
                    sp.wait_ge(s.out_done, it + 1 + s.before["out_done"])
                    sp.dma_start(rows_of(out_d, half_of(it, 0)), o[:, :, :]).then_inc(s.stored, 16)
                    if rd.kind == GIN:
                        sp.wait_ge(s.norm_done, it + 1 + s.before["norm_done"])
                        sp.dma_start(rows_of(dram["s1"], half_of(it, 0)), o2[:, :, :]).then_inc(s.stored2, 16)

                def step(it):
                    if exists(it + 1):
                        load(it + 1, 0)
                    if not rd.norm:
                        store(it - 1)
                    if exists(it + 1):
                        load(it + 1, 1)
                    load_residual(it - 1 if rd.kind == GCN else it)
                    if rd.kind == GCN:
                        store(it - 1 - rd.layer)
                    elif rd.norm:
                        store(it - lag_of(rd))

                load(0, 0)
                load(0, 1)
                for it in range(steps_before_loop(rd)):
                    step(it)
                with sp.Fori(steps_before_loop(rd), NPAIR - 2) as it:
                    step(it)
                for it in range(NPAIR - 2, NPAIR + steps_after(rd)):
                    step(it)
            sp.wait_ge(R[-1].stored, 16 * NPAIR + R[-1].before["stored"])

        @block.gpsimd
        def _(pool):
            nc.gpsimd.iota(col_i[:, :], pattern=[[1, HALF]], base=0, channel_multiplier=0).then_inc(iotas, 1)
            nc.gpsimd.iota(row_i[:, :], pattern=[[0, 1]], base=0, channel_multiplier=1).then_inc(iotas, 1)
            nc.gpsimd.iota(base_i[:, :], pattern=[[-PAIR, NPAIR], [HALF, 2]], base=TOP,
                           channel_multiplier=0).then_inc(iotas, 1)
            pool.wait_ge(edges_in, 16 * edge_loads)
            for r, rd in enumerate(rounds):
                s = R[r]
                if r:
                    pool.wait_ge(R[r - 1].stored, 16 * NPAIR + R[r - 1].before["stored"])
                    if rounds[r - 1].kind == GIN:
                        pool.wait_ge(R[r - 1].stored2, 16 * NPAIR + R[r - 1].before["stored2"])
                src_d = dram[rd.source]

                def pass_on(q, turns):
                    wait_apart(pool, gathered[q], turns * (16 * per_batch[r]) + 16 * landed_before[r])
                    pool.sem_inc(s.batch_in, 1)

                def turn(k, first):
                    for q in range(RING):
                        if not first:
                            pool.wait_ge(s.lo_done, RING * k + (q - RING + 1) + edge_v_used(rd) + s.before["lo_done"])
                        nc.gpsimd.tensor_copy(
                            idx_now[:, q * BATCH:(q + 1) * BATCH],
                            src_i[:, bass.ds((k * RING + q) * BATCH, BATCH)]).then_inc(s.idx_ready, 1)
                        wait_apart(pool, s.idx_ready, RING * k + (q + 1) + s.before["idx_ready"])
                        for j in range(q * BATCH, (q + 1) * BATCH):
                            nc.gpsimd.indirect_dma_start(
                                out=raw[:, j, :], out_offset=None, in_=src_d,
                                in_offset=bass.IndirectOffsetOnAxis(ap=idx_now[:, j:j + 1], axis=0),
                            ).then_inc(gathered[q], 16)
                        if rd.kind == GIN:
                            pool.dma_start(attr[:, q, :], A["edge_attr_16"][bass.ds(k * RING + q, 1), :, :].rearrange(
                                "o f e -> f (o e)")).then_inc(gathered[q], 16)
                        if q:
                            pass_on(q - 1, k + 1)
                        elif not first:
                            pass_on(RING - 1, k)

                turn(0, True)
                with pool.Fori(1, TURNS) as k:
                    turn(k, False)
                pass_on(RING - 1, TURNS)

        @block.scalar
        def _(act):
            PT = mybir.EngineType.Activation
            act.wait_ge(lists_in, 16)
            for r, rd in enumerate(rounds):
                s = R[r]
                act.wait_ge(s.weights_in, 16 * len(round_weights(rd)) + s.before["weights_in"])
                if r == 1:
                    act.wait_ge(deg_ready, 1)
                    nc.scalar.activation(dinv[:, :], dinv[:, :], ACT.Sqrt).then_inc(deg_root, 1)
                if rd.kind == GIN:
                    act.wait_ge(const_dve, 1)

                def hi(e, source, slot=0):
                    nc.scalar.activation(msg[:, bass.ds(e * BATCH, BATCH), 0:D],
                                         source[:, bass.ds(slot * BATCH, BATCH), :], ACT.Copy).then_inc(s.hi_done, 1)

                def weigh(e, source, slot, weight):
                    for j in range(BATCH):
                        last = nc.scalar.activation(
                            edge_v[:, j, :], tile_ap(source, slot * BATCH + j), ACT.Copy,
                            scale=weight[:, bass.ds(e * BATCH + j, 1)])
                    last.then_inc(weighed, 1)

                def batch(e):
                    wait_apart(act, s.batch_in, e + 1 + s.before["batch_in"])
                    if rd.kind == SAGE:
                        hi(e, raw, e % RING)
                    elif rd.kind == GCN:
                        wait_apart(act, s.lo_done, e + 1 + s.before["lo_done"])
                        weigh(e, raw, e % RING, ew)
                        wait_apart(act, weighed, e + 1 + weighed_before[r])
                        hi(e, edge_v)
                    elif rd.kind == GIN:
                        act.wait_ge(emb_used, 2 * e + 3)
                        nc.scalar.activation(flat(edge_v[:, :, :]), flat(edge_v[:, :, :]), ACT.Gelu
                                             ).then_inc(gelu_done, 1)
                        wait_apart(act, gelu_done, e + 1)
                        weigh(e, edge_v, 0, ew1)
                        wait_apart(act, weighed, e + 1 + weighed_before[r])
                        hi(e, edge_v)
                    else:
                        wait_apart(act, s.lo_done, e + 1 + s.before["lo_done"])
                        nc.scalar.activation(edge_v[:, :, :], raw[:, bass.ds((e % RING) * BATCH, BATCH), :], ACT.Copy
                                             ).then_inc(s.hi_done, 1)
                        for q, (j0, j1) in enumerate(QUARTERS):
                            act.wait_ge(s.et_done, 2 * e + (q + 1) + s.before["et_done"])
                            nc.scalar.activation(edge_t[:, j0:j1, :].rearrange("p j d -> p (j d)"),
                                                 (p_edge, p_tr)[q][:, 0:(j1 - j0) * D], ACT.Copy
                                                 ).then_inc(s.et_ready, 1)
                        for j in range(BATCH):
                            wait_apart(act, s.tile_summed, e * BATCH + max(j, 2) + s.before["tile_summed"])
                            wait_apart(act, s.rel_done, e * (2 * BATCH) + (2 * j + 2) + s.before["rel_done"])
                            for k in range(4):
                                last = nc.scalar.activation(
                                    chosen[j % 3][:, 4 + k, :], high_bank[j % 2][:, k * D:(k + 1) * D], ACT.Copy,
                                    scale=tile_ap(mask, e * BATCH + j, 4 + k, 5 + k))
                            last.then_inc(s.high_chosen, 1)
                        wait_apart(act, s.tile_summed, (e + 1) * BATCH + 2 + s.before["tile_summed"])
                        nc.scalar.activation(msg[:, bass.ds(e * BATCH, BATCH), 0:D], edge_v[:, :, :],
                                             ACT.Copy).then_inc(s.hi_done, 1)

                def turn_half(it, a):
                    act.wait_ge(s.tr_done, it * 2 + (a + 1) + s.before["tr_done"])
                    scale = {GIN: one_eps[:, 0:1], GCN: 2.0}.get(rd.kind, 1.0)
                    nc.scalar.activation(h_t[:, a, :], p_tr[:, :], ACT.Copy, scale=scale).then_inc(s.ht_done, 1)

                def store_free(it):
                    if not is_zero(it):
                        wait_apart(act, s.stored, it * 16 + s.before["stored"])

                def relu(it):
                    if not exists(it) or not rd.relu:
                        return
                    act.wait_ge(s.u_done, it * 2 + 2 + s.before["u_done"])
                    if rd.norm:
                        if not is_zero(it):
                            act.wait_ge(s.norm_done, it + s.before["norm_done"])
                        nc.scalar.activation(v[:, :, :], u[:, :, :], ACT.Relu).then_inc(s.relu_done, 1)
                    else:
                        store_free(it)
                        nc.scalar.activation(o[:, :, :], u[:, :, :], ACT.Relu).then_inc(s.out_done, 1)

                def normalise(dst, source, scale, shift_):
                    for b in range(BLOCKS):
                        last = nc.scalar.activation(dst[:, b, :], source[:, b, :], ACT.Identity,
                                                    bias=shift_[:, b:b + 1], scale=scale[:, b:b + 1])
                    return last

                def deviation(it, n):
                    if not exists(it) or n >= norms_of(rd):
                        return
                    act.wait_ge(s.var_done[n], it + 1 + s.before[f"var_done{n}"])
                    nc.scalar.activation(std[n][:, :], mv[n][:, :, 1:2].rearrange("p b o -> p (b o)"), ACT.Sqrt,
                                         bias=eps_col[:, 0:1]).then_inc(s.std_done[n], 1)

                def first_norm(it):
                    if not exists(it):
                        return
                    wait_apart(act, s.stats_done[0], it + 1 + s.before["stats_done0"])
                    if not is_zero(it):
                        if rd.layer == 1:
                            wait_apart(act, s.out_done, it + s.before["out_done"])
                        else:
                            wait_apart(act, s.res_used, it + s.before["res_used"])
                    scale, move = (rstd_d, nmr_d) if rd.layer == 1 else (rstd[0], nmr[0])
                    normalise(o2, v, scale, move).then_inc(s.norm_done, 1)

                def last_norm(it):
                    if not exists(it):
                        return
                    n = norms_of(rd) - 1
                    wait_apart(act, s.stats_done[n], it + 1 + s.before[f"stats_done{n}"])
                    store_free(it)
                    source = total if rd.kind == GCN else v
                    if rd.kind == GIN and not is_zero(it):
                        wait_apart(act, s.norm_done, it + s.before["norm_done"])
                    normalise(o, source, rstd[n], nmr[n]).then_inc(s.out_done, 1)

                def hidden(it, a):
                    for q in range(2):
                        act.wait_ge(hid_done, it * 4 + (2 * a + q + 1))
                        nc.scalar.activation(hid[:, a, q, :], p_wide[:, q, :], ACT.Relu,
                                             bias=b1_col[:, q:q + 1]).then_inc(hid_ready, 1)

                def stage(it, a):
                    pair, ta = back(it, a, lag_of(rd))
                    if rd.kind == GCN and ta == 1:
                        first_norm(pair - 1)
                    nxt, na = back(it, a, -1)
                    if exists(nxt):
                        turn_half(nxt, na)
                    if rd.kind == GIN and exists(it):
                        hidden(it, a)
                    if rd.kind == GCN:
                        if ta == 1:
                            relu(pair)
                            if rd.layer == 2:
                                last_norm(pair - 2)
                        else:
                            deviation(pair - 2, 1)
                            deviation(pair - 1, 0)
                    elif ta == 1:
                        relu(pair)
                        deviation(pair, 0)
                    elif rd.norm:
                        last_norm(pair - 1)

                def batches(it):
                    if exists(it + 1):
                        each_batch(act, *batch_range(*load_list(act, PT, it * (2 * LROW) + LROW + 4, 2)), batch)

                def step(it):
                    if rd.kind in (SAGE, GCN):
                        batches(it)
                    stage(it, 0)
                    if rd.kind in (GIN, RGCN):
                        batches(it)
                    stage(it, 1)

                first_batches(act, PT, batch)
                turn_half(0, 0)
                for it in range(steps_before_loop(rd)):
                    step(it)
                with act.Fori(steps_before_loop(rd), NPAIR - 1) as it:
                    step(it)
                for it in range(NPAIR - 1, NPAIR + steps_after(rd)):
                    step(it)

        @block.tensor
        def _(pe):
            PT = mybir.EngineType.PE
            pe.wait_ge(prep_to_pe, 1)
            for q in range(4):
                last = nc.tensor.transpose(p_tr[0:NHALF, q * NHALF:(q + 1) * NHALF],
                                           touch[0:HT, q, :], ident[0:HT, 0:HT])
            last.then_inc(pe_prep, 1)
            pe.wait_ge(prep_to_pe, 2)
            nc.tensor.matmul(p_edge[0:NHALF, 0:1], before[0:NHALF, 0:NHALF], n_items[0:NHALF, 0:1],
                             start=True, stop=True)
            nc.tensor.matmul(p_wide[0:NHALF, 0, 0:NHALF], ones[0:NHALF, 0:NHALF], diag[0:NHALF, 0:NHALF],
                             start=True, stop=True).then_inc(pe_prep, 1)
            pe.wait_ge(prep_to_pe, 3)
            nc.tensor.matmul(p_wide[0:NHALF, 1, 0:1], ahead[0:NHALF, 0:NHALF], n_batches[0:NHALF, 0:1],
                             start=True, stop=True).then_inc(pe_prep, 1)
            pe.wait_ge(lists_in, 16)
            for r, rd in enumerate(rounds):
                s = R[r]
                pe.wait_ge(s.weights_in, 16 * len(round_weights(rd)) + s.before["weights_in"])
                if rd.kind == GCN and rd.layer == 1:
                    pe.wait_ge(const_pe, 1)
                    nc.tensor.matmul(p_wide[:, 0, 0:D], t_rep[:, :], w[:, 1, :], start=True, stop=True
                                     ).then_inc(const_used, 1)
                pe.sem_inc(s.oh_used, MORE)
                if rd.kind == GIN:
                    pe.sem_inc(emb_used, 1)
                if rd.kind == RGCN:
                    pe.sem_inc(s.low_chosen, 1)
                    pe.sem_inc(s.high_chosen, 1)

                def oh_block(slot, b):
                    return flat(onehot[:, bass.ds(slot, 1), b * P:(b + 1) * P])

                def item(a, t, slot, first):
                    oh = tile_ap(onehot, slot)
                    if r == 0:
                        for b in range(4):
                            nc.tensor.matmul(p_edge[:, 4 * b:4 * b + 4], oh_block(slot, b), tile_ap(ecol, t),
                                             start=first and b == 0, stop=True, skip_group_check=True)
                    nc.tensor.matmul(p_agg[:, a, :], tile_ap(msg, t, 0, D), oh, start=first, stop=True,
                                     skip_group_check=True)
                    return nc.tensor.matmul(p_agg[:, a, :], tile_ap(msg, t, D, 2 * D), oh, start=False, stop=True,
                                            skip_group_check=True)

                def batch(e):
                    if rd.kind == GIN:
                        for q, (j0, j1) in enumerate(((0, 4), (4, BATCH))):
                            if q == 0:
                                wait_apart(pe, attr_ready, e + 1)
                            pe.wait_ge(emb_used, 2 * e + (q + 1))
                            for j in range(j0, j1):
                                last = nc.tensor.matmul(
                                    p_edge[:, (j - j0) * D:(j - j0 + 1) * D],
                                    attr_now[0:BATCH * DE + 1, :], bond[0:BATCH * DE + 1, j, :], start=True, stop=True)
                            last.then_inc(emb_done, 1)
                    elif rd.kind == RGCN:
                        pe.wait_ge(s.hi_done, 2 * e + 1 + s.before["hi_done"])
                        for q, (j0, j1) in enumerate(QUARTERS):
                            for j in range(j0, j1):
                                last = nc.tensor.transpose((p_edge, p_tr)[q][:, (j - j0) * D:(j - j0 + 1) * D],
                                                           edge_v[:, j, :], ident[:, :])
                            last.then_inc(s.et_done, 1)
                        for j in range(BATCH):
                            if j < 2:
                                pe.wait_ge(s.et_ready, 2 * e + (j + 1) + s.before["et_ready"])
                            for q in range(2):
                                name = ("low_chosen", "high_chosen")[q]
                                pe.wait_ge((s.low_chosen, s.high_chosen)[q], e * BATCH + max(j, 1) + s.before[name])
                                nc.tensor.matmul((low_bank, high_bank)[q][j % 2], edge_t[:, j, :],
                                                 flat(w[:, 4 * q:4 * q + 4, :]), start=True, stop=True
                                                 ).then_inc(s.rel_done, 1)

                def half(it, a, items):
                    t0, i0, i1 = items
                    wait_apart(pe, s.every_ready, it * 2 + (a + 1) + s.before["every_ready"])
                    for k in range(EVERY):
                        item(a, (t0 + k).with_bounds(min_val=0, max_val=TILES - 1), EVERY * a + k, k == 0)

                    def more(i):
                        wait_apart(pe, s.oh_ready, i + 1)
                        item(a, tile_of(t0, i0, i), ring_place(i), False).then_inc(s.oh_used, 1)

                    with pe.If(i0 < i1):
                        with pe.Fori(i0, i1) as i:
                            more(i)
                    if not (is_zero(it) and a == 0):
                        pe.wait_ge(s.ht_done, it * 2 + a + s.before["ht_done"])
                    wait_apart(pe, s.h_loaded[a], it * 16 + 16 + s.before[f"h_loaded{a}"])
                    for b in range(4):
                        last = nc.tensor.transpose(p_tr[:, b * P:(b + 1) * P], h_in[:, 4 * a + b, :], ident[:, :])
                    last.then_inc(s.tr_done, 1)

                def dense(it, a):
                    if not exists(back(it, a, -1)[0]):
                        pe.wait_ge(s.u_done, it * 2 + (a - 1) + s.before["u_done"])
                    if rd.kind == GIN:
                        pe.wait_ge(hid_ready, it * 4 + (2 * a + 2))
                        for b in range(4):
                            for q in range(2):
                                last = nc.tensor.matmul(
                                    p_dense[:, a, b * D:(b + 1) * D], hid[:, a, q, b * P:(b + 1) * P],
                                    w[:, 2 + q, :], start=q == 0, stop=q == 1)
                        last.then_inc(s.dense_done, 1)
                        return
                    pe.wait_ge(s.agg_done, it * 2 + (a + 1) + s.before["agg_done"])
                    if rd.kind != GCN:
                        pe.wait_ge(s.ht_done, it * 2 + (a + 1) + s.before["ht_done"])
                    for b in range(4):
                        sl = slice(b * D, (b + 1) * D)
                        if rd.kind == SAGE:
                            nc.tensor.matmul(p_wide[:, a, sl], agg_t[:, a, sl], w[:, 0, :], start=True, stop=True)
                            last = nc.tensor.matmul(p_dense[:, a, sl], h_t[:, a, sl], w[:, 1, :],
                                                    start=True, stop=True)
                        elif rd.kind == GCN:
                            last = nc.tensor.matmul(p_dense[:, a, sl], agg_t[:, a, sl], w[:, 0, :],
                                                    start=True, stop=True)
                        else:
                            nc.tensor.matmul(p_dense[:, a, sl], agg_t[:, a, sl], ident[:, :], start=True, stop=False)
                            last = nc.tensor.matmul(p_dense[:, a, sl], h_t[:, a, sl], w[:, REL, :],
                                                    start=False, stop=True)
                    last.then_inc(s.dense_done, 1)

                def hidden(it, a):
                    pe.wait_ge(s.agg_done, it * 2 + (a + 1) + s.before["agg_done"])
                    for q in range(2):
                        if not (is_zero(it) and a == 0):
                            pe.wait_ge(hid_ready, it * 4 + (2 * a + q - 1))
                        nc.tensor.matmul(p_wide[:, q, :], w[:, q, :], agg_t[:, a, :], start=True, stop=True
                                         ).then_inc(hid_done, 1)

                def batches(it, these):
                    if not exists(it + 1):
                        return
                    if rd.kind == RGCN:
                        pe.wait_ge(s.ht_done, it * 2 + 2 + s.before["ht_done"])
                    each_batch(pe, *these, batch)

                def stage(it, a, items, these=None):
                    nxt, na = back(it, a, -1)
                    if exists(nxt):
                        half(nxt, na, items)
                    if rd.kind == GIN:
                        if exists(it):
                            hidden(it, a)
                        if a == 0:
                            batches(it, these)
                        last, la = back(it, a, 1)
                        if exists(last):
                            dense(last, la)
                    else:
                        dense(it, a)

                def step(it):
                    these, items, next_items = step_list(pe, PT, it)
                    stage(it, 0, items, these)
                    if rd.kind == RGCN:
                        batches(it, these)
                    stage(it, 1, next_items)

                if rd.kind in (GIN, RGCN):
                    first_batches(pe, PT, batch)
                half(0, 0, single_items(pe, PT, 0, 0))
                step(0)
                with pe.Fori(1, NPAIR - 1) as it:
                    step(it)
                step(NPAIR - 1)
                if rd.kind == GIN:
                    dense(NPAIR - 1, 1)

        @block.vector
        def _(dve):
            PT = mybir.EngineType.DVE
            V = nc.vector
            prepared = [0]

            def link(ins):
                prepared[0] += 1
                ins.then_inc(dve_prep, 1)
                dve.wait_ge(dve_prep, prepared[0])

            V.memset(dst_rows[:, :, :], -1)
            V.memset(bond[:, :, :], 0.0)
            V.memset(attr_now[:, :], 1.0).then_inc(pads_set, 1)
            V.memset(ecol[:, :, 0:3], 0.0)
            V.memset(ecol[:, :, 3:4], 1.0)
            V.memset(eps_col[:, :], EPS)
            V.memset(ones[:, :], 1.0)
            dve.wait_ge(iotas, 3)
            V.tensor_copy(iota[:, :], col_i[:, :])
            V.tensor_copy(colf[:, :], col_i[:, 0:P])
            V.tensor_copy(basef[:, :], base_i[:, :])
            link(V.tensor_copy(rowf[:, :], row_i[:, :]))
            for a in range(2):
                link(V.memset(basef[:, NHALF - 2 + a:NHALF - 1 + a], float(a * HALF)))
            V.tensor_scalar(negbase[:, :], basef[:, :], -1.0, None, ALU.mult)
            V.tensor_scalar(ident[:, :], colf[:, :], rowf[:, 0:1], None, ALU.is_equal)
            V.tensor_scalar(before[:, :], colf[:, :], rowf[:, 0:1], None, ALU.is_gt)
            link(V.tensor_scalar(ahead[:, :], colf[:, :], 2.0, float(NHALF - 1), ALU.add, ALU.min))
            link(V.tensor_scalar(ahead[:, :], ahead[:, :], rowf[:, 0:1], None, ALU.is_equal))
            dve.wait_ge(edges_in, 16 * edge_loads)
            V.tensor_copy(etype_f[:, :], etype_i[:, :])
            link(V.tensor_copy(dst_f[:, :], dst_i[:, :]))
            last_tile = dst_f[:, TILES - 1:TILES]
            V.tensor_scalar(col[0][:, :], rowf[:, :], float(LAST), None, ALU.is_lt)
            link(V.tensor_scalar(last_tile, last_tile, 1.0, None, ALU.add))
            link(V.tensor_tensor(last_tile, last_tile, col[0][:, :], ALU.mult))
            link(V.tensor_scalar(last_tile, last_tile, -1.0, None, ALU.add))
            for k in range(REL):
                V.tensor_scalar(mask[:, :, k:k + 1].rearrange("p t o -> p (t o)"), etype_f[:, :], float(k), None, ALU.is_equal)
            rest = flat(u[:, 0:2, :])[:, 0:TILES]
            part = [ecol[:, 0:TILES, k:k + 1].rearrange("p t o -> p (t o)") for k in range(3)]
            link(V.tensor_copy(part[0], ew[:, :]))
            link(V.tensor_tensor(rest, ew[:, :], part[0], ALU.subtract))
            link(V.tensor_copy(part[1], rest))
            link(V.tensor_tensor(rest, rest, part[1], ALU.subtract))
            link(V.tensor_copy(part[2], rest))

            rows, low = v[0:HT, 0:2, :], u[0:HT, 2:4, :]
            link(V.tensor_copy(rows, dst_rows[:, :, :]))
            link(V.tensor_scalar(low, rows, 0.0, 1e6, ALU.is_lt, ALU.mult))
            link(V.tensor_tensor(low, low, rows, ALU.add))
            V.tensor_reduce(t_max[:, :], rows, AX.X, ALU.max)
            link(V.tensor_reduce(t_min[:, :], low, AX.X, ALU.min))
            high, both = o[0:HT, 0, 0:NHALF], o2[0:HT, 0, 0:NHALF]
            for q in range(2):
                V.tensor_scalar(col[q][0:HT, :], rowf[0:HT, :], -1.0, float(2 * P - q * HT), ALU.mult, ALU.add)
                V.tensor_scalar(col[2 + q][0:HT, :], rowf[0:HT, :], float(1 + q * HT), None, ALU.add)
                V.tensor_scalar(high, basef[0:HT, :], t_max[:, q:q + 1], None, ALU.is_le)
                link(V.tensor_scalar(both, basef[0:HT, :], float(HALF - 1), t_min[:, q:q + 1], ALU.add, ALU.is_ge))
                link(V.tensor_tensor(both, both, high, ALU.mult))
                V.tensor_scalar(touch[:, q, :], both, col[q][0:HT, 0:1], None, ALU.mult)
                link(V.tensor_scalar(touch[:, 2 + q, :], both, col[2 + q][0:HT, 0:1], None, ALU.mult))
            V.drain().then_inc(prep_to_pe, 1)
            g = slice(0, NHALF)
            near, far, some, first, last1 = (c[g, :] for c in col[0:5])
            dve.wait_ge(pe_prep, 1)
            V.tensor_reduce(near, p_tr[g, 0:2 * NHALF], AX.X, ALU.max)
            link(V.tensor_reduce(far, p_tr[g, 2 * NHALF:4 * NHALF], AX.X, ALU.max))
            V.tensor_scalar(some, near, 0.0, None, ALU.is_gt)
            link(V.tensor_scalar(first, near, -1.0, float(2 * P), ALU.mult, ALU.add))
            link(V.tensor_tensor(first, first, some, ALU.mult))
            link(V.tensor_scalar(first, first, float(TILES - EVERY), None, ALU.min))
            link(V.tensor_scalar(last1, first, float(EVERY), None, ALU.add))
            link(V.tensor_tensor(last1, last1, far, ALU.max))
            link(V.scalar_tensor_tensor(out=n_items[g, :], in0=last1, scalar=float(-EVERY), in1=first,
                                        op0=ALU.add, op1=ALU.subtract))
            link(V.tensor_scalar(diag[g, g], ident[g, g], last1, None, ALU.mult))
            V.drain().then_inc(prep_to_pe, 1)
            needed, seen = col[5][g, :], o[g, 0, g]
            dve.wait_ge(pe_prep, 2)
            V.memset(list_f[:, :], 0.0)
            link(V.tensor_scalar(seen, colf[g, g], rowf[g, 0:1], None, ALU.is_le))
            link(V.tensor_tensor(seen, seen, p_wide[g, 0, g], ALU.mult))
            link(V.tensor_reduce(needed, seen, AX.X, ALU.max))
            link(V.tensor_scalar(o[g, 1, 0:BATCHES], colf[g, 0:BATCHES], float(BATCH), needed, ALU.mult, ALU.is_lt))
            link(V.tensor_reduce(n_batches[g, :], o[g, 1, 0:BATCHES], AX.X, ALU.add))
            link(V.tensor_scalar(some, rowf[g, :], 0.5, 0.5, ALU.mult, ALU.add))
            link(V.tensor_scalar(some, some, float(BATCHES), None, ALU.min))
            link(V.tensor_tensor(n_batches[g, :], n_batches[g, :], some, ALU.max))
            link(V.tensor_scalar(far, rowf[g, :], float(NHALF - 1), float(BATCHES), ALU.is_equal, ALU.mult))
            link(V.tensor_tensor(n_batches[g, :], n_batches[g, :], far, ALU.max))
            V.drain().then_inc(prep_to_pe, 1)
            for at in (0, 6):
                V.tensor_copy(list_f[:, at + 1:at + 2], first)
                link(V.tensor_copy(list_f[:, at:at + 1], p_edge[g, 0:1]))
            link(V.tensor_tensor(list_f[:, 2:3], list_f[:, 0:1], n_items[g, :], ALU.add))
            link(V.tensor_copy(list_f[:, 4:5], n_batches[g, :]))
            dve.wait_ge(pe_prep, 3)
            link(V.tensor_copy(list_f[:, 5:6], p_wide[g, 1, 0:1]))
            V.tensor_copy(list_rows[:, :], list_f[:, :]).then_inc(rows_ready, 1)
            dve.wait_ge(lists_in, 16)

            for r, rd in enumerate(rounds):
                s = R[r]
                sage, gin, gcn, rgcn = (rd.kind == k for k in (SAGE, GIN, GCN, RGCN))
                dve.wait_ge(s.weights_in, 16 * len(round_weights(rd)) + s.before["weights_in"])
                if r == 1:
                    link(V.tensor_scalar(deg[:, :], deg[:, :], 2.0, None, ALU.add))
                    V.tensor_scalar(dinv[:, :], deg[:, :], 1e-30, None, ALU.max).then_inc(deg_ready, 1)
                    dve.wait_ge(deg_root, 1)
                    link(V.reciprocal(dinv[:, :], dinv[:, :]))
                    link(V.tensor_scalar(deg[:, :], deg[:, :], 0.0, None, ALU.is_gt))
                    link(V.tensor_tensor(dinv[:, :], dinv[:, :], deg[:, :], ALU.mult))
                if gin:
                    V.tensor_scalar(one_eps[:, :], one_eps[:, :], 1.0, None, ALU.add).then_inc(const_dve, 1)
                if gcn and rd.layer == 1:
                    V.tensor_scalar(t_rep[:, :], ones[:, :], t_col[:, 0:1], None, ALU.mult).then_inc(const_pe, 1)
                    dve.wait_ge(const_used, 1)
                    link(V.tensor_tensor(bt[:, :], bt[:, :], p_wide[:, 0, 0:D], ALU.add))
                    link(V.tensor_scalar(bt[:, :], bt[:, :], 0.0, None, ALU.max))
                    link(V.tensor_tensor(bt[:, :], bt[:, :], shift[:, :], ALU.add))

                def lo(e, source, slot=0):
                    return V.tensor_tensor(msg[:, bass.ds(e * BATCH, BATCH), D:2 * D],
                                           source[:, bass.ds(slot * BATCH, BATCH), :],
                                           msg[:, bass.ds(e * BATCH, BATCH), 0:D], ALU.subtract).then_inc(s.lo_done, 1)

                if edge_v_used(rd):
                    dve.sem_inc(s.lo_done, 1)
                if rgcn:
                    dve.sem_inc(s.tile_summed, 2)

                def batch(e):
                    if gin:
                        wait_apart(dve, s.batch_in, e + 1 + s.before["batch_in"])
                        V.tensor_copy(attr_now[0:BATCH * DE, :], tile_ap(attr, e % RING)).then_inc(attr_ready, 1)
                        wait_apart(dve, s.lo_done, e + 1 + s.before["lo_done"])
                        for q, (j0, j1) in enumerate(((0, 4), (4, BATCH))):
                            dve.wait_ge(emb_done, 2 * e + (q + 1))
                            V.tensor_tensor(
                                edge_v[:, j0:j1, :], raw[:, bass.ds((e % RING) * BATCH + j0, j1 - j0), :],
                                p_edge[:, 0:(j1 - j0) * D].rearrange("p (j d) -> p j d", d=D),
                                ALU.add).then_inc(emb_used, 1)
                        dve.wait_ge(s.hi_done, e + 1 + s.before["hi_done"])
                        lo(e, edge_v)
                    elif sage or gcn:
                        dve.wait_ge(s.hi_done, e + 1 + s.before["hi_done"])
                        if gcn:
                            lo(e, edge_v)
                        else:
                            lo(e, raw, e % RING)
                    else:
                        dve.wait_ge(s.et_done, 2 * e + 2 + s.before["et_done"])

                        def choose(j):
                            dve.wait_ge(s.tile_summed, e * BATCH + max(j, 2) + s.before["tile_summed"])
                            dve.wait_ge(s.rel_done, e * (2 * BATCH) + (2 * j + 1) + s.before["rel_done"])
                            own = mask[:, bass.ds(e * BATCH + j, 1), 0:4].rearrange("p o k -> p (o k)")
                            V.tensor_tensor(chosen[j % 3][:, 0:4, :],
                                            low_bank[j % 2].rearrange("p (k d) -> p k d", d=D),
                                            own.unsqueeze(2).to_broadcast([P, 4, D]), ALU.mult
                                            ).then_inc(s.low_chosen, 1)

                        choose(0)
                        for j in range(BATCH):
                            if j + 1 < BATCH:
                                choose(j + 1)
                            dve.wait_ge(s.low_chosen, e * BATCH + (j + 2) + s.before["low_chosen"])
                            dve.wait_ge(s.high_chosen, e * BATCH + (j + 2) + s.before["high_chosen"])
                            V.tensor_reduce(edge_v[:, j, :], chosen[j % 3].rearrange("p k d -> p d k"),
                                            AX.X, ALU.add).then_inc(s.tile_summed, 1)
                        dve.wait_ge(s.hi_done, 2 * e + 2 + s.before["hi_done"])
                        lo(e, edge_v)

                def onehots(it, a, items):
                    t0, i0, i1 = items

                    def compare(slot, t):
                        return V.tensor_scalar(tile_ap(onehot, slot), iota[:, :], dst_f[:, bass.ds(t, 1)],
                                               negbase[:, bass.ds(it * 2 + a, 1)], ALU.subtract, ALU.is_equal)

                    for k in range(EVERY):
                        last = compare(EVERY * a + k, (t0 + k).with_bounds(min_val=0, max_val=TILES - 1))
                    last.then_inc(s.every_ready, 1)
                    with dve.If(i0 < i1):
                        with dve.Fori(i0, i1) as i:
                            dve.wait_ge(s.oh_used, i + 1)
                            compare(ring_place(i), tile_of(t0, i0, i)).then_inc(s.oh_ready, 1)

                def sums(it, a):
                    dve.wait_ge(s.tr_done, it * 2 + (a + 1) + s.before["tr_done"])
                    if gin or gcn:
                        dve.wait_ge(s.ht_done, it * 2 + (a + 1) + s.before["ht_done"])
                        V.tensor_tensor(agg_t[:, a, :], p_agg[:, a, :], h_t[:, a, :], ALU.add).then_inc(s.agg_done, 1)
                    else:
                        V.tensor_copy(agg_t[:, a, :], p_agg[:, a, :]).then_inc(s.agg_done, 1)

                def degrees(it, a):
                    dve.wait_ge(s.tr_done, it * 2 + (a + 1) + s.before["tr_done"])
                    if not (is_zero(it) and a == 0):
                        dve.wait_ge(deg_used, it * 2 + a)
                    sums_ = p_edge[:, 0:16].rearrange("p (b c) -> p b c", c=4)
                    V.tensor_reduce(deg[:, bass.ds(it * BLOCKS + 4 * a, 4)], sums_[:, :, 0:3], AX.X, ALU.add)
                    V.tensor_scalar(count[:, :], sums_[:, :, 3:4].rearrange("p b c -> p (b c)"),
                                    1.0, None, ALU.max).then_inc(count_done, 1)

                def one_over_count(it, a):
                    dve.wait_ge(count_done, it * 2 + (a + 1))
                    V.reciprocal(inv[:, bass.ds(it * BLOCKS + 4 * a, 4)], count[:, :]).then_inc(deg_used, 1)

                def chain(ins, semaphore, name, count):
                    ins.then_inc(semaphore, 1)
                    dve.wait_ge(semaphore, count + s.before[name])

                def wide(row):
                    return row[:, :].unsqueeze(1).to_broadcast([P, BLOCKS, D])

                def take(it, a):
                    if not exists(it):
                        return
                    if a == 0 and not is_zero(it):
                        if not rd.relu:
                            dve.wait_ge(s.res_used, it + s.before["res_used"])
                        elif rd.norm:
                            dve.wait_ge(s.relu_done, it + s.before["relu_done"])
                        else:
                            dve.wait_ge(s.out_done, it + s.before["out_done"])
                    if r == 0:
                        dve.wait_ge(deg_used, it * 2 + (a + 1))
                    dve.wait_ge(s.dense_done, it * 2 + (a + 1) + s.before["dense_done"])
                    half_u = u[:, 4 * a:4 * a + 4, :]
                    product = p_dense[:, a, :].rearrange("p (b d) -> p b d", d=D)
                    if sage or gcn:
                        scale, source = (inv, p_wide) if sage else (dinv, p_dense)
                        for b in range(4):
                            last = V.scalar_tensor_tensor(
                                out=u[:, 4 * a + b, :], in0=source[:, a, b * D:(b + 1) * D],
                                scalar=scale[:, bass.ds(it * BLOCKS + (4 * a + b), 1)], in1=bias[:, :],
                                op0=ALU.mult, op1=ALU.add)
                        if sage:
                            chain(last, s.scaled_done, "scaled_done", it * 2 + (a + 1))
                            last = V.tensor_tensor(half_u, half_u, product, ALU.add)
                    else:
                        last = V.tensor_tensor(half_u, product, bias[:, :].unsqueeze(1).to_broadcast([P, 4, D]), ALU.add)
                    last.then_inc(s.u_done, 1)

                def mean_variance(it, source, n):
                    if not is_zero(it):
                        dve.wait_ge(s.stats_done[n], it + s.before[f"stats_done{n}"])
                    for b in range(BLOCKS):
                        last = V.bn_stats(stats[n][:, b, :], source[:, b, :])
                    chain(last, s.bn_done[n], f"bn_done{n}", it + 1)
                    dve.sem_inc(passed, 1)
                    for b in range(BLOCKS):
                        last = V.bn_aggr(mv[n][:, b, :], stats[n][:, b, :])
                    last.then_inc(s.var_done[n], 1)

                def scale_and_move(it, n):
                    if not exists(it) or n >= norms_of(rd):
                        return
                    scaled = scaled_by_dinv(rd)
                    step, name, per = s.rstd_step[n], f"rstd_step{n}", 1 + scaled
                    mean = mv[n][:, :, 0:1].rearrange("p b o -> p (b o)")
                    dve.wait_ge(s.std_done[n], it + 1 + s.before[f"std_done{n}"])
                    chain(V.reciprocal(rstd[n][:, :], std[n][:, :]), step, name, it * per + 1)
                    last = V.scalar_tensor_tensor(out=nmr[n][:, :], in0=mean, scalar=-1.0, in1=rstd[n][:, :],
                                                  op0=ALU.mult, op1=ALU.mult)
                    if scaled:
                        chain(last, step, name, it * per + 2)
                        at = bass.ds(it * BLOCKS, BLOCKS)
                        V.tensor_tensor(rstd_d[:, :], rstd[n][:, :], dinv[:, at], ALU.mult)
                        last = V.tensor_tensor(nmr_d[:, :], nmr[n][:, :], dinv[:, at], ALU.mult)
                    last.then_inc(s.stats_done[n], 1)

                def add_residual(it, dst, source):
                    dve.wait_ge(s.res_loaded, it * 16 + 16 + s.before["res_loaded"])
                    V.tensor_tensor(dst[:, :, :], source[:, :, :], res_in[:, :, :], ALU.add).then_inc(s.res_used, 1)
                    dve.wait_ge(s.res_used, it + 1 + s.before["res_used"])

                def residual_and_stats(it):
                    if not exists(it) or not rd.norm:
                        return
                    if not is_zero(it):
                        dve.wait_ge(s.out_done, it + s.before["out_done"])
                    dve.wait_ge(s.u_done, it * 2 + 2 + s.before["u_done"])
                    add_residual(it, v, u)
                    mean_variance(it, v, 0)

                def scale_rows(it):
                    if not exists(it):
                        return
                    if not is_zero(it):
                        dve.wait_ge(s.stored2, it * 16 + s.before["stored2"])
                    dve.wait_ge(s.out_done, it + 1 + s.before["out_done"])
                    V.tensor_tensor(o2[:, :, :], o[:, :, :],
                                    dinv[:, bass.ds(it * BLOCKS, BLOCKS)].unsqueeze(2).to_broadcast([P, BLOCKS, D]),
                                    ALU.mult).then_inc(s.norm_done, 1)

                def relu_stats(it):
                    if not exists(it):
                        return
                    dve.wait_ge(s.relu_done, it + 1 + s.before["relu_done"])
                    mean_variance(it, v, 0)

                def gain_and_shift(it):
                    if not exists(it):
                        return
                    per = rd.layer
                    dve.wait_ge(s.norm_done, it + 1 + s.before["norm_done"])
                    chain(V.tensor_tensor(o2[:, :, :], o2[:, :, :], wide(gain), ALU.mult),
                          s.gain_step, "gain_step", it * per + 1)
                    if rd.layer == 1:
                        if not is_zero(it):
                            dve.wait_ge(s.stored, it * 16 + s.before["stored"])
                        for b in range(BLOCKS):
                            last = V.scalar_tensor_tensor(
                                out=o[:, b, :], in0=bt[:, :], scalar=dinv[:, bass.ds(it * BLOCKS + b, 1)],
                                in1=o2[:, b, :], op0=ALU.mult, op1=ALU.add)
                        last.then_inc(s.out_done, 1)
                        return
                    chain(V.tensor_tensor(o2[:, :, :], o2[:, :, :], wide(shift), ALU.add),
                          s.gain_step, "gain_step", it * per + 2)
                    if not is_zero(it):
                        dve.wait_ge(s.out_done, it + s.before["out_done"])
                    add_residual(it, total, o2)
                    mean_variance(it, total, 1)

                def stage(it, a, items):
                    if r == 0 and exists(it):
                        degrees(it, a)
                    nxt, na = back(it, a, -1)
                    if exists(nxt):
                        onehots(nxt, na, items)
                    pair, ta = back(it, a, lag_of(rd))
                    if ta == int(gcn):
                        scale_and_move(pair - 1, 0)
                        scale_and_move(pair - 2, 1)
                    if exists(it):
                        sums(it, a)
                        if r == 0:
                            one_over_count(it, a)
                    take(pair, ta)
                    if gcn:
                        if ta == 0:
                            relu_stats(pair - 1)
                            gain_and_shift(pair - 2)
                    elif ta == 1:
                        if gin:
                            scale_rows(pair - 1)
                        residual_and_stats(pair)

                def step(it):
                    these, items, next_items = step_list(dve, PT, it)
                    stage(it, 0, items)
                    if exists(it + 1):
                        each_batch(dve, *these, batch)
                    stage(it, 1, next_items)

                first_batches(dve, PT, batch)
                onehots(0, 0, single_items(dve, PT, 0, 0))
                for it in range(steps_before_loop(rd)):
                    step(it)
                with dve.Fori(steps_before_loop(rd), NPAIR - 1) as it:
                    step(it)
                for it in range(NPAIR - 1, NPAIR + steps_after(rd)):
                    step(it)


def kernel(**inputs):
    import numpy as _np
    import concourse.bacc as _bacc
    from concourse import mybir as _mybir
    from concourse.bass_utils import run_bass_kernel_spmd as _run

    edge_arrays = ("src", "dst", "edge_weight", "edge_weight1", "edge_type_8")

    def by_tile(a):
        full = _np.zeros(TILES * P, a.dtype)
        full[:E] = a.reshape(E)[::-1]
        return _np.ascontiguousarray(full.reshape(TILES, P).T)

    def by_batch(a):
        full = _np.zeros((TILES * P, DE), a.dtype)
        full[:E] = a[::-1]
        return _np.ascontiguousarray(full.reshape(BATCHES, BATCH, P, DE).transpose(0, 1, 3, 2)).reshape(
            BATCHES, BATCH * DE, P)

    nc = _bacc.Bacc("TRN2", target_bir_lowering=False, num_devices=1)
    laid = {"dst_flat": _np.ascontiguousarray(_np.asarray(inputs["dst"])[::-1])}
    for name, a in inputs.items():
        a = _np.asarray(a)
        if name in edge_arrays:
            a = by_tile(a)
        elif name == "edge_attr_16":
            a = by_batch(a)
        elif name == "L1_gnn_b1":
            a = a.reshape(2, P).T
        laid[name] = _np.ascontiguousarray(a)
    arrays, aps = {}, {}
    for name, a in laid.items():
        arrays[f"in_{name}"] = a
        aps[name] = nc.dram_tensor(f"in_{name}", a.shape, _mybir.dt.from_np(a.dtype), kind="ExternalInput").ap()
    out = nc.dram_tensor("out", (N, D), F32, kind="ExternalOutput").ap()
    build_gnn(nc, aps, out)
    return _run(nc, [arrays], core_ids=[0]).results[0]["out"]
```
